# Optimizing a Trainium2 kernel written in Bass

```python
import numpy as np
import jax
import jax.numpy as jnp

def _softmax(x, axis=-1):
    return jax.nn.softmax(x, axis=axis)

def _gelu(x):
    return jax.nn.gelu(x, approximate=True)

def _silu(x):
    return jax.nn.silu(x)

def _sigmoid(x):
    return jax.nn.sigmoid(x)

def _layernorm(x, axis=-1, eps=1e-05):
    m = jnp.mean(x, axis=axis, keepdims=True)
    v = jnp.var(x, axis=axis, keepdims=True)
    return (x - m) / jnp.sqrt(v + eps)

def _scatter_add(tgt, idx, src, axis=0):
    return tgt.at[idx].add(src)

def _segment_sum(src, seg, n):
    return jax.ops.segment_sum(src, seg, n)
kernel_name = 'mk_xattn_ffn_d2_seqx_r8_a82b44'

def setup_inputs(seed: int=0):
    np.random.seed(seed)
    _w = jnp.asarray

    def _rec_inputs():
        import jax
        import jax.numpy as jnp
        _rk = jax.random.key(seed)
        x = -0.0005146 + 1 * jax.random.normal(jax.random.fold_in(_rk, 1), (4, 256, 128), jnp.float32)
        _lenS = 256 - jax.random.randint(jax.random.fold_in(_rk, 7), (4,), 0, max(1, 256 // 4) + 1, jnp.int32)
        _lenS2 = 512 - jax.random.randint(jax.random.fold_in(_rk, 8), (4,), 0, max(1, 512 // 4) + 1, jnp.int32)
        _ctx_1024P = jax.random.normal(jax.random.fold_in(_rk, 11), (4, 16, 128), jnp.float32)
        _ctx_1024c = jax.random.dirichlet(jax.random.fold_in(_rk, 511), 0.3 * jnp.ones((16,), jnp.float32), (4, 512))
        _ctx_1024t = jnp.einsum('bsk,bkd->bsd', _ctx_1024c, _ctx_1024P)
        _ctx_1024t = _ctx_1024t * jax.lax.rsqrt(jnp.mean(jnp.square(_ctx_1024t)) + 1e-12) * 0.953939
        ctx_1024 = -0.000392918 + 0.999932 * (_ctx_1024t + 0.3 * jax.random.normal(jax.random.fold_in(_rk, 611), (4, 512, 128), jnp.float32))
        _validS = jnp.arange(256)[None, :] < _lenS[:, None]
        _validS2 = jnp.arange(512)[None, :] < _lenS2[:, None]
        _causal = jnp.tril(jnp.ones((256, 256), dtype=bool))
        mask_BxS2_bf1 = jnp.ones((4, 512), dtype=bool)
        mask_1xSxS2_ff0 = jnp.where(jnp.ones((1, 256, 512), dtype=bool), 0.0, -1000000000.0).astype(jnp.float32)
        return (x, ctx_1024, mask_BxS2_bf1, mask_1xSxS2_ff0)
    x, ctx_1024, mask_BxS2_bf1, mask_1xSxS2_ff0 = _rec_inputs()

    def _L0_xattn_setup():
        import jax, jax.numpy as jnp
        import numpy as np
        DIM = 128
        DIM_LATENT = 128
        DIM_HEAD = 64
        HEADS = 16
        INNER = HEADS * DIM_HEAD

        def layernorm(x, g, b, eps=1e-05):
            m = jnp.mean(x, axis=-1, keepdims=True)
            v = jnp.mean((x - m) ** 2, axis=-1, keepdims=True)
            return (x - m) / jnp.sqrt(v + eps) * g + b

        def rmsnorm(x, gamma, eps=1e-08):
            n = jnp.linalg.norm(x, axis=-1, keepdims=True) * x.shape[-1] ** (-0.5)
            return x / jnp.maximum(n, eps) * gamma
        key = jax.random.key(seed)
        ks = jax.random.split(key, 8)
        b, n, m = (4, 512, 64)
        x = jax.random.normal(ks[0], (b, n, DIM), dtype=jnp.float32)
        latents = jax.random.normal(ks[1], (b, m, DIM_LATENT), dtype=jnp.float32)
        mask = jnp.ones((b, n), dtype=bool)
        s = 0.02
        return {'x': x, 'latents': latents, 'mask': mask, 'ln_x_g': jnp.ones((DIM,), jnp.float32), 'ln_x_b': jnp.zeros((DIM,), jnp.float32), 'ln_l_g': jnp.ones((DIM_LATENT,), jnp.float32), 'ln_l_b': jnp.zeros((DIM_LATENT,), jnp.float32), 'qn_g': jnp.ones((DIM_HEAD,), jnp.float32), 'kn_g': jnp.ones((DIM_HEAD,), jnp.float32), 'Wq': jax.random.normal(ks[2], (DIM_LATENT, INNER), jnp.float32) * s, 'Wkv': jax.random.normal(ks[3], (DIM, 2 * INNER), jnp.float32) * s, 'Wout': jax.random.normal(ks[4], (INNER, DIM_LATENT), jnp.float32) * s, 'bout': jnp.zeros((DIM_LATENT,), jnp.float32)}
    _L0_xattn_all = _L0_xattn_setup()
    _L0_xattn_in = {k: v for k, v in _L0_xattn_all.items() if k in ('ln_x_g', 'ln_x_b', 'ln_l_g', 'ln_l_b', 'qn_g', 'kn_g', 'Wq', 'Wkv', 'Wout', 'bout')}
    del _L0_xattn_all

    def _L0_ffn_setup():
        import jax, jax.numpy as jnp
        import numpy as np
        B, S, D = (2, 256, 128)
        E, G, K = (32, 8, 4)
        H, SH = (256, 256)
        CAP_FACTOR = 1.25

        def _l2norm(v):
            n = jnp.linalg.norm(v, axis=-1, keepdims=True)
            return v / jnp.maximum(n, 1e-12)
        key = jax.random.key(seed)
        ks = jax.random.split(key, 10)
        x = jax.random.normal(ks[0], (B, S, D), jnp.float32)
        group_centroids = jax.random.normal(ks[1], (G, D), jnp.float32) * 0.02
        expert_centroids = jax.random.normal(ks[2], (E, D), jnp.float32) * 0.02
        bias = jnp.zeros((E,), jnp.float32)
        sd_in = 1.0 / np.sqrt(D).astype(np.float32)
        sd_h = 1.0 / np.sqrt(H).astype(np.float32)
        wg = jax.random.normal(ks[3], (E, D, H), jnp.float32) * sd_in
        wu = jax.random.normal(ks[4], (E, D, H), jnp.float32) * sd_in
        wd = jax.random.normal(ks[5], (E, H, D), jnp.float32) * sd_h
        sg = jax.random.normal(ks[6], (D, SH), jnp.float32) * sd_in
        su = jax.random.normal(ks[7], (D, SH), jnp.float32) * sd_in
        sd_w = jax.random.normal(ks[8], (SH, D), jnp.float32) * sd_h
        return dict(x=x, group_centroids=group_centroids, expert_centroids=expert_centroids, bias=bias, wg=wg, wu=wu, wd=wd, sg=sg, su=su, sd=sd_w)
    _L0_ffn_all = _L0_ffn_setup()
    _L0_ffn_in = {k: v for k, v in _L0_ffn_all.items() if k in ('group_centroids', 'expert_centroids', 'bias', 'wg', 'wu', 'wd', 'sg', 'su', 'sd')}
    del _L0_ffn_all

    def _L1_xattn_setup():
        import jax, jax.numpy as jnp
        import numpy as np
        B, S, D_IN, D_MODEL = (4, 256, 128, 128)
        key = jax.random.key(seed)
        ks = jax.random.split(key, 8)
        glorot = np.sqrt(6.0 / (D_IN + D_MODEL))
        inp = {'q': jax.random.normal(ks[0], (B, S, D_IN), dtype=jnp.float32), 'k': jax.random.normal(ks[1], (B, S, D_IN), dtype=jnp.float32), 'v': jax.random.normal(ks[2], (B, S, D_IN), dtype=jnp.float32), 'mask': jnp.zeros((1, S, S), dtype=jnp.float32), 'kernel_q': jax.random.uniform(ks[3], (1, 1, D_IN, D_MODEL), jnp.float32, -glorot, glorot), 'kernel_k': jax.random.uniform(ks[4], (1, 1, D_IN, D_MODEL), jnp.float32, -glorot, glorot), 'kernel_v': jax.random.uniform(ks[5], (1, 1, D_IN, D_MODEL), jnp.float32, -glorot, glorot), 'bias_q': 0.05 * jax.random.normal(ks[6], (D_MODEL,), dtype=jnp.float32), 'bias_k': 0.05 * jax.random.normal(ks[7], (D_MODEL,), dtype=jnp.float32), 'bias_v': 0.05 * jax.random.normal(jax.random.fold_in(key, 7), (D_MODEL,), dtype=jnp.float32)}
        return inp
    _L1_xattn_all = _L1_xattn_setup()
    _L1_xattn_in = {k: v for k, v in _L1_xattn_all.items() if k in ('kernel_q', 'kernel_k', 'kernel_v', 'bias_q', 'bias_k', 'bias_v')}
    del _L1_xattn_all

    def _L1_ffn_setup():
        import jax, jax.numpy as jnp
        import numpy as np
        H, I, E, K = (128, 64, 32, 8)
        B, S = (4, 128)

        def silu(x):
            return x * jax.nn.sigmoid(x)
        key = jax.random.key(seed)
        ks = jax.random.split(key, 14)

        def w(k, shape, fan_in):
            return jax.random.normal(k, shape, jnp.float32) / np.float32(np.sqrt(fan_in))
        return {'hidden_states': jax.random.normal(ks[0], (B, S, H), jnp.float32), 'Wr': w(ks[1], (H, E), H), 'br': jnp.zeros((E,), jnp.float32), 'Wg_s': w(ks[2], (H, I), H), 'bg_s': jnp.zeros((I,), jnp.float32), 'Wu_s': w(ks[3], (H, I), H), 'bu_s': jnp.zeros((I,), jnp.float32), 'Wd_s': w(ks[4], (I, H), I), 'bd_s': jnp.zeros((H,), jnp.float32), 'Wg': w(ks[5], (E, H, I), H), 'bg': jnp.zeros((E, I), jnp.float32), 'Wu': w(ks[6], (E, H, I), H), 'bu': jnp.zeros((E, I), jnp.float32), 'Wd': w(ks[7], (E, I, H), I), 'bd': jnp.zeros((E, H), jnp.float32)}
    _L1_ffn_all = _L1_ffn_setup()
    _L1_ffn_in = {k: v for k, v in _L1_ffn_all.items() if k in ('Wr', 'br', 'Wg_s', 'bg_s', 'Wu_s', 'bu_s', 'Wd_s', 'bd_s', 'Wg', 'bg', 'Wu', 'bu', 'Wd', 'bd')}
    del _L1_ffn_all
    return {'x': x, 'ctx_1024': ctx_1024, 'mask_BxS2_bf1': mask_BxS2_bf1, 'mask_1xSxS2_ff0': mask_1xSxS2_ff0, 'L0_xattn_ln_x_g': _L0_xattn_in['ln_x_g'], 'L0_xattn_ln_x_b': _L0_xattn_in['ln_x_b'], 'L0_xattn_ln_l_g': _L0_xattn_in['ln_l_g'], 'L0_xattn_ln_l_b': _L0_xattn_in['ln_l_b'], 'L0_xattn_qn_g': _L0_xattn_in['qn_g'], 'L0_xattn_kn_g': _L0_xattn_in['kn_g'], 'L0_xattn_Wq': _L0_xattn_in['Wq'], 'L0_xattn_Wkv': _L0_xattn_in['Wkv'], 'L0_xattn_Wout': _L0_xattn_in['Wout'], 'L0_xattn_bout': _L0_xattn_in['bout'], 'L0_ffn_group_centroids': _L0_ffn_in['group_centroids'], 'L0_ffn_expert_centroids': _L0_ffn_in['expert_centroids'], 'L0_ffn_bias': _L0_ffn_in['bias'], 'L0_ffn_wg': _L0_ffn_in['wg'], 'L0_ffn_wu': _L0_ffn_in['wu'], 'L0_ffn_wd': _L0_ffn_in['wd'], 'L0_ffn_sg': _L0_ffn_in['sg'], 'L0_ffn_su': _L0_ffn_in['su'], 'L0_ffn_sd': _L0_ffn_in['sd'], 'L1_xattn_kernel_q': _L1_xattn_in['kernel_q'], 'L1_xattn_kernel_k': _L1_xattn_in['kernel_k'], 'L1_xattn_kernel_v': _L1_xattn_in['kernel_v'], 'L1_xattn_bias_q': _L1_xattn_in['bias_q'], 'L1_xattn_bias_k': _L1_xattn_in['bias_k'], 'L1_xattn_bias_v': _L1_xattn_in['bias_v'], 'L1_ffn_Wr': _L1_ffn_in['Wr'], 'L1_ffn_br': _L1_ffn_in['br'], 'L1_ffn_Wg_s': _L1_ffn_in['Wg_s'], 'L1_ffn_bg_s': _L1_ffn_in['bg_s'], 'L1_ffn_Wu_s': _L1_ffn_in['Wu_s'], 'L1_ffn_bu_s': _L1_ffn_in['bu_s'], 'L1_ffn_Wd_s': _L1_ffn_in['Wd_s'], 'L1_ffn_bd_s': _L1_ffn_in['bd_s'], 'L1_ffn_Wg': _L1_ffn_in['Wg'], 'L1_ffn_bg': _L1_ffn_in['bg'], 'L1_ffn_Wu': _L1_ffn_in['Wu'], 'L1_ffn_bu': _L1_ffn_in['bu'], 'L1_ffn_Wd': _L1_ffn_in['Wd'], 'L1_ffn_bd': _L1_ffn_in['bd']}

def reference(x, ctx_1024, mask_BxS2_bf1, mask_1xSxS2_ff0, L0_xattn_ln_x_g, L0_xattn_ln_x_b, L0_xattn_ln_l_g, L0_xattn_ln_l_b, L0_xattn_qn_g, L0_xattn_kn_g, L0_xattn_Wq, L0_xattn_Wkv, L0_xattn_Wout, L0_xattn_bout, L0_ffn_group_centroids, L0_ffn_expert_centroids, L0_ffn_bias, L0_ffn_wg, L0_ffn_wu, L0_ffn_wd, L0_ffn_sg, L0_ffn_su, L0_ffn_sd, L1_xattn_kernel_q, L1_xattn_kernel_k, L1_xattn_kernel_v, L1_xattn_bias_q, L1_xattn_bias_k, L1_xattn_bias_v, L1_ffn_Wr, L1_ffn_br, L1_ffn_Wg_s, L1_ffn_bg_s, L1_ffn_Wu_s, L1_ffn_bu_s, L1_ffn_Wd_s, L1_ffn_bd_s, L1_ffn_Wg, L1_ffn_bg, L1_ffn_Wu, L1_ffn_bu, L1_ffn_Wd, L1_ffn_bd):
    import jax
    import jax.numpy as jnp

    def _L0_xattn_ref(x, latents, mask, ln_x_g, ln_x_b, ln_l_g, ln_l_b, qn_g, kn_g, Wq, Wkv, Wout, bout):
        import jax, jax.numpy as jnp
        import numpy as np
        DIM = 128
        DIM_LATENT = 128
        DIM_HEAD = 64
        HEADS = 16
        INNER = HEADS * DIM_HEAD

        def layernorm(x, g, b, eps=1e-05):
            m = jnp.mean(x, axis=-1, keepdims=True)
            v = jnp.mean((x - m) ** 2, axis=-1, keepdims=True)
            return (x - m) / jnp.sqrt(v + eps) * g + b

        def rmsnorm(x, gamma, eps=1e-08):
            n = jnp.linalg.norm(x, axis=-1, keepdims=True) * x.shape[-1] ** (-0.5)
            return x / jnp.maximum(n, eps) * gamma
        b, n, _ = x.shape
        m = latents.shape[1]
        h, d = (HEADS, DIM_HEAD)
        scale = d ** (-0.5)
        xn = layernorm(x, ln_x_g, ln_x_b)
        ln = layernorm(latents, ln_l_g, ln_l_b)
        q = (ln @ Wq).reshape(b, m, h, d).transpose(0, 2, 1, 3)
        kv = jnp.concatenate([xn @ Wkv, ln @ Wkv], axis=1)
        kv = kv.reshape(b, n + m, 2, h, d)
        k = kv[:, :, 0].transpose(0, 2, 1, 3)
        v = kv[:, :, 1].transpose(0, 2, 1, 3)
        qn = rmsnorm(q, qn_g) * scale
        kn = rmsnorm(k, kn_g)
        sim = jnp.einsum('bhid,bhjd->bhij', qn, kn)
        max_neg = -jnp.finfo(sim.dtype).max
        padded_mask = jnp.concatenate([mask, jnp.ones((b, m), bool)], axis=1)
        sim = jnp.where(padded_mask[:, None, None, :], sim, max_neg)
        attn = jax.nn.softmax(sim.astype(jnp.float32), axis=-1).astype(sim.dtype)
        out = jnp.einsum('bhij,bhjd->bhid', attn, v)
        out = out.transpose(0, 2, 1, 3).reshape(b, m, h * d)
        return out @ Wout + bout

    def _L0_ffn_ref(x, group_centroids, expert_centroids, bias, wg, wu, wd, sg, su, sd):
        import jax, jax.numpy as jnp
        import numpy as np
        B, S, D = (2, 256, 128)
        E, G, K = (32, 8, 4)
        H, SH = (256, 256)
        CAP_FACTOR = 1.25

        def _l2norm(v):
            n = jnp.linalg.norm(v, axis=-1, keepdims=True)
            return v / jnp.maximum(n, 1e-12)
        b, s, d = x.shape
        xf = x.reshape(-1, d)
        N = xf.shape[0]
        shared = jax.nn.silu(xf @ sg) * (xf @ su) @ sd
        xn = _l2norm(xf)
        group_scores = xn @ _l2norm(group_centroids).T
        n_top_groups = max(1, G // 2)
        _, top_group_idx = jax.lax.top_k(group_scores, n_top_groups)
        expert_scores = xn @ _l2norm(expert_centroids).T + bias
        expert_to_group = jnp.arange(E) // (E // G)
        sel = jnp.zeros((N, G), xf.dtype).at[jnp.arange(N)[:, None], top_group_idx].set(1.0)
        group_mask = sel[:, expert_to_group]
        masked = expert_scores * group_mask + (1.0 - group_mask) * -1000000000.0
        top_scores, top_idx = jax.lax.top_k(masked, K)
        gates = jax.nn.softmax(top_scores, axis=-1)
        capacity = max(1, int(N / E * K * CAP_FACTOR))
        flat_e = top_idx.reshape(-1)
        flat_g = gates.reshape(-1)
        tok = jnp.repeat(jnp.arange(N), K)
        onehot = jax.nn.one_hot(flat_e, E, dtype=jnp.int32)
        pos = jnp.cumsum(onehot, axis=0)[jnp.arange(N * K), flat_e] - 1
        keep = pos < capacity
        e_s = jnp.where(keep, flat_e, E)
        p_s = jnp.where(keep, pos, 0)
        buf = jnp.zeros((E + 1, capacity, d), xf.dtype).at[e_s, p_s].set(xf[tok])[:E]
        h = jax.nn.silu(jnp.einsum('ecd,edh->ech', buf, wg)) * jnp.einsum('ecd,edh->ech', buf, wu)
        out_e = jnp.einsum('ech,ehd->ecd', h, wd)
        gathered = out_e[flat_e, jnp.minimum(pos, capacity - 1)]
        contrib = gathered * (flat_g * keep.astype(xf.dtype))[:, None]
        routed = jnp.zeros_like(xf).at[tok].add(contrib)
        return (shared + routed).reshape(b, s, d)

    def _L1_xattn_ref(q, k, v, mask, kernel_q, kernel_k, kernel_v, bias_q, bias_k, bias_v):
        import jax, jax.numpy as jnp
        import numpy as np
        B, S, D_IN, D_MODEL = (4, 256, 128, 128)
        Wq, Wk, Wv = (kernel_q[0, 0], kernel_k[0, 0], kernel_v[0, 0])
        qp = jax.nn.relu(jnp.einsum('bsd,de->bse', q, Wq) + bias_q)
        kp = jax.nn.relu(jnp.einsum('bsd,de->bse', k, Wk) + bias_k)
        vp = jax.nn.relu(jnp.einsum('bsd,de->bse', v, Wv) + bias_v)
        scores = jax.nn.relu(jnp.einsum('bqe,bke->bqk', qp, kp))
        dk = jnp.asarray(kp.shape[-1], dtype=scores.dtype)
        logits = scores / jnp.sqrt(dk) + mask
        out = jax.nn.relu(jnp.einsum('bqk,bke->bqe', logits, vp))
        return out

    def _L1_ffn_ref(hidden_states, Wr, br, Wg_s, bg_s, Wu_s, bu_s, Wd_s, bd_s, Wg, bg, Wu, bu, Wd, bd):
        import jax, jax.numpy as jnp
        import numpy as np
        H, I, E, K = (128, 64, 32, 8)
        B, S = (4, 128)

        def silu(x):
            return x * jax.nn.sigmoid(x)
        b, s, h = hidden_states.shape
        T = b * s
        x = hidden_states.reshape(T, h)
        logits = jnp.dot(x.astype(jnp.float32), Wr) + br
        aff = jax.nn.sigmoid(logits)
        top_v, top_i = jax.lax.top_k(aff, K)
        top_w = top_v / (jnp.sum(top_v, axis=-1, keepdims=True) + 1e-09)
        top_w = top_w.astype(hidden_states.dtype)
        e_total = Wr.shape[1]
        w_full = jnp.zeros((T, e_total), hidden_states.dtype)
        w_full = w_full.at[jnp.arange(T)[:, None], top_i].set(top_w)
        shared = jnp.dot(silu(jnp.dot(x, Wg_s) + bg_s) * (jnp.dot(x, Wu_s) + bu_s), Wd_s) + bd_s
        gate = silu(jnp.einsum('th,ehi->eti', x, Wg) + bg[:, None, :])
        up = jnp.einsum('th,ehi->eti', x, Wu) + bu[:, None, :]
        down = jnp.einsum('eti,eih->eth', gate * up, Wd) + bd[:, None, :]
        routed = jnp.einsum('te,eth->th', w_full, down)
        return (shared + routed).reshape(b, s, h)
    x = x + _L0_xattn_ref(ctx_1024, _layernorm(x, axis=-1), mask_BxS2_bf1, L0_xattn_ln_x_g, L0_xattn_ln_x_b, L0_xattn_ln_l_g, L0_xattn_ln_l_b, L0_xattn_qn_g, L0_xattn_kn_g, L0_xattn_Wq, L0_xattn_Wkv, L0_xattn_Wout, L0_xattn_bout)
    x = x + _L0_ffn_ref(_layernorm(x, axis=-1), L0_ffn_group_centroids, L0_ffn_expert_centroids, L0_ffn_bias, L0_ffn_wg, L0_ffn_wu, L0_ffn_wd, L0_ffn_sg, L0_ffn_su, L0_ffn_sd)
    x = x + _L1_xattn_ref(_layernorm(x, axis=-1), ctx_1024, ctx_1024, mask_1xSxS2_ff0, L1_xattn_kernel_q, L1_xattn_kernel_k, L1_xattn_kernel_v, L1_xattn_bias_q, L1_xattn_bias_k, L1_xattn_bias_v)
    x = x + _L1_ffn_ref(_layernorm(x, axis=-1), L1_ffn_Wr, L1_ffn_br, L1_ffn_Wg_s, L1_ffn_bg_s, L1_ffn_Wu_s, L1_ffn_bu_s, L1_ffn_Wd_s, L1_ffn_bd_s, L1_ffn_Wg, L1_ffn_bg, L1_ffn_Wu, L1_ffn_bu, L1_ffn_Wd, L1_ffn_bd)
    return x

_drawn_inputs = setup_inputs


def setup_inputs(seed=0):
    import zlib

    import numpy as np

    out = dict(_drawn_inputs(seed))
    spreads = {'L0_xattn_ln_x_g': (1.0, 0.6),
     'L0_xattn_ln_x_b': (0.0, 0.8),
     'L0_xattn_ln_l_g': (1.0, 0.6),
     'L0_xattn_ln_l_b': (0.0, 0.8),
     'L0_xattn_qn_g': (1.0, 0.6),
     'L0_xattn_kn_g': (1.0, 0.6),
     'L0_xattn_bout': (0.0, 0.281),
     'L0_ffn_bias': (0.0, 0.1),
     'L1_ffn_br': (0.0, 0.8),
     'L1_ffn_bg_s': (0.0, 0.8),
     'L1_ffn_bu_s': (0.0, 0.8),
     'L1_ffn_bd_s': (0.0, 2.0),
     'L1_ffn_bg': (0.0, 2.0),
     'L1_ffn_bu': (0.0, 2.0),
     'L1_ffn_bd': (0.0, 2.0)}
    factors = {'L0_xattn_Wq': 5.567,
     'L0_xattn_Wkv': 3.433,
     'L0_xattn_Wout': 3.397,
     'L1_xattn_bias_q': 6.016,
     'L1_xattn_bias_k': 6.188,
     'L1_ffn_Wr': 8.0,
     'L1_ffn_Wg_s': 8.0,
     'L1_ffn_Wu_s': 8.0,
     'L1_ffn_Wd_s': 8.0,
     'L1_ffn_Wg': 8.0,
     'L1_ffn_Wu': 8.0,
     'L1_ffn_Wd': 8.0}
    for name, (base, spread) in spreads.items():
        noise = np.random.default_rng([zlib.crc32(name.encode()), seed]).standard_normal(out[name].shape)
        drawn = base * np.exp(spread * noise) if base else spread * noise
        out[name] = jnp.asarray(drawn.astype(out[name].dtype))
    for name, factor in factors.items():
        out[name] = (out[name] * factor).astype(out[name].dtype)
    return out
```

```python
from contextlib import ExitStack

import concourse.bass as bass
from concourse import mybir


def build(nc, A, out):
    f32, bf16, u8, u32 = mybir.dt.float32, mybir.dt.bfloat16, mybir.dt.uint8, mybir.dt.uint32
    ALU = mybir.AluOpType
    ACT = mybir.ActivationFunctionType
    AX = mybir.AxisListType

    P = 128
    NB, S, D = A["x"].shape
    SC = A["ctx_1024"].shape[1]
    XT = NB * S // P
    CT = NB * SC // P
    CTB = SC // P
    QT = S // P
    KT = CTB + QT
    NKEY = KT * P
    DH = A["L0_xattn_qn_g"].shape[0]
    INNER = A["L0_xattn_Wq"].shape[1]
    HP = INNER // P
    NP = NB * HP
    HA = DH + 2
    NE, _, HID = A["L0_ffn_wg"].shape
    NG = A["L0_ffn_group_centroids"].shape[0]
    EG = NE // NG
    K0 = 4
    CAP = int(NB * S / NE * K0 * 1.25)
    HCAP = CAP // 2
    HT = HID // P
    RING = 8
    E2, _, I2 = A["L1_ffn_Wg"].shape
    K1 = 8
    PR = E2 // 2
    NHALF = NB * S // 512
    BIG_NEG = -1.0e30

    ctx = ExitStack()
    with ctx:
        def sb(name, shape, dt=f32):
            return ctx.enter_context(nc.sbuf_tensor(name, shape, dt))

        def sem(name):
            return ctx.enter_context(nc.semaphore(name))

        slots_in = nc.dram_tensor("slots_in", (NE * CAP, D), f32, kind="Internal").ap()
        slots_out = nc.dram_tensor("slots_out", (NE * CAP, D), f32, kind="Internal").ap()

        ident = sb("ident", [P, P])
        ident_b = sb("ident_b", [P, P], bf16)
        earlier = sb("earlier", [P, P], bf16)
        ones_b = sb("ones_b", [P, P], bf16)
        iota_e = sb("iota_e", [P, NE])
        lower_g = sb("lower_g", [P, NG, NG])
        pair_sel = sb("pair_sel", [96, PR, P], bf16)
        neg_half = sb("neg_half", [P, 32])
        zero_row = sb("zero_row", [P, D])

        vec_rows = sb("vec_rows", [48, P])
        vec = sb("vec", [P, 48])
        mask_u8 = sb("mask_u8", [CT, P], u8)
        mask_f = sb("mask_f", [CT, P])
        mask_bias = sb("mask_bias", [P, CT])
        q_scale = sb("q_scale", [HA, 1])
        cent = sb("cent", [NG + NE, D])
        cent_sq = sb("cent_sq", [NG + NE, D])
        cent_n = sb("cent_n", [NG + NE, 1])
        centT = sb("centT", [D, NG + NE])
        bias0_b = sb("bias0_b", [P, NE])
        bv_b = sb("bv_b", [P, D])
        bout_b = sb("bout_b", [P, D])
        br_b = sb("br_b", [P, E2])
        x_tok = sb("x_tok", [P, XT, D])
        ctx_tok = sb("ctx_tok", [P, CT, D])
        ctxT = sb("ctxT", [D, NB * SC])
        actT = sb("actT", [D, NB, NKEY])
        w_qkv = sb("w_qkv", [D, 3, INNER])
        w_out = sb("w_out", [P, HP, D])
        w_kqv1 = sb("w_kqv1", [D, 3, D])
        kpT = sb("kpT", [D, NB * SC])
        vp = sb("vp", [P, CT, D])
        ff0 = sb("ff0", [P, QT, SC])
        ff0T = sb("ff0T", [P, CTB, S])
        w_sh0 = sb("w_sh0", [D, 2, HID])
        w_shd0 = sb("w_shd0", [P, HT, D])
        w_r1 = sb("w_r1", [D, E2])
        w_sh1 = sb("w_sh1", [D, 2, I2])
        w_shd1 = sb("w_shd1", [I2, D])
        bd_rows = sb("bd_rows", [E2 + 1, D])

        st = sb("st", [P, CT + XT, 6])
        mv = sb("mv", [P, CT + XT, 2])
        ve = sb("ve", [P, CT + XT])
        rstd = sb("rstd", [P, CT + XT])
        h_tok = sb("h_tok", [P, XT, D])
        hT = sb("hT", [D, XT * P])

        act_cur = [sb(f"act_cur{p}", [D, NKEY]) for p in range(2)]
        kq_raw = sb("kq_raw", [P, KT + QT, P])
        kq_sq = sb("kq_sq", [P, KT + QT, P])
        ss = sb("ss", [P, 2 * (KT + QT)])
        ssm = sb("ssm", [P, 2 * (KT + QT)])
        rk = sb("rk", [P, 2 * (KT + QT)])
        kn_aug = sb("kn_aug", [P, KT + QT, 2, HA])
        v_aug = [sb(f"v_aug{p}", [P, KT, 2, DH + 1]) for p in range(2)]
        kT = [sb(f"kT{p}", [HA, 2, NKEY]) for p in range(2)]
        qT = [sb(f"qT{p}", [HA, 2, S]) for p in range(2)]
        kTb = sb("kTb", [HA, 2, NKEY], bf16)
        qTb = sb("qTb", [HA, 2, S], bf16)
        mx4 = sb("mx4", [P, QT, 2])
        negm = sb("negm", [P, QT], bf16)
        pT = [sb(f"pT{p}", [P, 2, S]) for p in range(2)]
        rc = [sb(f"rc{p}", [P, QT]) for p in range(2)]
        o_tok = [sb(f"o_tok{p}", [P, QT, P]) for p in range(2)]
        oT = sb("oT", [P, NP, S])

        rn = sb("rn", [P, XT])
        hsq = kq_sq
        score = sb("score", [P, XT, NG + NE])
        cmp1 = sb("cmp1", [P, XT, NG, NG])
        cmp2 = sb("cmp2", [P, XT, NG, NG])
        gmask = sb("gmask", [P, XT, NG])
        gneg = sb("gneg", [P, XT, NG])
        masked = sb("masked", [P, XT, NE])
        top_v = sb("top_v", [P, XT, 8])
        top_i = sb("top_i", [P, XT, 8], u32)
        top_f = sb("top_f", [P, XT, K0])
        gate = sb("gate", [P, XT, K0])
        gsum = sb("gsum", [P, XT])
        oneh = kq_raw[:, :, :].rearrange("p t (k e) -> p t k e", k=K0)
        ohp = kn_aug[:, :, :, :].rearrange("p t h d -> p (t h d)")[:, 0:XT * K0 * NE] \
            .rearrange("p (t k e) -> p t k e", t=XT, k=K0)
        sel_b = sb("sel_b", [P, XT, NE], bf16)
        posk = sb("posk", [P, XT, K0])
        keep = sb("keep", [P, XT, K0])
        slot_f = sb("slot_f", [P, XT, K0])
        slot_s = sb("slot_s", [P, XT, K0])
        dest_in = sb("dest_in", [P, XT, K0], u32)
        dest_out = sb("dest_out", [P, XT, K0], u32)
        sg_t = [ff0[:, p, :] for p in range(2)]
        hsT = ctx_tok[:, :, :].rearrange("p t d -> p (t d)").rearrange("p (j n) -> p j n", j=HT)

        w_g = [sb(f"w_g{r}", [D, HID]) for r in range(RING)]
        w_u = [sb(f"w_u{r}", [D, HID]) for r in range(RING)]
        w_d = [ctxT[:, r * HT * D:(r + 1) * HT * D].rearrange("p (c d) -> p c d", c=HT) for r in range(RING)]
        spare1 = actT[:, :, :].rearrange("d b k -> d (b k)")
        spare2 = w_qkv[:, :, :].rearrange("d a n -> d (a n)")
        xe = [spare2[0:HCAP, r * 2 * D:(r + 1) * 2 * D].rearrange("p (c d) -> p c d", c=2) for r in range(RING)]
        xeT = [spare1[:, p * CAP:(p + 1) * CAP] for p in range(2)]
        sge, heT = ([spare1[:, (2 + 2 * HT * i + HT * p) * CAP:(2 + 2 * HT * i + HT * (p + 1)) * CAP]
                     .rearrange("p (j c) -> p j c", j=HT) for p in range(2)] for i in range(2))
        ye0 = (2 + 4 * HT) * CAP
        ye = [spare1[0:HCAP, ye0 + p * 2 * D:ye0 + (p + 1) * 2 * D].rearrange("p (c d) -> p c d", c=2)
              for p in range(4)]
        yg = oT[:, :, :].rearrange("p n s -> p (n s)")[:, 0:XT * K0 * D] \
            .rearrange("p (t k d) -> p t k d", t=XT, k=K0)

        ctx_n = oT[:, :, :].rearrange("p n s -> p (n s)")[:, 0:CT * D].rearrange("p (t d) -> p t d", t=CT)

        f_w = [w_g[r][:, :].rearrange("d (a e i) -> d a e i", a=2, e=2) for r in range(4)]
        f_wd = [w_u[r][:, 0:D] for r in range(4)]
        w_tok = sb("w_tok", [P, XT, E2 + 1])
        aff = sb("aff", [P, XT, E2])
        aff2 = sb("aff2", [P, XT, E2])
        top1 = sb("top1", [P, XT, 8])
        tsum = sb("tsum", [P, XT])
        split = v_aug[0][:, :, :, :].rearrange("p t h d -> p (t h d)").bitcast(bf16)[:, 0:XT * 3 * E2] \
            .rearrange("p (t s e) -> p t s e", t=XT, s=3)
        resid = masked
        wT = kT[0][0:E2 + 1, :, :].rearrange("p h k -> p (h k)")[:, 0:XT * P]
        splitT = v_aug[1][:, :, :, :].rearrange("p t h d -> p (t h d)").bitcast(bf16)[0:96, 0:XT * P]
        lg = [spare1[:, p * CTB * S:(p + 1) * CTB * S].rearrange("p (k q) -> p k q", k=CTB) for p in range(2)]
        qpT = spare1[:, 2 * CTB * S:2 * CTB * S + XT * P]
        f_sg, f_t, f_hT = ([spare2[:, (2 * i + p) * 512:(2 * i + p + 1) * 512] for p in range(2)] for i in range(3))


        PS = ctx.enter_context(nc.psum_tensor("PS", [P, 8, 512], f32))

        ld_x, ld_ctx, ld_rows, ld_mask, ld_cent, ld_qkv, ld_k1, ld_bc, ld_ff0, ld_w0, ld_w1 = (
            sem("ld_" + n) for n in "x ctx rows mask cent qkv k1 bc ff0 w0 w1".split())
        rows_clear = sem("rows_clear")
        consts_ready = sem("consts_ready")
        dve_step, pool_step, act_step = sem("dve_step"), sem("pool_step"), sem("act_step")
        slots_cleared = sem("slots_cleared")
        stats0, rstd0, lat1, lat_stats, lat_rstd, norm_x, norm_ctx = (
            sem(n) for n in "stats0 rstd0 lat1 lat_stats lat_rstd norm_x norm_ctx".split())
        cent_ss, cent_rn, cent_ready = sem("cent_ss"), sem("cent_rn"), sem("cent_ready")
        mask_ready, vec_ready = sem("mask_ready"), sem("vec_ready")
        s0_filled, s0_act, s0_dve = sem("s0_filled"), sem("s0_act"), sem("s0_dve")
        xb_ready, mask_cast, vp_ready, op_filled = (sem(n) for n in "xb_ready mask_cast vp_ready op_filled".split())
        nk_step, o2_read, logits_ready, f_gated = (sem(n) for n in "nk_step o2_read logits_ready f_gated".split())
        pool_passed, act_passed = sem("pool_passed"), sem("act_passed")
        n_row_dmas = 12
        cur_done = [sem(f"cur_done{p}") for p in range(2)]
        ss_done, kn_done, cast_done = (sem(n) for n in "ss_done kn_done cast_done".split())
        w_filled, w_act, w_dve = sem("w_filled"), sem("w_act"), sem("w_dve")
        m_filled, m_read, neg_done = sem("m_filled"), sem("m_read"), sem("neg_done")
        st_done, exp_done, pv_done, o_done, rc_done = (
            sem(n) for n in "st_done exp_done pv_done o_done rc_done".split())
        ln_in, ln_stats, ln_rstd, ln_norm, ln_T, ln_evac = (
            sem(n) for n in "ln_in ln_stats ln_rstd ln_norm ln_T ln_evac".split())
        hsq_done, rn_done, scores_ready, top_ready, gexp_done, sel_ready, pos_ready, dest_ready = (
            sem(n) for n in
            "hsq_done rn_done scores_ready top_ready gexp_done sel_ready pos_ready dest_ready".split())
        sh_filled, sh_silu, sh_mul, sh_down, sh_added = (
            sem(n) for n in "sh_filled sh_silu sh_mul sh_down sh_added".split())
        scattered = sem("scattered")
        w_slot = [sem(f"w_slot{r}") for r in range(RING)]
        x_slot = [sem(f"x_slot{r}") for r in range(RING)]
        t_filled, xeT_done, gu_filled, silu_done, he_done, y_filled, y_evac = (
            sem(n) for n in
            "t_filled xeT_done gu_filled silu_done he_done y_filled y_evac".split())
        y_stored = [sem(f"y_stored{r}") for r in range(4)]
        gathered = [sem(f"gathered{t}") for t in range(XT)]
        qp_filled, qp_ready, s2_filled, s2_relu, s2_masked, o2_filled = (
            sem(n) for n in "qp_filled qp_ready s2_filled s2_relu s2_masked o2_filled".split())
        r1_filled, e1_exp, w_tok_ready, split_ready, wT_filled, wT_ready = (
            sem(n) for n in
            "r1_filled e1_exp w_tok_ready split_ready wT_filled wT_ready".split())
        f_filled, f_silu, f_h, f_acc = sem("f_filled"), sem("f_silu"), sem("f_h"), sem("f_acc")
        f_slot = [sem(f"f_slot{r}") for r in range(4)]
        out_ready, out_stored = sem("out_ready"), sem("out_stored")

        SETUP = ([("vec", "dve")] + [("ctx_raw", "act")] * 4 + [("kp", "act")] * 4
                 + [("vp", "dve")] * 4 + [("cent", "dve")]
                 + [("lat", "dve")] * 2 + [("ctx_n", "dve")] * 4 + [("ff0", "act")] * 2)

        def setup_emptied(f):
            who = SETUP[f - 8][1]
            return who, sum(1 for s in SETUP[:f - 7] if s[1] == who)

        def setup_own(kind, k):
            return [i for i, s in enumerate(SETUP) if s[0] == kind][k]

        def work_fills(s):
            v, k = s < NP - 1, s < NP - 2
            return (["V0", "V1"] * v + ["R1"] + ["OT"] * (s > 0) + ["T0", "T1"] * v + ["K0", "K1"] * k
                    + ["T2", "T3", "R0"] * v)

        PRO = ["K0", "K1", "V0", "V1", "T0", "T1", "T2", "T3", "R0", "K2", "K3"]

        E_BANK, M_BANK, O_BANK = 0, 2, 7
        W_BANK = {name: 4 + k % 3 for k, name in enumerate(work_fills(1))} | {"K2": 4, "K3": 5}

        def by_dve(seq):
            return sum(1 for f in seq if f[0] == "T")

        def by_act(seq):
            return len(seq) - by_dve(seq)

        def until_left(seq, name):
            while seq and W_BANK[seq[-1]] != W_BANK[name]:
                seq = seq[:-1]
            return seq

        def work(n, s, name):
            seq = work_fills(s)
            k = seq.index(name)
            every, steady = work_fills(0), work_fills(1)
            short = len(steady) - len(work_fills(NP - 2)) if s == NP - 1 else 0

            def base(count, m):
                return (count(PRO) + count(every) - count(steady) + count(steady) * m - short if s > 0
                        else count(PRO))

            before = PRO if s == 0 else work_fills(s - 1)
            at = until_left((before + seq)[:len(before) + k], name)
            who = "dve" if at[-1][0] == "T" else "act"
            count = by_dve if who == "dve" else by_act
            free = (who, base(count, n) - count(before) + count(at))
            if who == "dve" and short:
                free = (who, free[1] + short)
            dves = by_dve(PRO) + by_dve(steady) * n + by_dve(seq[:k + 1])
            return base(len, n) + k + 1, W_BANK[name], base(by_act, n) + by_act(seq[:k + 1]), dves, free

        def work_pro(name):
            k = PRO.index(name)
            at = until_left(PRO[:k], name)
            free = None if not at else ("dve", by_dve(at)) if at[-1][0] == "T" else ("act", by_act(at))
            return k + 1, W_BANK[name], by_act(PRO[:k + 1]), by_dve(PRO[:k + 1]), free

        def pairs(eng, pair):
            pair(0, 0)
            pair(1, 1)
            with eng.Fori(1, NP // 2 - 1) as q:
                pair(2 * q, 2)
                pair(2 * q + 1, 3)
            pair(NP - 2, NP - 2)
            pair(NP - 1, NP - 1)

        block = ctx.enter_context(nc.Block())

        @block.sync
        def _(sp):
            sp.dma_start(ctx_tok[:, 0:8, :], A["ctx_1024"].rearrange("b (t p) d -> p (b t) d", p=P)[:, 0:8, :]) \
                .then_inc(ld_ctx, 16)
            sp.dma_start(ctx_tok[:, 8:16, :], A["ctx_1024"].rearrange("b (t p) d -> p (b t) d", p=P)[:, 8:16, :]) \
                .then_inc(ld_ctx, 16)
            sp.dma_start(w_kqv1[:, 0, :], A["L1_xattn_kernel_q"][0, 0]).then_inc(ld_k1, 16)
            sp.dma_start(w_kqv1[:, 1, :], A["L1_xattn_kernel_k"][0, 0]).then_inc(ld_k1, 16)
            sp.dma_start(w_kqv1[:, 2, :], A["L1_xattn_kernel_v"][0, 0]).then_inc(ld_k1, 16)
            sp.dma_start(w_qkv[:, 0:2, :], A["L0_xattn_Wkv"].rearrange("d (a n) -> d a n", a=2)) \
                .then_inc(ld_qkv, 16)
            sp.dma_start(w_qkv[:, 2, :], A["L0_xattn_Wq"]).then_inc(ld_qkv, 16)
            sp.dma_start(ff0[:, :, :], A["mask_1xSxS2_ff0"][0].rearrange("(t p) k -> p t k", p=P)) \
                .then_inc(ld_ff0, 16)
            sp.dma_start(w_out[:, :, :], A["L0_xattn_Wout"].rearrange("(c p) d -> p c d", p=P)) \
                .then_inc(ld_w0, 16)
            sp.dma_start(w_sh0[:, 0, :], A["L0_ffn_sg"]).then_inc(ld_w0, 16)
            sp.dma_start(w_sh0[:, 1, :], A["L0_ffn_su"]).then_inc(ld_w0, 16)
            sp.dma_start(w_shd0[:, :, :], A["L0_ffn_sd"].rearrange("(c p) d -> p c d", p=P)) \
                .then_inc(ld_w0, 16)
            sp.dma_start(w_r1[:, :], A["L1_ffn_Wr"]).then_inc(ld_w1, 16)
            sp.dma_start(w_sh1[:, 0, :], A["L1_ffn_Wg_s"]).then_inc(ld_w1, 16)
            sp.dma_start(w_sh1[:, 1, :], A["L1_ffn_Wu_s"]).then_inc(ld_w1, 16)
            sp.dma_start(w_shd1[:, :], A["L1_ffn_Wd_s"]).then_inc(ld_w1, 16)
            sp.dma_start(bd_rows[0:E2, :], A["L1_ffn_bd"]).then_inc(ld_w1, 16)
            sp.dma_start(bd_rows[E2:E2 + 1, :], A["L1_ffn_bd_s"].rearrange("(a d) -> a d", a=1)) \
                .then_inc(ld_w1, 16)
            sp.wait_ge(consts_ready, 9)
            sp.dma_start(slots_in.rearrange("(p a) d -> p a d", p=P),
                         zero_row[:, :].unsqueeze(1).broadcast_to([P, NE * CAP // P, D])) \
                .then_inc(slots_cleared, 16)
            sp.wait_ge(s0_filled, setup_own("vp", 3) + 1)

            def load_weights(e, r):
                sp.dma_start(w_g[r][:, :], A["L0_ffn_wg"][bass.ds(e, 1)].rearrange("a d h -> (a d) h")) \
                    .then_inc(w_slot[r], 16)
                sp.dma_start(w_u[r][:, :], A["L0_ffn_wu"][bass.ds(e, 1)].rearrange("a d h -> (a d) h")) \
                    .then_inc(w_slot[r], 16)
                sp.dma_start(w_d[r][:, :, :],
                             A["L0_ffn_wd"][bass.ds(e, 1)].rearrange("a (c p) d -> p (a c) d", p=P)) \
                    .then_inc(w_slot[r], 16)

            def load_slots(e, r):
                sp.dma_start(xe[r][:, :, :],
                             slots_in[bass.ds(e * CAP, CAP), :].rearrange("(c p) d -> p c d", p=HCAP)) \
                    .then_inc(x_slot[r], 16)

            def store_y(e, k):
                sp.wait_ge(y_evac, e + 1)
                sp.dma_start(slots_out[bass.ds(e * CAP, CAP), :].rearrange("(c p) d -> p c d", p=HCAP),
                             ye[k % 4][:, :, :]).then_inc(y_stored[k % 4], 16)

            for r in range(RING):
                load_weights(r, r)

            def copy_cur(m, p):
                sp.dma_start(act_cur[p][:, :], actT[:, bass.ds(m // HP, 1), :].rearrange("d a k -> d (a k)")) \
                    .then_inc(cur_done[p], 16)

            sp.wait_ge(s0_dve, sum(1 for s in SETUP if s[1] == "dve"))
            copy_cur(0, 0)
            copy_cur(1, 1)
            sp.wait_ge(w_filled, work_pro("V1")[0])
            copy_cur(2, 0)

            def copy_after(n, s):
                sp.wait_ge(w_filled, work(n, s, "V1")[0])
                copy_cur(n + 3, (s + 1) % 2)

            copy_after(0, 0)
            copy_after(1, 1)
            with sp.Fori(1, NP // 2 - 2) as q:
                copy_after(2 * q, 2)
                copy_after(2 * q + 1, 3)
            copy_after(NP - 4, NP - 4)
            sp.wait_ge(scattered, 16 * XT * K0)
            for r in range(RING):
                load_slots(r, r)
            with sp.Fori(0, NE // RING - 1) as q:
                e0 = RING * q
                for k in range(RING):
                    sp.wait_ge(y_filled, e0 + k + 1)
                    load_weights(e0 + RING + k, k)
                    load_slots(e0 + RING + k, k)
                    store_y(e0 + k, k)
            for k in range(RING):
                store_y(NE - RING + k, k)

            def load_pair(j, r):
                dst = f_w[r]
                sp.dma_start(dst[:, 0, :, :], A["L1_ffn_Wg"][bass.ds(2 * j, 2)].rearrange("e d i -> d e i")) \
                    .then_inc(f_slot[r], 16)
                sp.dma_start(dst[:, 1, :, :], A["L1_ffn_Wu"][bass.ds(2 * j, 2)].rearrange("e d i -> d e i")) \
                    .then_inc(f_slot[r], 16)
                sp.dma_start(f_wd[r], A["L1_ffn_Wd"][bass.ds(2 * j, 2)].rearrange("e i d -> (e i) d")) \
                    .then_inc(f_slot[r], 16)

            for r in range(4):
                load_pair(r, r)
            with sp.Fori(0, PR // 4 - 1) as q:
                j0 = 4 * q
                for r in range(4):
                    sp.wait_ge(f_acc, NHALF * (j0 + r + 2))
                    load_pair(j0 + 4 + r, r)
            for t in range(XT):
                sp.wait_ge(out_ready, t + 1)
                sp.dma_start(out.rearrange("b (t p) d -> p (b t) d", p=P)[:, t, :], h_tok[:, t, :]) \
                    .then_inc(out_stored, 16)
            sp.wait_ge(out_stored, 16 * XT)

        @block.gpsimd
        def _(pool):
            g = nc.gpsimd
            pool_n = [0]

            def link(ins):
                pool_n[0] += 1
                ins.then_inc(pool_step, 1)
                pool.wait_ge(pool_step, pool_n[0])

            link(g.memset(ident[:, :], 0.0))
            g.affine_select(out=ident[:, :], in_=ident[:, :], compare_op=ALU.not_equal, fill=1.0, base=0,
                            pattern=[[-1, P]], channel_multiplier=1).then_inc(consts_ready, 1)
            g.memset(neg_half[:, :], -0.5).then_inc(consts_ready, 1)
            pool.wait_ge(consts_ready, 2)
            g.tensor_copy(ident_b[:, :], ident[:, :]).then_inc(consts_ready, 1)
            g.memset(kn_aug[:, :, :, :], 0.0).then_inc(consts_ready, 1)
            link(g.memset(ones_b[:, :], 1.0))
            g.affine_select(out=earlier[:, :], in_=ones_b[:, :], compare_op=ALU.is_gt, fill=0.0, base=0,
                            pattern=[[1, P]], channel_multiplier=-1).then_inc(consts_ready, 1)
            g.iota(iota_e[:, :], pattern=[[1, NE]], base=0, channel_multiplier=0,
                   allow_small_or_imprecise_dtypes=True).then_inc(consts_ready, 1)
            link(g.memset(lower_g[:, :, :], 1.0))
            g.affine_select(out=lower_g[:, :, :], in_=lower_g[:, :, :], compare_op=ALU.is_gt, fill=0.0,
                            base=0, pattern=[[1, NG], [-1, NG]], channel_multiplier=0) \
                .then_inc(consts_ready, 1)
            g.memset(w_tok[:, :, E2:E2 + 1], 1.0).then_inc(consts_ready, 1)
            g.memset(zero_row[:, :], 0.0).then_inc(consts_ready, 1)
            pool.wait_ge(stats0, XT)
            link(g.tensor_scalar(ve[:, CT:], mv[:, CT:, 1], 1e-5, None, ALU.add))
            g.tensor_tensor(rstd[:, CT:], ve[:, CT:], neg_half[:, 0:XT], ALU.pow).then_inc(rstd0, 1)
            pool.wait_ge(stats0, CT + XT)
            link(g.tensor_scalar(ve[:, 0:CT], mv[:, 0:CT, 1], 1e-5, None, ALU.add))
            g.tensor_tensor(rstd[:, 0:CT], ve[:, 0:CT], neg_half[:, 0:CT], ALU.pow).then_inc(rstd0, 1)
            pool.wait_ge(lat_stats, XT)
            link(g.tensor_scalar(ve[:, CT:], mv[:, CT:, 1], 1e-5, None, ALU.add))
            g.tensor_tensor(rstd[:, CT:], ve[:, CT:], neg_half[:, 0:XT], ALU.pow).then_inc(lat_rstd, 1)
            pool.wait_ge(ld_bc, 64)
            g.tensor_tensor(x_tok[:, :, :], x_tok[:, :, :], bout_b[:, :].unsqueeze(1).broadcast_to([P, XT, D]),
                            ALU.add).then_inc(xb_ready, 1)
            pool.wait_ge(ld_cent, 32)
            g.tensor_tensor(cent_sq[:, :], cent[:, :], cent[:, :], ALU.mult).then_inc(cent_ss, 1)
            pool.wait_ge(cent_ss, 2)
            link(g.tensor_scalar(cent_n[:, :], cent_n[:, :], 1e-24, None, ALU.max))
            link(g.tensor_tensor(cent_n[:, :], cent_n[:, :], neg_half[0:NG + NE, 0:1], ALU.pow))
            g.tensor_scalar(cent[:, :], cent[:, :], cent_n[:, 0:1], None, ALU.mult).then_inc(cent_ready, 1)
            link(g.memset(pair_sel[:, :, :], 0.0))
            for s in range(3):
                view = pair_sel[32 * s:32 * s + 32, :, :].rearrange("p j (c i) -> p j c i", c=2)
                g.affine_select(out=view, in_=view, compare_op=ALU.not_equal, fill=1.0, base=0,
                                pattern=[[-2, PR], [-1, 2], [0, I2]], channel_multiplier=1) \
                    .then_inc(consts_ready, 1)

            pool.wait_ge(consts_ready, 12)
            g.memset(kn_aug[:, 0:KT, :, DH:DH + 1], 1.0).then_inc(consts_ready, 1)
            g.memset(kn_aug[:, KT:KT + QT, :, DH + 1:DH + 2], 1.0).then_inc(consts_ready, 1)
            for p in range(2):
                g.memset(v_aug[p][:, :, :, DH:DH + 1], 1.0).then_inc(consts_ready, 1)
            pool.wait_ge(consts_ready, 16)

            def stand_alone():
                pool.sem_inc(pool_passed, 1)

            def norm_heads(m, t3_count):
                b = m // HP
                for j in range(2):
                    tiles, cols = slice(4 * j, 4 * j + 4), slice(8 * j, 8 * j + 8)
                    pool.wait_ge(ss_done, 2 * m + j + 1)
                    stand_alone()
                    g.tensor_scalar(ssm[:, cols], ss[:, cols], 1.0 / DH, 1e-16, ALU.mult, ALU.max) \
                        .then_inc(nk_step, 1)
                    pool.wait_ge(nk_step, 4 * m + 2 * j + 1)
                    g.tensor_tensor(rk[:, cols], ssm[:, cols], neg_half[:, 0:8], ALU.pow).then_inc(nk_step, 1)
                    pool.wait_ge(nk_step, 4 * m + 2 * j + 2)
                    if j == 0 and t3_count is not None:
                        pool.wait_ge(w_filled, t3_count)
                        stand_alone()
                    g.tensor_tensor(
                        kn_aug[:, tiles, :, 0:DH],
                        kq_raw[:, tiles, :].rearrange("p t (h d) -> p t h d", h=2),
                        rk[:, cols].rearrange("p (t h) -> p t h", h=2).unsqueeze(3).broadcast_to([P, 4, 2, DH]),
                        ALU.mult).then_inc(kn_done, 1)
                    if j == 0:
                        g.tensor_copy(
                            kn_aug[:, 0:CTB, :, DH + 1:DH + 2].rearrange("p t h a -> p t (h a)"),
                            mask_bias[:, bass.ds(b * CTB, CTB)].unsqueeze(2).broadcast_to([P, CTB, 2])) \
                            .then_inc(kn_done, 1)

            def norm_of(n, s):
                norm_heads(n + 2, work(n, s, "T3")[0])

            pool.wait_ge(mask_ready, 1)
            norm_heads(0, None)
            norm_heads(1, work_pro("T3")[0])
            norm_of(0, 0)
            norm_of(1, 1)
            with pool.Fori(1, NP // 2 - 1) as q:
                norm_of(2 * q, 2)
                norm_of(2 * q + 1, 3)

            def ln_pow(k):
                pool.wait_ge(ln_stats, XT * (k + 1))
                link(g.tensor_scalar(ve[:, 0:XT], mv[:, 0:XT, 1], 1e-5, None, ALU.add))
                g.tensor_tensor(rstd[:, 0:XT], ve[:, 0:XT], neg_half[:, 0:XT], ALU.pow).then_inc(ln_rstd, 1)

            ln_pow(0)
            pool.wait_ge(ln_norm, XT)
            g.tensor_tensor(hsq[:, :, :], h_tok[:, :, :], h_tok[:, :, :], ALU.mult).then_inc(hsq_done, 1)
            pool.wait_ge(hsq_done, 2)
            link(g.tensor_scalar(rn[:, :], rn[:, :], 1e-24, None, ALU.max))
            g.tensor_tensor(rn[:, :], rn[:, :], neg_half[:, 0:XT], ALU.pow).then_inc(rn_done, 1)
            pool.wait_ge(slots_cleared, 16)
            pool.wait_ge(dest_ready, 2)
            for t in range(XT):
                for k in range(K0):
                    g.indirect_dma_start(
                        out=slots_in[:, :],
                        out_offset=bass.IndirectOffsetOnAxis(ap=dest_in[:, t, k:k + 1], axis=0),
                        in_=h_tok[:, t, :], in_offset=None,
                        bounds_check=NE * CAP - 1, oob_is_err=False).then_inc(scattered, 16)
            for r in range(4):
                pool.wait_ge(y_stored[r], 16 * NE // 4)
            for t in range(XT):
                for k in range(K0):
                    g.indirect_dma_start(
                        out=yg[:, t, k, :], out_offset=None, in_=slots_out[:, :],
                        in_offset=bass.IndirectOffsetOnAxis(ap=dest_out[:, t, k:k + 1], axis=0),
                        bounds_check=NE * CAP - 1, oob_is_err=False).then_inc(gathered[t], 16)
            ln_pow(1)
            for i in range(2 * NB):
                b, c = i // 2, i % 2
                pool.wait_ge(s2_relu, i + 1)
                g.tensor_tensor(lg[b % 2][:, 2 * c:2 * c + 2, :], lg[b % 2][:, 2 * c:2 * c + 2, :],
                                ff0T[:, 2 * c:2 * c + 2, :], ALU.add).then_inc(s2_masked, 1)
            ln_pow(2)

        @block.tensor
        def _(pe):
            t = nc.tensor

            def emptied(free):
                if free is not None:
                    pe.wait_ge(w_act if free[0] == "act" else w_dve, free[1])

            def setup_bank(f):
                if f >= 8:
                    who, n = setup_emptied(f)
                    pe.wait_ge(s0_act if who == "act" else s0_dve, n)
                return f % 8

            pe.wait_ge(consts_ready, 2)
            for f, (kind, _) in enumerate(SETUP):
                k = f - setup_own(kind, 0)
                bank = setup_bank(f)
                if kind == "vec":
                    pe.wait_ge(ld_rows, 16 * n_row_dmas)
                    pe.wait_ge(mask_cast, 1)
                    t.transpose(PS[:, bank, 0:48], vec_rows[:, :], ident[0:48, 0:48])
                    last = t.transpose(PS[:, bank, 64:64 + CT], mask_f[:, :], ident[0:CT, 0:CT])
                elif kind == "ctx_raw":
                    pe.wait_ge(ld_ctx, 32)
                    for i in range(4):
                        last = t.transpose(PS[:, bank, i * P:(i + 1) * P], ctx_tok[:, 4 * k + i, :], ident[:, :])
                elif kind == "kp":
                    pe.wait_ge(ld_k1, 48)
                    pe.wait_ge(s0_act, k + 1)
                    last = t.matmul(PS[:, bank, :], w_kqv1[:, 1, :], ctxT[:, 512 * k:512 * (k + 1)],
                                    start=True, stop=True)
                elif kind == "vp":
                    pe.wait_ge(s0_act, 4)
                    for i in range(4):
                        last = t.matmul(PS[:, bank, i * P:(i + 1) * P], ctxT[:, (4 * k + i) * P:(4 * k + i + 1) * P],
                                        w_kqv1[:, 2, :], start=True, stop=True)
                elif kind == "cent":
                    pe.wait_ge(cent_ready, 1)
                    last = t.transpose(PS[:, bank, 0:NG + NE], cent[:, :], ident[0:NG + NE, 0:NG + NE])
                elif kind == "lat":
                    pe.wait_ge(norm_x, 4 * k + 4)
                    for i in range(4):
                        last = t.transpose(PS[:, bank, i * P:(i + 1) * P], h_tok[:, 4 * k + i, :], ident[:, :])
                elif kind == "ctx_n":
                    pe.wait_ge(norm_ctx, 4 * k + 4)
                    for i in range(4):
                        last = t.transpose(PS[:, bank, i * P:(i + 1) * P], ctx_n[:, 4 * k + i, :], ident[:, :])
                elif kind == "ff0":
                    pe.wait_ge(ld_ff0, 16)
                    for i in range(CTB):
                        last = t.transpose(PS[:, bank, i * P:(i + 1) * P], ff0[:, k, i * P:(i + 1) * P], ident[:, :])
                last.then_inc(s0_filled, 1)
            pe.wait_ge(s0_act, sum(1 for s in SETUP if s[1] == "act"))
            pe.wait_ge(s0_dve, sum(1 for s in SETUP if s[1] == "dve"))

            def project(m, s, name, info):
                _, bank, _, _, free = info
                emptied(free)
                half = int(name[1]) % 2
                if name[0] == "K" and half == 0:
                    pe.wait_ge(cur_done[s % 2], (m - s % 2) * 8 + 16)
                cols = bass.ds(m % HP * P, P)
                for i in range(2 if name == "V1" else 4):
                    tile_i = 4 * half + i
                    a = 1 if name[0] == "V" else 2 if tile_i >= KT else 0
                    if tile_i >= KT:
                        tile_i -= QT
                    last = t.matmul(PS[:, bank, i * P:(i + 1) * P], act_cur[s % 2][:, tile_i * P:(tile_i + 1) * P],
                                    w_qkv[:, a, cols], start=True, stop=True)
                last.then_inc(w_filled, 1)

            def turn(m, name, info):
                _, bank, _, _, free = info
                emptied(free)
                j = int(name[1])
                if j < 2:
                    pe.wait_ge(kn_done, 3 * m + 2 + j)
                for i in range(4):
                    last = t.transpose(PS[0:HA, bank, i * P:(i + 1) * P],
                                       kn_aug[:, 4 * (j % 2) + i, j // 2, :], ident[:, :])
                last.then_inc(w_filled, 1)

            def maxima(n, h, js):
                for j in js:
                    qt, c = j // 2, j % 2
                    pe.wait_ge(cast_done, 4 * n + 2 * h + 2)
                    if not (isinstance(n, int) and 8 * n + 4 * h + j < 2):
                        pe.wait_ge(m_read, 8 * n + 4 * h + j - 1)
                    t.matmul(PS[:, M_BANK + j % 2, 0:NKEY // 2], qTb[:, h, qt * P:(qt + 1) * P],
                             kTb[:, h, c * (NKEY // 2):(c + 1) * (NKEY // 2)], start=True, stop=True) \
                        .then_inc(m_filled, 1)

            def shift_row(n, h, info):
                _, bank, _, _, free = info
                emptied(free)
                pe.wait_ge(neg_done, 2 * n + h + 1)
                for qt in range(QT):
                    last = t.matmul(PS[DH:DH + 1, bank, qt * P:(qt + 1) * P], negm[:, qt:qt + 1], ident_b[:, :],
                                    start=True, stop=True)
                last.then_inc(w_filled, 1)

            def by_act_before(n, s):
                return work(n, s, "R1")[2] - (3 if s < NP - 1 else 1)

            def scores(n, s, c, row_count):
                h, kc = c // 3, c % 3
                if kc == 0:
                    pe.wait_ge(w_act, row_count)
                if not (s == 0 and c < 2):
                    pe.wait_ge(exp_done, 6 * n + c - 1)
                for kt in range(2):
                    last = t.matmul(PS[:, E_BANK + c % 2, kt * S:(kt + 1) * S],
                                    kT[s % 2][:, h, (2 * kc + kt) * P:(2 * kc + kt + 1) * P],
                                    qT[s % 2][:, h, :], start=True, stop=True)
                last.then_inc(st_done, 1)

            def weigh(n, s, c):
                h, kc = c // 3, c % 3
                pe.wait_ge(exp_done, 6 * n + c + 1)
                if kc == 0 and not (s == 0 and h == 0):
                    pe.wait_ge(o_done, 2 * n + h)
                for kt in range(2):
                    for qt in range(QT):
                        last = t.matmul(PS[:, O_BANK, qt * (DH + 1):(qt + 1) * (DH + 1)],
                                        pT[c % 2][:, kt, qt * P:(qt + 1) * P], v_aug[s % 2][:, 2 * kc + kt, h, :],
                                        start=(kc == 0 and kt == 0 and qt == 0), stop=(kc == 2 and kt == 1),
                                        skip_group_check=True)
                last.then_inc(pv_done, 1)

            def turn_out(n, s, info):
                _, bank, _, _, free = info
                emptied(free)
                pe.wait_ge(o_done, 2 * n + 2)
                for qt in range(QT):
                    last = t.transpose(PS[:, bank, qt * P:(qt + 1) * P], o_tok[s % 2][:, qt, :], ident[:, :])
                last.then_inc(w_filled, 1)

            pe.wait_ge(ld_qkv, 32)
            for name in ("K0", "K1", "V0", "V1"):
                project(0, 0, name, work_pro(name))
            for name in ("T0", "T1", "T2", "T3"):
                turn(0, name, work_pro(name))
            maxima(0, 0, range(4))
            shift_row(0, 0, work_pro("R0"))
            for name in ("K2", "K3"):
                project(1, 1, name, work_pro(name))

            def pair(n, s):
                def w(name):
                    return work(n, s, name)

                last, kq = s > NP - 2, s < NP - 2
                if s > 0:
                    weigh(n - 1, s - 1, 5)
                scores(n, s, 0, work_pro("R0")[2] if s == 0 else by_act_before(n, s))
                maxima(n, 1, (0, 1))
                if not last:
                    project(n + 1, s + 1, "V0", w("V0"))
                scores(n, s, 1, None)
                weigh(n, s, 0)
                maxima(n, 1, (2, 3))
                if not last:
                    project(n + 1, s + 1, "V1", w("V1"))
                scores(n, s, 2, None)
                weigh(n, s, 1)
                shift_row(n, 1, w("R1"))
                if s > 0:
                    turn_out(n - 1, s - 1, w("OT"))
                if not last:
                    turn(n + 1, "T0", w("T0"))
                    turn(n + 1, "T1", w("T1"))
                if kq:
                    project(n + 2, s + 2, "K0", w("K0"))
                scores(n, s, 3, w("R1")[2])
                weigh(n, s, 2)
                if kq:
                    project(n + 2, s + 2, "K1", w("K1"))
                if not last:
                    turn(n + 1, "T2", w("T2"))
                    turn(n + 1, "T3", w("T3"))
                    maxima(n + 1, 0, (0, 1))
                scores(n, s, 4, None)
                weigh(n, s, 3)
                if not last:
                    maxima(n + 1, 0, (2, 3))
                scores(n, s, 5, None)
                weigh(n, s, 4)
                if not last:
                    shift_row(n + 1, 0, w("R0"))

            pairs(pe, pair)
            weigh(NP - 1, NP - 1, 5)
            END = work(NP - 1, NP - 1, "OT")
            pe.wait_ge(w_act, END[2])
            pe.wait_ge(o_done, 2 * NP)
            for qt in range(QT):
                last = t.transpose(PS[:, W_BANK["OT"], qt * P:(qt + 1) * P], o_tok[(NP - 1) % 2][:, qt, :], ident[:, :])
            last.then_inc(w_filled, 1)

            pe.wait_ge(ld_w0, 64)
            pe.wait_ge(w_act, END[2] + 1)
            pe.wait_ge(exp_done, 6 * NP)
            pe.wait_ge(m_read, 8 * NP)
            for i in range(XT):
                b, qt = i // QT, i % QT
                for c in range(HP):
                    last = t.matmul(PS[:, i, 0:D], oT[:, b * HP + c, qt * P:(qt + 1) * P], w_out[:, c, :],
                                    start=(c == 0), stop=(c == HP - 1))
                last.then_inc(op_filled, 1)

            def turn_h(k):
                for i in range(XT):
                    if i % 4 == 0:
                        pe.wait_ge(ln_norm, XT * k + i + 4)
                    last = t.transpose(PS[:, i // 4, (i % 4) * P:(i % 4 + 1) * P], h_tok[:, i, :], ident[:, :])
                    if i % 4 == 3:
                        last.then_inc(ln_T, 1)

            turn_h(0)
            pe.wait_ge(ln_evac, 2)
            for i in range(XT):
                last = t.matmul(PS[:, 6, i * (NG + NE):(i + 1) * (NG + NE)], hT[:, i * P:(i + 1) * P], centT[:, :],
                                start=True, stop=True)
            last.then_inc(scores_ready, 1)

            def shared_up(v):
                j, half = v // 2, v % 2
                if v >= 2:
                    pe.wait_ge(sh_mul, v - 1)
                for a in range(2):
                    last = t.matmul(PS[:, 2 + 2 * a + v % 2, :], w_sh0[:, a, j * P:(j + 1) * P],
                                    hT[:, half * 512:(half + 1) * 512], start=True, stop=True)
                last.then_inc(sh_filled, 1)

            shared_up(0)
            shared_up(1)
            pe.wait_ge(sel_ready, 1)
            for i in range(XT):
                for j in range(i + 1):
                    last = t.matmul(PS[:, 7, i * NE:(i + 1) * NE], earlier[:, :] if j == i else ones_b[:, :],
                                    sel_b[:, j, :], start=(j == 0), stop=(j == i))
            last.then_inc(pos_ready, 1)
            shared_up(2)
            shared_up(3)
            pe.wait_ge(sh_mul, 4)
            for i in range(XT):
                for j in range(HT):
                    last = t.matmul(PS[:, i // 4, (i % 4) * P:(i % 4 + 1) * P], hsT[:, j, i * P:(i + 1) * P],
                                    w_shd0[:, j, :], start=(j == 0), stop=(j == HT - 1))
                if i % 4 == 3:
                    last.then_inc(sh_down, 1)

            pe.wait_ge(sh_added, 2)

            def expert(e, k, up, down, turn_in=True):
                if turn_in:
                    pe.wait_ge(x_slot[k], (e - k) * 2 + 16)
                    if up:
                        if not (isinstance(e, int) and e < 2):
                            pe.wait_ge(xeT_done, e - 1)
                    for c in range(2):
                        last = t.transpose(PS[:, k % 2, c * HCAP:(c + 1) * HCAP], xe[k][:, c, :],
                                           ident[0:HCAP, 0:HCAP])
                    last.then_inc(t_filled, 1)
                if up:
                    r = (k - 1) % RING
                    pe.wait_ge(xeT_done, e)
                    pe.wait_ge(w_slot[r], (e - 1 - r) * 6 + 48)
                    if not (isinstance(e, int) and e < 3):
                        pe.wait_ge(he_done, e - 2)
                    for a, w in enumerate((w_g[r], w_u[r])):
                        for j in range(HT):
                            last = t.matmul(PS[:, 2 + 2 * a + r % 2, j * CAP:(j + 1) * CAP],
                                            w[:, j * P:(j + 1) * P], xeT[r % 2][:, :], start=True, stop=True)
                    last.then_inc(gu_filled, 1)
                if down:
                    r = (k - 2) % RING
                    pe.wait_ge(he_done, e - 1)
                    if not (isinstance(e, int) and e < 4):
                        pe.wait_ge(y_evac, e - 3)
                    for c in range(2):
                        for j in range(HT):
                            last = t.matmul(PS[0:HCAP, 6 + r % 2, c * D:(c + 1) * D],
                                            heT[r % 2][:, j, c * HCAP:(c + 1) * HCAP], w_d[r][:, j, :],
                                            start=(j == 0), stop=(j == HT - 1))
                    last.then_inc(y_filled, 1)

            for e in range(RING):
                expert(e, e, e >= 1, e >= 2)
            with pe.Fori(1, NE // RING) as q:
                e0 = RING * q
                for k in range(RING):
                    expert(e0 + k, k, True, True)
            expert(NE, 0, True, True, turn_in=False)
            expert(NE + 1, 1, False, True, turn_in=False)

            turn_h(1)
            pe.wait_ge(ln_evac, 4)
            pe.wait_ge(he_done, NE)
            for half in range(2):
                t.matmul(PS[:, 2 + half, :], w_kqv1[:, 0, :], hT[:, half * 512:(half + 1) * 512],
                         start=True, stop=True).then_inc(qp_filled, 1)
            pe.wait_ge(qp_ready, 2)
            pe.wait_ge(y_evac, NE)

            def scores1(i):
                b, c = i // 2, i % 2
                if i >= 2:
                    pe.wait_ge(s2_relu, i - 1)
                for kt in range(2):
                    col = b * SC + (2 * c + kt) * P
                    last = t.matmul(PS[:, 4 + i % 2, kt * S:(kt + 1) * S], kpT[:, col:col + P],
                                    qpT[:, b * S:(b + 1) * S], start=True, stop=True)
                last.then_inc(s2_filled, 1)

            def weigh1(b):
                pe.wait_ge(s2_masked, 2 * b + 2)
                if b >= 2:
                    pe.wait_ge(o2_read, b - 1)
                for qt in range(QT):
                    for kt in range(CTB):
                        last = t.matmul(PS[:, 6 + b % 2, qt * D:(qt + 1) * D], lg[b % 2][:, kt, qt * P:(qt + 1) * P],
                                        vp[:, b * CTB + kt, :], start=(kt == 0), stop=(kt == CTB - 1))
                last.then_inc(o2_filled, 1)

            for b in range(NB):
                scores1(2 * b)
                scores1(2 * b + 1)
                if b:
                    weigh1(b - 1)
            weigh1(NB - 1)

            turn_h(2)
            pe.wait_ge(ln_evac, 6)
            pe.wait_ge(ld_w1, 96)
            for i in range(XT):
                last = t.matmul(PS[:, 6, i * E2:(i + 1) * E2], hT[:, i * P:(i + 1) * P], w_r1[:, :],
                                start=True, stop=True)
            last.then_inc(r1_filled, 1)

            def up1(v, v0, w_gate, w_up, rows, spread=None):
                half = v0 % 2
                if not (isinstance(v, int) and v < 2):
                    pe.wait_ge(f_h, v - 1)
                cols = hT[:, half * 512:(half + 1) * 512]
                t.matmul(PS[0:rows, 0 + half, :], w_gate, cols, start=True, stop=True)
                last = t.matmul(PS[0:rows, 2 + half, :], w_up, cols, start=True, stop=True)
                if spread is not None:
                    last = t.matmul(PS[:, 4 + half, :], spread, splitT[:, half * 512:(half + 1) * 512],
                                    start=True, stop=True)
                last.then_inc(f_filled, 1)

            def down1(v, half, w, rows, first=False):
                pe.wait_ge(f_h, v + 1)
                for q in range(4):
                    last = t.matmul(PS[:, 6 + half, q * D:(q + 1) * D], f_hT[half][0:rows, q * P:(q + 1) * P], w,
                                    start=(first and q == 0), stop=True, skip_group_check=True)
                last.then_inc(f_acc, 1)

            for half in range(2):
                up1(half, half, w_sh1[:, 0, :], w_sh1[:, 1, :], I2)
            pe.wait_ge(w_tok_ready, 1)
            for i in range(XT):
                last = t.transpose(PS[0:E2 + 1, 4 + i // 4, (i % 4) * P:(i % 4 + 1) * P], w_tok[:, i, :], ident[:, :])
                if i % 4 == 3:
                    last.then_inc(wT_filled, 1)
            pe.wait_ge(split_ready, 1)
            split_ps = PS[:, 7, :].bitcast(bf16)
            for i in range(XT):
                last = t.transpose(split_ps[0:96, i * P:(i + 1) * P], split[:, i, :, :].rearrange("p s e -> p (s e)"),
                                   ident_b[:, :])
            last.then_inc(wT_filled, 1)
            pe.wait_ge(wT_ready, 3)
            for half in range(2):
                down1(half, half, w_shd1[:, :], I2, first=True)
            for half in range(2):
                for q in range(4):
                    t.matmul(PS[:, 6 + half, q * D:(q + 1) * D], wT[:, (4 * half + q) * P:(4 * half + q + 1) * P],
                             bd_rows[:, :], start=False, stop=True, skip_group_check=True)

            def unit(j, r, half, down):
                v = 2 * j + 2 + half
                if half == 0:
                    pe.wait_ge(f_slot[r], (j - r) * 12 + 48)
                up1(v, half, f_w[r][:, 0, :, :].rearrange("d e i -> d (e i)"),
                    f_w[r][:, 1, :, :].rearrange("d e i -> d (e i)"), P,
                    spread=pair_sel[:, bass.ds(j, 1), :].rearrange("p a c -> p (a c)"))
                if down:
                    rd = r if half else (r - 1) % 4
                    down1(v - 1, 1 - half, f_wd[rd], P)

            unit(0, 0, 0, False)
            unit(0, 0, 1, True)
            for r in range(1, 4):
                unit(r, r, 0, True)
                unit(r, r, 1, True)
            with pe.Fori(1, PR // 4) as q:
                j0 = 4 * q
                for r in range(4):
                    unit(j0 + r, r, 0, True)
                    unit(j0 + r, r, 1, True)
            down1(2 * PR + 1, 1, f_wd[3], P)

        @block.scalar
        def _(act):
            s_ = nc.scalar
            act.dma_start(x_tok[:, :, :], A["x"].rearrange("b (t p) d -> p (b t) d", p=P)).then_inc(ld_x, 16)
            act.dma_start(mask_u8[:, :], A["mask_BxS2_bf1"].rearrange("b (t p) -> (b t) p", p=P)) \
                .then_inc(ld_mask, 16)
            act.dma_start(cent[0:NG, :], A["L0_ffn_group_centroids"]).then_inc(ld_cent, 16)
            act.dma_start(cent[NG:, :], A["L0_ffn_expert_centroids"]).then_inc(ld_cent, 16)
            act.wait_ge(rows_clear, 1)

            def row(i, name, lo, n):
                act.dma_start(vec_rows[i:i + 1, lo:lo + n], A[name].rearrange("(a n) -> a n", a=1)) \
                    .then_inc(ld_rows, 16)

            for i, name in enumerate(("L0_xattn_ln_x_g", "L0_xattn_ln_x_b", "L0_xattn_ln_l_g", "L0_xattn_ln_l_b",
                                      "L1_xattn_bias_q", "L1_xattn_bias_k")):
                row(i, name, 0, P)
            for i, name in enumerate(("L0_xattn_qn_g", "L0_xattn_kn_g", "L1_ffn_bg_s", "L1_ffn_bu_s")):
                row(6 + i, name, 0, DH)
            act.dma_start(vec_rows[10:10 + PR, :], A["L1_ffn_bg"].rearrange("(j e) i -> j (e i)", e=2)) \
                .then_inc(ld_rows, 16)
            act.dma_start(vec_rows[10 + PR:10 + 2 * PR, :], A["L1_ffn_bu"].rearrange("(j e) i -> j (e i)", e=2)) \
                .then_inc(ld_rows, 16)
            for dst, name, n in ((bias0_b, "L0_ffn_bias", NE), (bv_b, "L1_xattn_bias_v", D),
                                 (bout_b, "L0_xattn_bout", D), (br_b, "L1_ffn_br", E2)):
                act.dma_start(dst[:, :], A[name].partition_broadcast(P)).then_inc(ld_bc, 16)

            for f, (kind, who) in enumerate(SETUP):
                if who != "act":
                    continue
                k = f - setup_own(kind, 0)
                src = PS[:, f % 8, :]
                act.wait_ge(s0_filled, f + 1)
                if kind == "ctx_raw":
                    s_.activation(ctxT[:, 512 * k:512 * (k + 1)], src, ACT.Copy).then_inc(s0_act, 1)
                elif kind == "kp":
                    act.wait_ge(vec_ready, 1)
                    s_.activation(kpT[:, 512 * k:512 * (k + 1)], src, ACT.Relu, bias=vec[:, 5:6]) \
                        .then_inc(s0_act, 1)
                elif kind == "ff0":
                    s_.activation(ff0T[:, :, k * P:(k + 1) * P], src.rearrange("p (c q) -> p c q", c=CTB), ACT.Copy) \
                        .then_inc(s0_act, 1)

            def keep_v(s, name, info):
                count, bank, _, _, _ = info
                act.wait_ge(w_filled, count)
                lo, hi = (0, 4) if name == "V0" else (4, KT)
                s_.activation(v_aug[s % 2][:, lo:hi, :, 0:DH],
                              PS[:, bank, 0:(hi - lo) * P].rearrange("p (t h d) -> p t h d", t=hi - lo, h=2),
                              ACT.Copy).then_inc(w_act, 1)

            def keep_kq(m, s, j, info):
                count, bank, _, _, _ = info
                act.wait_ge(w_filled, count)
                if j == 0 and s > 0:
                    act.wait_ge(kn_done, 3 * m)
                src = PS[:, bank, :].rearrange("p (t n) -> p t n", t=4)
                s_.activation(kq_sq[:, 4 * j:4 * j + 4, :], src, ACT.Square)
                s_.activation(kq_raw[:, 4 * j:4 * j + 4, :], src, ACT.Copy).then_inc(w_act, 1)

            def cast(s, name, info):
                act.wait_ge(w_dve, info[3])
                h = int(name[1]) // 2
                if int(name[1]) % 2 == 0:
                    s_.activation(kTb[:, h, 0:4 * P], kT[s % 2][:, h, 0:4 * P], ACT.Copy).then_inc(cast_done, 1)
                else:
                    s_.activation(kTb[:, h, 4 * P:6 * P], kT[s % 2][:, h, 4 * P:6 * P], ACT.Copy)
                    s_.activation(qTb[:, h, :], qT[s % 2][:, h, :], ACT.Copy).then_inc(cast_done, 1)

            def keep_row(s, h, info):
                count, bank, _, _, _ = info
                act.wait_ge(w_filled, count)
                s_.activation(qT[s % 2][DH:DH + 1, h, :], PS[DH:DH + 1, bank, 0:S], ACT.Copy).then_inc(w_act, 1)

            def keep_out(n, count, bank):
                act.wait_ge(w_filled, count)
                act.sem_inc(act_passed, 1)
                s_.activation(oT[:, bass.ds(n, 1), :].rearrange("p a s -> p (a s)"), PS[:, bank, 0:S], ACT.Copy) \
                    .then_inc(w_act, 1)

            def exps(n, s, c):
                act.wait_ge(st_done, 6 * n + c + 1)
                if not (s == 0 and c < 2):
                    act.wait_ge(pv_done, 6 * n + c - 1)
                s_.activation(pT[c % 2][:, :, :], PS[:, E_BANK + c % 2, :].rearrange("p (k q) -> p k q", k=2),
                              ACT.Exp).then_inc(exp_done, 1)

            for j in range(2):
                keep_kq(0, 0, j, work_pro(f"K{j}"))
            for name in ("V0", "V1"):
                keep_v(0, name, work_pro(name))
            for name in ("T0", "T1", "T2", "T3"):
                cast(0, name, work_pro(name))
            keep_row(0, 0, work_pro("R0"))
            for j in range(2):
                keep_kq(1, 1, j, work_pro(f"K{2 + j}"))

            def pair(n, s):
                def w(name):
                    return work(n, s, name)

                last, kq = s > NP - 2, s < NP - 2
                exps(n, s, 0)
                if not last:
                    keep_v(s + 1, "V0", w("V0"))
                exps(n, s, 1)
                if not last:
                    keep_v(s + 1, "V1", w("V1"))
                exps(n, s, 2)
                keep_row(s, 1, w("R1"))
                if s > 0:
                    keep_out(n - 1, w("OT")[0], w("OT")[1])
                if not last:
                    cast(s + 1, "T0", w("T0"))
                    cast(s + 1, "T1", w("T1"))
                if kq:
                    keep_kq(n + 2, s + 2, 0, w("K0"))
                exps(n, s, 3)
                if kq:
                    keep_kq(n + 2, s + 2, 1, w("K1"))
                if not last:
                    cast(s + 1, "T2", w("T2"))
                    cast(s + 1, "T3", w("T3"))
                exps(n, s, 4)
                exps(n, s, 5)
                if not last:
                    keep_row(s + 1, 0, w("R0"))

            pairs(act, pair)
            keep_out(NP - 1, work(NP - 1, NP - 1, "OT")[0] + 1, W_BANK["OT"])

            def keep_hT(k):
                for i in range(2):
                    act.wait_ge(ln_T, 2 * k + i + 1)
                    s_.activation(hT[:, 512 * i:512 * (i + 1)], PS[:, i, :], ACT.Copy).then_inc(ln_evac, 1)

            keep_hT(0)

            def shared_silu(v):
                act.wait_ge(sh_filled, v + 1)
                if v >= 2:
                    act.wait_ge(sh_mul, v - 1)
                s_.activation(sg_t[v % 2][:, :], PS[:, 2 + v % 2, :], ACT.Silu).then_inc(sh_silu, 1)

            shared_silu(0)
            shared_silu(1)
            act.wait_ge(top_ready, 1)
            s_.activation(gate[:, :, :], gate[:, :, :], ACT.Exp).then_inc(gexp_done, 1)
            shared_silu(2)
            shared_silu(3)

            def expert(e, k, up, turn_in=True):
                if turn_in:
                    act.wait_ge(t_filled, e + 1)
                    if not (isinstance(e, int) and e < 2):
                        act.wait_ge(gu_filled, e - 1)
                    s_.activation(xeT[k % 2][:, :], PS[:, k % 2, 0:CAP], ACT.Copy).then_inc(xeT_done, 1)
                if up:
                    r = (k - 1) % RING
                    act.wait_ge(gu_filled, e)
                    if not (isinstance(e, int) and e < 3):
                        act.wait_ge(he_done, e - 2)
                    s_.activation(sge[r % 2][:, :, :], PS[:, 2 + r % 2, 0:HT * CAP].rearrange("p (j c) -> p j c", j=HT),
                                  ACT.Silu).then_inc(silu_done, 1)

            for e in range(RING):
                expert(e, e, e >= 1)
            with act.Fori(1, NE // RING) as q:
                e0 = RING * q
                for k in range(RING):
                    expert(e0 + k, k, True)
            expert(NE, 0, True, turn_in=False)

            keep_hT(1)
            for half in range(2):
                act.wait_ge(qp_filled, half + 1)
                s_.activation(qpT[:, half * 512:(half + 1) * 512], PS[:, 2 + half, :], ACT.Relu, bias=vec[:, 4:5]) \
                    .then_inc(qp_ready, 1)
            for i in range(2 * NB):
                b, c = i // 2, i % 2
                act.wait_ge(s2_filled, i + 1)
                if b >= 2:
                    act.wait_ge(o2_filled, b - 1)
                s_.activation(lg[b % 2][:, 2 * c:2 * c + 2, :], PS[:, 4 + i % 2, :].rearrange("p (k q) -> p k q", k=2),
                              ACT.Relu, scale=float(D) ** -0.5).then_inc(s2_relu, 1)

            keep_hT(2)
            act.wait_ge(logits_ready, 1)
            s_.activation(aff2[:, :, :], aff[:, :, :], ACT.Exp, scale=-1.0).then_inc(e1_exp, 1)

            def silu1(v, half, rows, bias):
                act.wait_ge(f_filled, v + 1)
                if not (isinstance(v, int) and v < 2):
                    act.wait_ge(f_h, v - 1)
                act.sem_inc(act_passed, 1)
                s_.activation(f_sg[half][0:rows, :], PS[0:rows, half, :], ACT.Silu, bias=bias).then_inc(f_silu, 1)

            for half in range(2):
                silu1(half, half, I2, vec[0:I2, 8:9])
            for i in range(2):
                act.wait_ge(wT_filled, i + 1)
                s_.activation(wT[:, 512 * i:512 * (i + 1)], PS[0:E2 + 1, 4 + i, :], ACT.Copy).then_inc(wT_ready, 1)
            act.wait_ge(wT_filled, 3)
            s_.activation(splitT[:, :], PS[:, 7, :].bitcast(bf16)[0:96, 0:XT * P], ACT.Copy).then_inc(wT_ready, 1)
            with act.Fori(0, PR) as j:
                for half in range(2):
                    silu1(2 * j + 2 + half, half, P, vec[:, bass.ds(10 + j, 1)])

        @block.vector
        def _(dve):
            v_ = nc.vector
            dve_n = [0]

            def link(ins):
                dve_n[0] += 1
                ins.then_inc(dve_step, 1)
                dve.wait_ge(dve_step, dve_n[0])

            def normalize(dst, src, t):
                return v_.tensor_scalar(dst, src, mv[:, t, 0:1], rstd[:, t:t + 1], ALU.subtract, ALU.mult)

            v_.memset(vec_rows[:, :], 0.0).then_inc(rows_clear, 1)
            link(v_.memset(q_scale[:, :], 1.0))
            dve.wait_ge(ld_x, 16)
            for i in range(XT):
                last = v_.bn_stats(st[:, CT + i, :], x_tok[:, i, :])
            link(last)
            for i in range(XT):
                v_.bn_aggr(mv[:, CT + i, :], st[:, CT + i, :]).then_inc(stats0, 1)
            dve.wait_ge(ld_mask, 16)
            v_.tensor_copy(mask_f[:, :], mask_u8[:, :]).then_inc(mask_cast, 1)
            dve.wait_ge(ld_ctx, 32)
            for i in range(CT):
                last = v_.bn_stats(st[:, i, :], ctx_tok[:, i, :])
            link(last)
            for i in range(CT):
                v_.bn_aggr(mv[:, i, :], st[:, i, :]).then_inc(stats0, 1)
            dve.wait_ge(rstd0, 1)
            for i in range(XT):
                last = normalize(h_tok[:, i, :], x_tok[:, i, :], CT + i)
            link(last)
            for i in range(XT):
                last = v_.bn_stats(st[:, CT + i, :], h_tok[:, i, :])
            link(last)
            for i in range(XT):
                v_.bn_aggr(mv[:, CT + i, :], st[:, CT + i, :]).then_inc(lat_stats, 1)
            dve.wait_ge(rstd0, 2)
            for i in range(CT):
                normalize(ctx_n[:, i, :], ctx_tok[:, i, :], i).then_inc(norm_ctx, 1)
            dve.wait_ge(lat_rstd, 1)
            for i in range(XT):
                normalize(h_tok[:, i, :], h_tok[:, i, :], CT + i).then_inc(norm_x, 1)
            dve.wait_ge(cent_ss, 1)
            v_.tensor_reduce(cent_n[:, :], cent_sq[:, :], AX.X, ALU.add).then_inc(cent_ss, 1)
            for f, (kind, who) in enumerate(SETUP):
                if who != "dve":
                    continue
                k = f - setup_own(kind, 0)
                src = PS[:, f % 8, :]
                dve.wait_ge(s0_filled, f + 1)
                if kind == "vec":
                    v_.tensor_copy(vec[:, :], src[:, 0:48]).then_inc(vec_ready, 1)
                    v_.tensor_scalar(mask_bias[:, :], src[:, 64:64 + CT], -BIG_NEG, BIG_NEG, ALU.mult, ALU.add) \
                        .then_inc(mask_ready, 1)
                    dve.wait_ge(mask_ready, 1)
                    v_.scalar_tensor_tensor(q_scale[0:DH, :], vec[0:DH, 6:7], float(DH) ** -0.5, vec[0:DH, 7:8],
                                            ALU.mult, ALU.mult).then_inc(s0_dve, 1)
                elif kind == "vp":
                    dve.wait_ge(ld_bc, 64)
                    dst = vp[:, 4 * k:4 * k + 4, :]
                    v_.tensor_tensor(dst, src.rearrange("p (t d) -> p t d", t=4),
                                     bv_b[:, :].unsqueeze(1).broadcast_to([P, 4, D]), ALU.add).then_inc(s0_dve, 1)
                elif kind == "cent":
                    v_.tensor_copy(centT[:, :], src[:, 0:NG + NE]).then_inc(s0_dve, 1)
                elif kind == "lat":
                    v_.tensor_scalar(actT[:, 2 * k:2 * k + 2, SC:NKEY], src.rearrange("p (b s) -> p b s", b=2),
                                     vec[:, 2:3], vec[:, 3:4], ALU.mult, ALU.add).then_inc(s0_dve, 1)
                elif kind == "ctx_n":
                    v_.tensor_scalar(actT[:, k, 0:SC], src, vec[:, 0:1], vec[:, 1:2], ALU.mult, ALU.add) \
                        .then_inc(s0_dve, 1)
            dve.wait_ge(s0_dve, sum(1 for f in SETUP if f[1] == "dve"))
            v_.tensor_scalar(vp[:, :, :], vp[:, :, :], 0.0, None, ALU.max).then_inc(vp_ready, 1)

            def sum_squares(j, w_act_count):
                dve.wait_ge(w_act, w_act_count)
                v_.tensor_reduce(ss[:, 8 * j:8 * j + 8],
                                 kq_sq[:, 4 * j:4 * j + 4, :].rearrange("p t (h d) -> p (t h) d", h=2), AX.X, ALU.add) \
                    .then_inc(ss_done, 1)

            def keep_turned(s, name, info):
                count, bank, _, _, _ = info
                dve.wait_ge(w_filled, count)
                h = int(name[1]) // 2
                if int(name[1]) % 2 == 0:
                    v_.tensor_copy(kT[s % 2][:, h, 0:4 * P], PS[0:HA, bank, :]).then_inc(w_dve, 1)
                else:
                    v_.tensor_copy(kT[s % 2][:, h, 4 * P:6 * P], PS[0:HA, bank, 0:2 * P])
                    v_.tensor_scalar(qT[s % 2][:, h, :], PS[0:HA, bank, 2 * P:4 * P], q_scale[:, 0:1], None,
                                     ALU.mult).then_inc(w_dve, 1)

            def row_maxima(n, h):
                for j in range(4):
                    dve.wait_ge(m_filled, 8 * n + 4 * h + j + 1)
                    v_.tensor_reduce(mx4[:, j // 2, j % 2:j % 2 + 1], PS[:, M_BANK + j % 2, 0:NKEY // 2], AX.X,
                                     ALU.max).then_inc(m_read, 1)
                dve.wait_ge(m_read, 8 * n + 4 * h + 4)
                v_.tensor_reduce(negm[:, :], mx4[:, :, :], AX.X, ALU.max, negate=True).then_inc(neg_done, 1)

            def divide(n, s, h):
                src = PS[:, O_BANK, 0:QT * (DH + 1)].rearrange("p (q d) -> p q d", q=QT)
                dve.wait_ge(pv_done, 6 * n + 3 * h + 3)
                v_.reciprocal(rc[h][:, :], src[:, :, DH]).then_inc(rc_done, 1)
                dve.wait_ge(rc_done, 2 * n + h + 1)
                v_.tensor_tensor(o_tok[s % 2][:, :, h * DH:(h + 1) * DH], src[:, :, 0:DH],
                                 rc[h][:, :].unsqueeze(2).broadcast_to([P, QT, DH]), ALU.mult).then_inc(o_done, 1)

            for j in range(2):
                sum_squares(j, work_pro(f"K{j}")[2])
            for name in ("T0", "T1", "T2", "T3"):
                keep_turned(0, name, work_pro(name))
            row_maxima(0, 0)
            for j in range(2):
                sum_squares(j, work_pro(f"K{2 + j}")[2])

            def pair(n, s):
                last, kq = s > NP - 2, s < NP - 2
                if s > 0:
                    divide(n - 1, s - 1, 1)
                row_maxima(n, 1)
                if not last:
                    for name in ("T0", "T1"):
                        keep_turned(s + 1, name, work(n, s, name))
                divide(n, s, 0)
                if kq:
                    sum_squares(0, work(n, s, "K0")[2])
                if not last:
                    for name in ("T2", "T3"):
                        keep_turned(s + 1, name, work(n, s, name))
                    row_maxima(n + 1, 0)
                if kq:
                    sum_squares(1, work(n, s, "K1")[2])

            pairs(dve, pair)
            divide(NP - 1, NP - 1, 1)

            dve.wait_ge(xb_ready, 1)
            for i in range(XT):
                dve.wait_ge(op_filled, i + 1)
                last = v_.tensor_tensor(x_tok[:, i, :], x_tok[:, i, :], PS[:, i, 0:D], ALU.add)
            link(last)

            def layernorm(k):
                for i in range(XT):
                    last = v_.bn_stats(st[:, i, :], x_tok[:, i, :])
                link(last)
                for i in range(XT):
                    v_.bn_aggr(mv[:, i, :], st[:, i, :]).then_inc(ln_stats, 1)
                dve.wait_ge(ln_rstd, k + 1)
                for i in range(XT):
                    normalize(h_tok[:, i, :], x_tok[:, i, :], i).then_inc(ln_norm, 1)

            layernorm(0)
            dve.wait_ge(hsq_done, 1)
            v_.tensor_reduce(rn[:, :], hsq[:, :, :], AX.X, ALU.add).then_inc(hsq_done, 1)
            dve.wait_ge(rn_done, 1)
            dve.wait_ge(scores_ready, 1)
            link(v_.tensor_tensor(score[:, :, :],
                                  PS[:, 6, 0:XT * (NG + NE)].rearrange("p (t g) -> p t g", t=XT),
                                  rn[:, :].unsqueeze(2).broadcast_to([P, XT, NG + NE]), ALU.mult))
            gs = score[:, :, 0:NG]
            other = gs.unsqueeze(2).broadcast_to([P, XT, NG, NG])
            own = gs.unsqueeze(3).broadcast_to([P, XT, NG, NG])
            v_.tensor_tensor(cmp1[:, :, :, :], other, own, ALU.is_gt)
            link(v_.tensor_tensor(cmp2[:, :, :, :], other, own, ALU.is_equal))
            link(v_.tensor_tensor(cmp2[:, :, :, :], cmp2[:, :, :, :],
                                  lower_g[:, :, :].unsqueeze(1).broadcast_to([P, XT, NG, NG]), ALU.mult))
            link(v_.tensor_tensor(cmp1[:, :, :, :], cmp1[:, :, :, :], cmp2[:, :, :, :], ALU.add))
            link(v_.tensor_reduce(gmask[:, :, :], cmp1[:, :, :, :], AX.X, ALU.add))
            link(v_.tensor_scalar(gmask[:, :, :], gmask[:, :, :], float(NG // 2), None, ALU.is_lt))
            v_.tensor_scalar(gneg[:, :, :], gmask[:, :, :], 1e9, -1e9, ALU.mult, ALU.add)
            link(v_.tensor_tensor(masked[:, :, :], score[:, :, NG:], bias0_b[:, :].unsqueeze(1)
                                  .broadcast_to([P, XT, NE]), ALU.add))
            by_group = masked[:, :, :].rearrange("p t (g e) -> p t g e", g=NG)
            link(v_.tensor_tensor(by_group, by_group, gmask[:, :, :].unsqueeze(3)
                                  .broadcast_to([P, XT, NG, EG]), ALU.mult))
            link(v_.tensor_tensor(by_group, by_group, gneg[:, :, :].unsqueeze(3)
                                  .broadcast_to([P, XT, NG, EG]), ALU.add))
            for i in range(XT):
                last = v_.max(top_v[:, i, :], masked[:, i, :])
            link(last)
            for i in range(XT):
                last = v_.max_index(top_i[:, i, :], top_v[:, i, :], masked[:, i, :])
            v_.tensor_tensor(gate[:, :, :], top_v[:, :, 0:K0], top_v[:, :, 0:1].broadcast_to([P, XT, K0]),
                             ALU.subtract).then_inc(top_ready, 1)
            dve.wait_ge(top_ready, 1)
            link(v_.tensor_copy(top_f[:, :, :], top_i[:, :, 0:K0]))
            link(v_.tensor_tensor(oneh[:, :, :, :], iota_e[:, :].unsqueeze(1).unsqueeze(1)
                                  .broadcast_to([P, XT, K0, NE]),
                                  top_f[:, :, :].unsqueeze(3).broadcast_to([P, XT, K0, NE]), ALU.is_equal))
            with nc.allow_low_precision(reason="zeros and ones, exact in bfloat16"):
                v_.tensor_reduce(sel_b[:, :, :], oneh[:, :, :, :].rearrange("p t k e -> p t e k"), AX.X, ALU.add) \
                    .then_inc(sel_ready, 1)
            dve.wait_ge(gexp_done, 1)
            link(v_.tensor_reduce(gsum[:, :], gate[:, :, :], AX.X, ALU.add))
            link(v_.reciprocal(gsum[:, :], gsum[:, :]))
            link(v_.tensor_tensor(gate[:, :, :], gate[:, :, :], gsum[:, :].unsqueeze(2).broadcast_to([P, XT, K0]),
                                  ALU.mult))
            dve.wait_ge(pos_ready, 1)
            link(v_.tensor_tensor(ohp[:, :, :, :], oneh[:, :, :, :],
                                  PS[:, 7, 0:XT * NE].rearrange("p (t e) -> p t e", t=XT).unsqueeze(2)
                                  .broadcast_to([P, XT, K0, NE]), ALU.mult))
            link(v_.tensor_reduce(posk[:, :, :], ohp[:, :, :, :], AX.X, ALU.add))
            v_.tensor_scalar(keep[:, :, :], posk[:, :, :], float(CAP), None, ALU.is_lt)
            link(v_.tensor_scalar(slot_s[:, :, :], posk[:, :, :], float(CAP - 1), None, ALU.min))
            link(v_.scalar_tensor_tensor(slot_f[:, :, :], top_f[:, :, :], float(CAP), slot_s[:, :, :],
                                         ALU.mult, ALU.add))
            v_.tensor_copy(dest_out[:, :, :], slot_f[:, :, :]).then_inc(dest_ready, 1)
            link(v_.scalar_tensor_tensor(posk[:, :, :], keep[:, :, :], -1e6, slot_f[:, :, :], ALU.mult, ALU.add))
            v_.tensor_scalar(dest_in[:, :, :], posk[:, :, :], 1e6, None, ALU.add).then_inc(dest_ready, 1)
            link(v_.tensor_tensor(gate[:, :, :], gate[:, :, :], keep[:, :, :], ALU.mult))
            for v in range(4):
                j, half = v // 2, v % 2
                dve.wait_ge(sh_silu, v + 1)
                v_.tensor_tensor(hsT[:, j, half * 512:(half + 1) * 512], sg_t[v % 2][:, :], PS[:, 4 + v % 2, :],
                                 ALU.mult).then_inc(sh_mul, 1)
            for i in range(2):
                dve.wait_ge(sh_down, i + 1)
                rows = x_tok[:, 4 * i:4 * i + 4, :]
                v_.tensor_tensor(rows, rows, PS[:, i, :].rearrange("p (t d) -> p t d", t=4), ALU.add) \
                    .then_inc(sh_added, 1)

            def expert(e, k, up, down):
                if up:
                    r = (k - 1) % RING
                    dve.wait_ge(silu_done, e)
                    if not (isinstance(e, int) and e < 3):
                        dve.wait_ge(y_filled, e - 2)
                    v_.tensor_tensor(heT[r % 2][:, :, :], sge[r % 2][:, :, :],
                                     PS[:, 4 + r % 2, 0:HT * CAP].rearrange("p (j c) -> p j c", j=HT), ALU.mult) \
                        .then_inc(he_done, 1)
                if down:
                    r = (k - 2) % RING
                    dve.wait_ge(y_filled, e - 1)
                    if not (isinstance(e, int) and e < 6):
                        dve.wait_ge(y_stored[r % 4], (e - 2 - r % 4) * 4)
                    v_.tensor_copy(ye[r % 4][:, :, :], PS[0:HCAP, 6 + r % 2, 0:2 * D]
                                   .rearrange("p (c d) -> p c d", c=2)).then_inc(y_evac, 1)

            for e in range(RING):
                expert(e, e, e >= 1, e >= 2)
            with dve.Fori(1, NE // RING) as q:
                e0 = RING * q
                for k in range(RING):
                    expert(e0 + k, k, True, True)
            expert(NE, 0, True, True)
            expert(NE + 1, 1, False, True)
            dve.wait_ge(sh_added, 2)
            for i in range(XT):
                dve.wait_ge(gathered[i], 16 * K0)
                for k in range(K0):
                    link(v_.scalar_tensor_tensor(x_tok[:, i, :], yg[:, i, k, :], gate[:, i, k:k + 1], x_tok[:, i, :],
                                                 ALU.mult, ALU.add))
            layernorm(1)

            for b in range(NB):
                dve.wait_ge(o2_filled, b + 1)
                rows = x_tok[:, QT * b:QT * (b + 1), :]
                v_.scalar_tensor_tensor(rows, PS[:, 6 + b % 2, 0:QT * D].rearrange("p (q d) -> p q d", q=QT), 0.0,
                                        rows, ALU.max, ALU.add).then_inc(o2_read, 1)
            dve.wait_ge(o2_read, NB)
            layernorm(2)

            dve.wait_ge(r1_filled, 1)
            v_.tensor_tensor(aff[:, :, :], PS[:, 6, 0:XT * E2].rearrange("p (t e) -> p t e", t=XT),
                             br_b[:, :].unsqueeze(1).broadcast_to([P, XT, E2]), ALU.add).then_inc(logits_ready, 1)
            dve.wait_ge(e1_exp, 1)
            link(v_.tensor_scalar(aff2[:, :, :], aff2[:, :, :], 1.0, None, ALU.add))
            link(v_.reciprocal(aff[:, :, :], aff2[:, :, :]))
            for i in range(XT):
                last = v_.max(top1[:, i, :], aff[:, i, :])
            link(last)
            link(v_.tensor_reduce(tsum[:, :], top1[:, :, :], AX.X, ALU.add))
            link(v_.tensor_scalar(tsum[:, :], tsum[:, :], 1e-9, None, ALU.add))
            link(v_.reciprocal(tsum[:, :], tsum[:, :]))
            for i in range(XT):
                last = v_.match_replace(aff2[:, i, :], top1[:, i, :], aff[:, i, :], -1.0)
            link(last)
            link(v_.tensor_tensor(aff2[:, :, :], aff2[:, :, :], aff[:, :, :], ALU.not_equal))
            link(v_.tensor_tensor(aff[:, :, :], aff[:, :, :], aff2[:, :, :], ALU.mult))
            v_.tensor_tensor(w_tok[:, :, 0:E2], aff[:, :, :], tsum[:, :].unsqueeze(2).broadcast_to([P, XT, E2]),
                             ALU.mult).then_inc(w_tok_ready, 1)
            dve.wait_ge(w_tok_ready, 1)
            link(v_.tensor_copy(split[:, :, 0, :], w_tok[:, :, 0:E2]))
            link(v_.tensor_tensor(resid[:, :, :], w_tok[:, :, 0:E2], split[:, :, 0, :], ALU.subtract))
            link(v_.tensor_copy(split[:, :, 1, :], resid[:, :, :]))
            link(v_.tensor_tensor(resid[:, :, :], resid[:, :, :], split[:, :, 1, :], ALU.subtract))
            v_.tensor_copy(split[:, :, 2, :], resid[:, :, :]).then_inc(split_ready, 1)

            def gated(v, half, rows, bias, weighted=True):
                dve.wait_ge(f_silu, v + 1)
                if not (isinstance(v, int) and v < 2):
                    dve.wait_ge(f_acc, v - 1)
                dst = f_t[half] if weighted else f_hT[half]
                ins = v_.scalar_tensor_tensor(dst[0:rows, :], PS[0:rows, 2 + half, :], bias, f_sg[half][0:rows, :],
                                              ALU.add, ALU.mult)
                if weighted:
                    ins.then_inc(f_gated, 1)
                    dve.wait_ge(f_gated, v - 1)
                    v_.tensor_tensor(f_hT[half][:, :], f_t[half][:, :], PS[:, 4 + half, :], ALU.mult) \
                        .then_inc(f_h, 1)
                else:
                    ins.then_inc(f_h, 1)

            for half in range(2):
                gated(half, half, I2, vec[0:I2, 9:10], weighted=False)
            with dve.Fori(0, PR) as j:
                for half in range(2):
                    gated(2 * j + 2 + half, half, P, vec[:, bass.ds(10 + PR + j, 1)])
            for i in range(XT):
                dve.wait_ge(f_acc, 2 * PR + 2 if i >= 4 else 2 * PR + 1)
                v_.tensor_tensor(h_tok[:, i, :], x_tok[:, i, :], PS[:, 6 + i // 4, (i % 4) * D:(i % 4 + 1) * D],
                                 ALU.add).then_inc(out_ready, 1)


def kernel(**inputs):
    import numpy as np
    import concourse.bacc as bacc
    from concourse.bass_utils import run_bass_kernel_spmd

    nc = bacc.Bacc("TRN2", target_bir_lowering=False, num_devices=1)
    arrays, aps = {}, {}
    for name, value in inputs.items():
        a = np.ascontiguousarray(value)
        arrays[f"in_{name}"] = a
        aps[name] = nc.dram_tensor(f"in_{name}", a.shape, mybir.dt.from_np(a.dtype), kind="ExternalInput").ap()
    out = nc.dram_tensor("out_x", arrays["in_x"].shape, mybir.dt.float32, kind="ExternalOutput").ap()
    build(nc, aps, out)
    r = run_bass_kernel_spmd(nc, [arrays], core_ids=[0])
    return r.results[0]["out_x"]
```

```python
from contextlib import ExitStack

import concourse.bass as bass
from concourse import mybir


def build(nc, A, out):
    f32, bf16, u8, u32 = mybir.dt.float32, mybir.dt.bfloat16, mybir.dt.uint8, mybir.dt.uint32
    ALU = mybir.AluOpType
    ACT = mybir.ActivationFunctionType
    AX = mybir.AxisListType

    P = 128
    NB, S, D = A["x"].shape
    SC = A["ctx_1024"].shape[1]
    XT = NB * S // P
    CT = NB * SC // P
    CTB = SC // P
    QT = S // P
    KT = CTB + QT
    NKEY = KT * P
    DH = A["L0_xattn_qn_g"].shape[0]
    INNER = A["L0_xattn_Wq"].shape[1]
    HP = INNER // P
    NP = NB * HP
    HA = DH + 2
    NE, _, HID = A["L0_ffn_wg"].shape
    NG = A["L0_ffn_group_centroids"].shape[0]
    EG = NE // NG
    K0 = 4
    CAP = int(NB * S / NE * K0 * 1.25)
    HCAP = CAP // 2
    HT = HID // P
    RING = 8
    E2, _, I2 = A["L1_ffn_Wg"].shape
    K1 = 8
    PR = E2 // 2
    NHALF = NB * S // 512
    BIG_NEG = -1.0e30

    ctx = ExitStack()
    with ctx:
        def sb(name, shape, dt=f32):
            return ctx.enter_context(nc.sbuf_tensor(name, shape, dt))

        def sem(name):
            return ctx.enter_context(nc.semaphore(name))

        slots_in = nc.dram_tensor("slots_in", (NE * CAP, D), f32, kind="Internal").ap()
        slots_out = nc.dram_tensor("slots_out", (NE * CAP, D), f32, kind="Internal").ap()

        ident = sb("ident", [P, P])
        ident_b = sb("ident_b", [P, P], bf16)
        earlier = sb("earlier", [P, P], bf16)
        ones_b = sb("ones_b", [P, P], bf16)
        iota_e = sb("iota_e", [P, NE])
        lower_g = sb("lower_g", [P, NG, NG])
        pair_sel = sb("pair_sel", [96, PR, P], bf16)
        neg_half = sb("neg_half", [P, 32])
        zero_row = sb("zero_row", [P, D])

        vec_rows = sb("vec_rows", [48, P])
        vec = sb("vec", [P, 48])
        mask_u8 = sb("mask_u8", [CT, P], u8)
        mask_f = sb("mask_f", [CT, P])
        mask_bias = sb("mask_bias", [P, CT])
        q_scale = sb("q_scale", [HA, 1])
        cent = sb("cent", [NG + NE, D])
        cent_sq = sb("cent_sq", [NG + NE, D])
        cent_n = sb("cent_n", [NG + NE, 1])
        centT = sb("centT", [D, NG + NE])
        bias0_b = sb("bias0_b", [P, NE])
        bv_b = sb("bv_b", [P, D])
        bout_b = sb("bout_b", [P, D])
        br_b = sb("br_b", [P, E2])
        x_tok = sb("x_tok", [P, XT, D])
        ctx_tok = sb("ctx_tok", [P, CT, D])
        ctxT = sb("ctxT", [D, NB * SC])
        actT = sb("actT", [D, NB, NKEY])
        w_qkv = sb("w_qkv", [D, 3, INNER])
        w_out = sb("w_out", [P, HP, D])
        w_kqv1 = sb("w_kqv1", [D, 3, D])
        kpT = sb("kpT", [D, NB * SC])
        vp = sb("vp", [P, CT, D])
        ff0 = sb("ff0", [P, QT, SC])
        ff0T = sb("ff0T", [P, CTB, S])
        w_sh0 = sb("w_sh0", [D, 2, HID])
        w_shd0 = sb("w_shd0", [P, HT, D])
        w_r1 = sb("w_r1", [D, E2])
        w_sh1 = sb("w_sh1", [D, 2, I2])
        w_shd1 = sb("w_shd1", [I2, D])
        bd_rows = sb("bd_rows", [E2 + 1, D])

        st = sb("st", [P, CT + XT, 6])
        mv = sb("mv", [P, CT + XT, 2])
        ve = sb("ve", [P, CT + XT])
        rstd = sb("rstd", [P, CT + XT])
        h_tok = sb("h_tok", [P, XT, D])
        hT = sb("hT", [D, XT * P])

        act_cur = [sb(f"act_cur{p}", [D, NKEY]) for p in range(2)]
        kq_raw = sb("kq_raw", [P, KT + QT, P])
        kq_sq = sb("kq_sq", [P, KT + QT, P])
        ss = sb("ss", [P, 2 * (KT + QT)])
        ssm = sb("ssm", [P, 2 * (KT + QT)])
        rk = sb("rk", [P, 2 * (KT + QT)])
        kn_aug = sb("kn_aug", [P, KT + QT, 2, HA])
        v_cur = [sb(f"v_cur{p}", [P, KT, 2, DH]) for p in range(2)]
        kT = [sb(f"kT{p}", [HA, 2, NKEY]) for p in range(2)]
        qT = [sb(f"qT{p}", [HA, 2, S]) for p in range(2)]
        kTb = sb("kTb", [HA, 2, NKEY], bf16)
        qTb = sb("qTb", [HA, 2, S], bf16)
        negm = sb("negm", [P, 2 * QT], bf16)
        pT = [sb(f"pT{p}", [P, 2, S]) for p in range(3)]
        p_sum = [sb(f"p_sum{p}", [P, 2, S]) for p in range(2)]
        rcT = sb("rcT", [P, S])
        ones_f = sb("ones_f", [P, P])
        oT = sb("oT", [P, NP, S])

        rn = sb("rn", [P, XT])
        hsq = kq_sq
        score = sb("score", [P, XT, NG + NE])
        cmp1, cmp2 = (p_sum[p][:, :, :].rearrange("p h q -> p (h q)").rearrange("p (t g e) -> p t g e", t=XT, g=NG)
                      for p in range(2))
        gmask = sb("gmask", [P, XT, NG])
        gneg = sb("gneg", [P, XT, NG])
        masked = sb("masked", [P, XT, NE])
        top_v = sb("top_v", [P, XT, 8])
        top_i = sb("top_i", [P, XT, 8], u32)
        top_f = sb("top_f", [P, XT, K0])
        gate = sb("gate", [P, XT, K0])
        gsum = sb("gsum", [P, XT])
        oneh = kq_raw[:, :, :].rearrange("p t (k e) -> p t k e", k=K0)
        ohp = kn_aug[:, :, :, :].rearrange("p t h d -> p (t h d)")[:, 0:XT * K0 * NE] \
            .rearrange("p (t k e) -> p t k e", t=XT, k=K0)
        sel_b = sb("sel_b", [P, XT, NE], bf16)
        posk = sb("posk", [P, XT, K0])
        keep = sb("keep", [P, XT, K0])
        slot_f = sb("slot_f", [P, XT, K0])
        slot_s = sb("slot_s", [P, XT, K0])
        dest_in = sb("dest_in", [P, XT, K0], u32)
        dest_out = sb("dest_out", [P, XT, K0], u32)
        sg_t = [ff0[:, p, :] for p in range(2)]
        hsT = ctx_tok[:, :, :].rearrange("p t d -> p (t d)").rearrange("p (j n) -> p j n", j=HT)

        w_g = [sb(f"w_g{r}", [D, HID]) for r in range(RING)]
        w_u = [sb(f"w_u{r}", [D, HID]) for r in range(RING)]
        w_d = [ctxT[:, r * HT * D:(r + 1) * HT * D].rearrange("p (c d) -> p c d", c=HT) for r in range(RING)]
        spare1 = actT[:, :, :].rearrange("d b k -> d (b k)")
        spare2 = w_qkv[:, :, :].rearrange("d a n -> d (a n)")
        xe = [spare2[0:HCAP, r * 2 * D:(r + 1) * 2 * D].rearrange("p (c d) -> p c d", c=2) for r in range(RING)]
        xeT = [spare1[:, p * CAP:(p + 1) * CAP] for p in range(2)]
        sge, heT = ([spare1[:, (2 + 2 * HT * i + HT * p) * CAP:(2 + 2 * HT * i + HT * (p + 1)) * CAP]
                     .rearrange("p (j c) -> p j c", j=HT) for p in range(2)] for i in range(2))
        ye0 = (2 + 4 * HT) * CAP
        ye = [spare1[0:HCAP, ye0 + p * 2 * D:ye0 + (p + 1) * 2 * D].rearrange("p (c d) -> p c d", c=2)
              for p in range(4)]
        yg = oT[:, :, :].rearrange("p n s -> p (n s)")[:, 0:XT * K0 * D] \
            .rearrange("p (t k d) -> p t k d", t=XT, k=K0)

        ctx_n = oT[:, :, :].rearrange("p n s -> p (n s)")[:, 0:CT * D].rearrange("p (t d) -> p t d", t=CT)

        f_w = [w_g[r][:, :].rearrange("d (a e i) -> d a e i", a=2, e=2) for r in range(4)]
        f_wd = [w_u[r][:, 0:D] for r in range(4)]
        w_tok = sb("w_tok", [P, XT, E2 + 1])
        aff, aff2 = (pT[p][:, 0, :].rearrange("p (t e) -> p t e", t=XT) for p in range(2))
        top1 = sb("top1", [P, XT, 8])
        tsum = sb("tsum", [P, XT])
        split = v_cur[0][:, :, :, :].rearrange("p t h d -> p (t h d)").bitcast(bf16)[:, 0:XT * 3 * E2] \
            .rearrange("p (t s e) -> p t s e", t=XT, s=3)
        resid = masked
        wT = kT[0][0:E2 + 1, :, :].rearrange("p h k -> p (h k)")[:, 0:XT * P]
        splitT = v_cur[1][:, :, :, :].rearrange("p t h d -> p (t h d)").bitcast(bf16)[0:96, 0:XT * P]
        lg = [spare1[:, p * CTB * S:(p + 1) * CTB * S].rearrange("p (k q) -> p k q", k=CTB) for p in range(2)]
        qpT = spare1[:, 2 * CTB * S:2 * CTB * S + XT * P]
        f_sg, f_t, f_hT = ([spare2[:, (2 * i + p) * 512:(2 * i + p + 1) * 512] for p in range(2)] for i in range(3))


        PS = ctx.enter_context(nc.psum_tensor("PS", [P, 8, 512], f32))

        ld_x, ld_ctx, ld_rows, ld_mask, ld_cent, ld_qkv, ld_k1, ld_bc, ld_ff0, ld_w0, ld_w1 = (
            sem("ld_" + n) for n in "x ctx rows mask cent qkv k1 bc ff0 w0 w1".split())
        rows_clear = sem("rows_clear")
        consts_ready = sem("consts_ready")
        dve_step, pool_step, act_step = sem("dve_step"), sem("pool_step"), sem("act_step")
        slots_cleared = sem("slots_cleared")
        stats0, rstd0, lat1, lat_stats, lat_rstd, norm_x, norm_ctx = (
            sem(n) for n in "stats0 rstd0 lat1 lat_stats lat_rstd norm_x norm_ctx".split())
        cent_ss, cent_rn, cent_ready = sem("cent_ss"), sem("cent_rn"), sem("cent_ready")
        mask_ready, vec_ready = sem("mask_ready"), sem("vec_ready")
        s0_filled, s0_act, s0_dve = sem("s0_filled"), sem("s0_act"), sem("s0_dve")
        xb_ready, mask_cast, kv1_filled, kv1_kept, op_filled = (
            sem(n) for n in "xb_ready mask_cast kv1_filled kv1_kept op_filled".split())
        nk_step, o2_read, logits_ready, f_gated = (sem(n) for n in "nk_step o2_read logits_ready f_gated".split())
        pool_passed, act_passed = sem("pool_passed"), sem("act_passed")
        n_row_dmas = 12
        cur_done = [sem(f"cur_done{p}") for p in range(2)]
        ss_done, kn_done, cast_done = (sem(n) for n in "ss_done kn_done cast_done".split())
        w_filled, w_act = sem("w_filled"), sem("w_act")
        m_filled, m_read = sem("m_filled"), sem("m_read")
        st_done, exp_done, pv_done, pool_added, dve_added, sum_done, o_done, rc_done = (
            sem(n) for n in "st_done exp_done pv_done pool_added dve_added sum_done o_done rc_done".split())
        ln_stats, ln_rstd, ln_norm, ln_T, ln_evac = (
            [sem(f"{n}{k}") for k in range(3)] for n in "ln_stats ln_rstd ln_norm ln_T ln_evac".split())
        hsq_done, hsq_summed, rn_done, scores_ready, top_ready, gexp_done, sel_ready, pos_ready, dest_ready = (
            sem(n) for n in
            "hsq_done hsq_summed rn_done scores_ready top_ready gexp_done sel_ready pos_ready dest_ready".split())
        sh_filled, sh_silu, sh_mul, sh_down, sh_added = (
            sem(n) for n in "sh_filled sh_silu sh_mul sh_down sh_added".split())
        scattered = sem("scattered")
        w_slot = [sem(f"w_slot{r}") for r in range(RING)]
        x_slot = [sem(f"x_slot{r}") for r in range(RING)]
        t_filled, xeT_done, gu_filled, silu_done, he_done, y_filled, y_evac = (
            sem(n) for n in
            "t_filled xeT_done gu_filled silu_done he_done y_filled y_evac".split())
        y_stored = [sem(f"y_stored{r}") for r in range(4)]
        gathered = [sem(f"gathered{t}") for t in range(XT)]
        qp_filled, qp_ready, s2_filled, s2_relu, s2_masked, o2_filled = (
            sem(n) for n in "qp_filled qp_ready s2_filled s2_relu s2_masked o2_filled".split())
        r1_filled, e1_exp, w_tok_ready, split_ready, wT_filled, wT_ready = (
            sem(n) for n in
            "r1_filled e1_exp w_tok_ready split_ready wT_filled wT_ready".split())
        f_filled, f_silu, f_h, f_acc = sem("f_filled"), sem("f_silu"), sem("f_h"), sem("f_acc")
        f_slot = [sem(f"f_slot{r}") for r in range(4)]
        out_ready, out_stored = sem("out_ready"), sem("out_stored")

        SETUP = ([("ctx_raw", "act")] * 4 + [("vec", "dve")] + [("ctx_n", "dve")] * 4 + [("lat", "dve")] * 2
                 + [("cent", "dve")] + [("ff0", "act")] * 2)

        def setup_emptied(f):
            who = SETUP[f - 8][1]
            return who, sum(1 for s in SETUP[:f - 7] if s[1] == who)

        def setup_own(kind, k):
            return [i for i, s in enumerate(SETUP) if s[0] == kind][k]

        def work_fills(s):
            if s > NP - 2:
                return []
            k = s < NP - 2
            return ["T0", "T1", "V0", "T2", "T3"] + ["K0", "K1"] * k + ["V1", "R0"]

        PRO = ["K0", "K1", "V0", "V1", "T0", "T1", "T2", "T3", "R0", "K2", "K3"]

        E_BANK, M_BANK, O_BANK = 0, 2, 7
        W_BANK = {name: 4 + k % 3 for k, name in enumerate(work_fills(1))} | {"K2": 6, "K3": 4}

        def until_left(seq, name):
            while seq and W_BANK[seq[-1]] != W_BANK[name]:
                seq = seq[:-1]
            return seq

        def work(n, s, name):
            steady, before = len(work_fills(1)), PRO if s == 0 else work_fills(s - 1)
            k = work_fills(s).index(name)
            at = until_left(before + work_fills(s)[:k], name)
            base = len(PRO) + steady * n
            return base + k + 1, W_BANK[name], base - len(before) + len(at)

        def work_pro(name):
            k = PRO.index(name)
            return k + 1, W_BANK[name], len(until_left(PRO[:k], name)) or None

        def pairs(eng, pair):
            pair(0, 0)
            pair(1, 1)
            with eng.Fori(1, NP // 2 - 1) as q:
                pair(2 * q, 2)
                pair(2 * q + 1, 3)
            pair(NP - 2, NP - 2)
            pair(NP - 1, NP - 1)

        block = ctx.enter_context(nc.Block())

        def row(eng, i, name, lo, n):
            eng.dma_start(vec_rows[i:i + 1, lo:lo + n], A[name].rearrange("(a n) -> a n", a=1)).then_inc(ld_rows, 16)

        @block.sync
        def _(sp):
            sp.dma_start(ctx_tok[:, 0:8, :], A["ctx_1024"].rearrange("b (t p) d -> p (b t) d", p=P)[:, 0:8, :]) \
                .then_inc(ld_ctx, 16)
            sp.dma_start(ctx_tok[:, 8:16, :], A["ctx_1024"].rearrange("b (t p) d -> p (b t) d", p=P)[:, 8:16, :]) \
                .then_inc(ld_ctx, 16)
            sp.wait_ge(rows_clear, 1)
            for i, name in enumerate(("L0_xattn_ln_x_g", "L0_xattn_ln_x_b", "L0_xattn_ln_l_g", "L0_xattn_ln_l_b")):
                row(sp, i, name, 0, P)
            sp.dma_start(w_qkv[:, 0:2, :], A["L0_xattn_Wkv"].rearrange("d (a n) -> d a n", a=2)) \
                .then_inc(ld_qkv, 16)
            sp.dma_start(w_qkv[:, 2, :], A["L0_xattn_Wq"]).then_inc(ld_qkv, 16)
            sp.dma_start(w_kqv1[:, 0, :], A["L1_xattn_kernel_q"][0, 0]).then_inc(ld_k1, 16)
            sp.dma_start(w_kqv1[:, 1, :], A["L1_xattn_kernel_k"][0, 0]).then_inc(ld_k1, 16)
            sp.dma_start(w_kqv1[:, 2, :], A["L1_xattn_kernel_v"][0, 0]).then_inc(ld_k1, 16)
            sp.dma_start(ff0[:, :, :], A["mask_1xSxS2_ff0"][0].rearrange("(t p) k -> p t k", p=P)) \
                .then_inc(ld_ff0, 16)
            sp.dma_start(w_out[:, :, :], A["L0_xattn_Wout"].rearrange("(c p) d -> p c d", p=P)) \
                .then_inc(ld_w0, 16)
            sp.dma_start(w_sh0[:, 0, :], A["L0_ffn_sg"]).then_inc(ld_w0, 16)
            sp.dma_start(w_sh0[:, 1, :], A["L0_ffn_su"]).then_inc(ld_w0, 16)
            sp.dma_start(w_shd0[:, :, :], A["L0_ffn_sd"].rearrange("(c p) d -> p c d", p=P)) \
                .then_inc(ld_w0, 16)
            sp.dma_start(w_r1[:, :], A["L1_ffn_Wr"]).then_inc(ld_w1, 16)
            sp.dma_start(w_sh1[:, 0, :], A["L1_ffn_Wg_s"]).then_inc(ld_w1, 16)
            sp.dma_start(w_sh1[:, 1, :], A["L1_ffn_Wu_s"]).then_inc(ld_w1, 16)
            sp.dma_start(w_shd1[:, :], A["L1_ffn_Wd_s"]).then_inc(ld_w1, 16)
            sp.dma_start(bd_rows[0:E2, :], A["L1_ffn_bd"]).then_inc(ld_w1, 16)
            sp.dma_start(bd_rows[E2:E2 + 1, :], A["L1_ffn_bd_s"].rearrange("(a d) -> a d", a=1)) \
                .then_inc(ld_w1, 16)
            sp.wait_ge(consts_ready, 9)
            sp.dma_start(slots_in.rearrange("(p a) d -> p a d", p=P),
                         zero_row[:, :].unsqueeze(1).broadcast_to([P, NE * CAP // P, D])) \
                .then_inc(slots_cleared, 16)
            def load_weights(e, r):
                sp.dma_start(w_g[r][:, :], A["L0_ffn_wg"][bass.ds(e, 1)].rearrange("a d h -> (a d) h")) \
                    .then_inc(w_slot[r], 16)
                sp.dma_start(w_u[r][:, :], A["L0_ffn_wu"][bass.ds(e, 1)].rearrange("a d h -> (a d) h")) \
                    .then_inc(w_slot[r], 16)

            def load_down(e, r):
                sp.dma_start(w_d[r][:, :, :],
                             A["L0_ffn_wd"][bass.ds(e, 1)].rearrange("a (c p) d -> p (a c) d", p=P)) \
                    .then_inc(w_slot[r], 16)

            def load_slots(e, r):
                sp.dma_start(xe[r][:, :, :],
                             slots_in[bass.ds(e * CAP, CAP), :].rearrange("(c p) d -> p c d", p=HCAP)) \
                    .then_inc(x_slot[r], 16)

            def store_y(e, k):
                sp.wait_ge(y_evac, e + 1)
                sp.dma_start(slots_out[bass.ds(e * CAP, CAP), :].rearrange("(c p) d -> p c d", p=HCAP),
                             ye[k % 4][:, :, :]).then_inc(y_stored[k % 4], 16)

            def copy_cur(m, p):
                sp.dma_start(act_cur[p][:, :], actT[:, bass.ds(m // HP, 1), :].rearrange("d a k -> d (a k)")) \
                    .then_inc(cur_done[p], 16)

            sp.wait_ge(s0_dve, sum(1 for s in SETUP if s[1] == "dve"))
            copy_cur(0, 0)
            copy_cur(1, 1)
            sp.wait_ge(w_filled, work_pro("V1")[0])
            copy_cur(2, 0)

            def copy_after(n, s):
                sp.wait_ge(w_filled, work(n, s, "V1")[0])
                copy_cur(n + 3, (s + 1) % 2)

            for r in range(RING):
                load_weights(r, r)
            copy_after(0, 0)
            copy_after(1, 1)
            with sp.Fori(1, NP // 2 - 2) as q:
                copy_after(2 * q, 2)
                copy_after(2 * q + 1, 3)
            copy_after(NP - 4, NP - 4)
            sp.wait_ge(kv1_filled, 8)
            for r in range(RING):
                load_down(r, r)
            sp.wait_ge(scattered, 16 * XT * K0)
            for r in range(RING):
                load_slots(r, r)
            with sp.Fori(0, NE // RING - 1) as q:
                e0 = RING * q
                for k in range(RING):
                    sp.wait_ge(y_filled, e0 + k + 1)
                    load_weights(e0 + RING + k, k)
                    load_down(e0 + RING + k, k)
                    load_slots(e0 + RING + k, k)
                    store_y(e0 + k, k)
            for k in range(RING):
                store_y(NE - RING + k, k)

            def load_pair(j, r):
                dst = f_w[r]
                sp.dma_start(dst[:, 0, :, :], A["L1_ffn_Wg"][bass.ds(2 * j, 2)].rearrange("e d i -> d e i")) \
                    .then_inc(f_slot[r], 16)
                sp.dma_start(dst[:, 1, :, :], A["L1_ffn_Wu"][bass.ds(2 * j, 2)].rearrange("e d i -> d e i")) \
                    .then_inc(f_slot[r], 16)
                sp.dma_start(f_wd[r], A["L1_ffn_Wd"][bass.ds(2 * j, 2)].rearrange("e i d -> (e i) d")) \
                    .then_inc(f_slot[r], 16)

            for r in range(4):
                load_pair(r, r)
            with sp.Fori(0, PR // 4 - 1) as q:
                j0 = 4 * q
                for r in range(4):
                    sp.wait_ge(f_acc, NHALF * (j0 + r + 2))
                    load_pair(j0 + 4 + r, r)
            for t in range(XT):
                sp.wait_ge(out_ready, t + 1)
                sp.dma_start(out.rearrange("b (t p) d -> p (b t) d", p=P)[:, t, :], h_tok[:, t, :]) \
                    .then_inc(out_stored, 16)
            sp.wait_ge(out_stored, 16 * XT)

        @block.gpsimd
        def _(pool):
            g = nc.gpsimd
            pool_n = [0]

            def link(ins):
                pool_n[0] += 1
                ins.then_inc(pool_step, 1)
                pool.wait_ge(pool_step, pool_n[0])

            link(g.memset(ident[:, :], 0.0))
            g.affine_select(out=ident[:, :], in_=ident[:, :], compare_op=ALU.not_equal, fill=1.0, base=0,
                            pattern=[[-1, P]], channel_multiplier=1).then_inc(consts_ready, 1)
            g.memset(neg_half[:, :], -0.5).then_inc(consts_ready, 1)
            pool.wait_ge(consts_ready, 2)
            g.tensor_copy(ident_b[:, :], ident[:, :]).then_inc(consts_ready, 1)
            g.memset(kn_aug[:, :, :, :], 0.0).then_inc(consts_ready, 1)
            link(g.memset(ones_b[:, :], 1.0))
            g.affine_select(out=earlier[:, :], in_=ones_b[:, :], compare_op=ALU.is_gt, fill=0.0, base=0,
                            pattern=[[1, P]], channel_multiplier=-1).then_inc(consts_ready, 1)
            g.iota(iota_e[:, :], pattern=[[1, NE]], base=0, channel_multiplier=0,
                   allow_small_or_imprecise_dtypes=True).then_inc(consts_ready, 1)
            link(g.memset(lower_g[:, :, :], 1.0))
            g.affine_select(out=lower_g[:, :, :], in_=lower_g[:, :, :], compare_op=ALU.is_gt, fill=0.0,
                            base=0, pattern=[[1, NG], [-1, NG]], channel_multiplier=0) \
                .then_inc(consts_ready, 1)
            g.memset(w_tok[:, :, E2:E2 + 1], 1.0).then_inc(consts_ready, 1)
            g.memset(zero_row[:, :], 0.0).then_inc(consts_ready, 1)
            pool.wait_ge(consts_ready, 9)
            g.memset(kn_aug[:, 0:KT, :, DH:DH + 1], 1.0).then_inc(consts_ready, 1)
            g.memset(kn_aug[:, KT:KT + QT, :, DH + 1:DH + 2], 1.0).then_inc(consts_ready, 1)
            g.memset(ones_f[:, :], 1.0).then_inc(consts_ready, 1)
            pool.wait_ge(stats0, XT)
            link(g.tensor_scalar(ve[:, CT:], mv[:, CT:, 1], 1e-5, None, ALU.add))
            g.tensor_tensor(rstd[:, CT:], ve[:, CT:], neg_half[:, 0:XT], ALU.pow).then_inc(rstd0, 1)
            pool.wait_ge(stats0, CT + XT)
            link(g.tensor_scalar(ve[:, 0:CT], mv[:, 0:CT, 1], 1e-5, None, ALU.add))
            g.tensor_tensor(rstd[:, 0:CT], ve[:, 0:CT], neg_half[:, 0:CT], ALU.pow).then_inc(rstd0, 1)
            pool.wait_ge(lat_stats, XT)
            link(g.tensor_scalar(ve[:, CT:], mv[:, CT:, 1], 1e-5, None, ALU.add))
            g.tensor_tensor(rstd[:, CT:], ve[:, CT:], neg_half[:, 0:XT], ALU.pow).then_inc(lat_rstd, 1)
            pool.wait_ge(ld_cent, 32)
            g.tensor_tensor(cent_sq[:, :], cent[:, :], cent[:, :], ALU.mult).then_inc(cent_ss, 1)
            pool.wait_ge(cent_ss, 2)
            link(g.tensor_scalar(cent_n[:, :], cent_n[:, :], 1e-24, None, ALU.max))
            link(g.tensor_tensor(cent_n[:, :], cent_n[:, :], neg_half[0:NG + NE, 0:1], ALU.pow))
            g.tensor_scalar(cent[:, :], cent[:, :], cent_n[:, 0:1], None, ALU.mult).then_inc(cent_ready, 1)
            def stand_alone():
                pool.sem_inc(pool_passed, 1)

            def norm_half(m, j, t3_count):
                b = m // HP
                tiles, cols = slice(4 * j, 4 * j + 4), slice(8 * j, 8 * j + 8)
                pool.wait_ge(ss_done, 2 * m + j + 1)
                stand_alone()
                g.tensor_scalar(ssm[:, cols], ss[:, cols], 1.0 / DH, 1e-16, ALU.mult, ALU.max) \
                    .then_inc(nk_step, 1)
                pool.wait_ge(nk_step, 4 * m + 2 * j + 1)
                g.tensor_tensor(rk[:, cols], ssm[:, cols], neg_half[:, 0:8], ALU.pow).then_inc(nk_step, 1)
                pool.wait_ge(nk_step, 4 * m + 2 * j + 2)
                if j == 0 and t3_count is not None:
                    pool.wait_ge(w_filled, t3_count)
                    stand_alone()
                g.tensor_tensor(
                    kn_aug[:, tiles, :, 0:DH],
                    kq_raw[:, tiles, :].rearrange("p t (h d) -> p t h d", h=2),
                    rk[:, cols].rearrange("p (t h) -> p t h", h=2).unsqueeze(3).broadcast_to([P, 4, 2, DH]),
                    ALU.mult).then_inc(kn_done, 1)
                if j == 0:
                    g.tensor_copy(
                        kn_aug[:, 0:CTB, :, DH + 1:DH + 2].rearrange("p t h a -> p t (h a)"),
                        mask_bias[:, bass.ds(b * CTB, CTB)].unsqueeze(2).broadcast_to([P, CTB, 2])) \
                        .then_inc(kn_done, 1)

            def add(n, s, c):
                pool.wait_ge(exp_done, 6 * n + c + 1)
                if c == 1:
                    if s > 1:
                        pool.wait_ge(sum_done, n - 1)
                    first = pT[0]
                else:
                    pool.wait_ge(pool_added, 2 * n + c - 1)
                    first = p_sum[s % 2]
                stand_alone()
                g.tensor_tensor(p_sum[s % 2][:, :, :], first[:, :, :], pT[c % 3][:, :, :], ALU.add) \
                    .then_inc(pool_added, 1)

            pool.wait_ge(mask_ready, 1)
            for j in range(2):
                norm_half(0, j, None)
            pool.wait_ge(ld_bc, 64)
            g.tensor_tensor(x_tok[:, :, :], x_tok[:, :, :], bout_b[:, :].unsqueeze(1).broadcast_to([P, XT, D]),
                            ALU.add).then_inc(xb_ready, 1)
            for j in range(2):
                norm_half(1, j, work_pro("T3")[0])

            def pair(n, s):
                add(n, s, 1)
                add(n, s, 2)
                if s < NP - 2:
                    norm_half(n + 2, 0, work(n, s, "T3")[0])
                if s < NP - 2:
                    norm_half(n + 2, 1, None)

            pairs(pool, pair)

            def ln_pow(k, b):
                tiles = slice(QT * b, QT * (b + 1))
                pool.wait_ge(ln_stats[k], QT * (b + 1))
                link(g.tensor_scalar(ve[:, tiles], mv[:, tiles, 1], 1e-5, None, ALU.add))
                g.tensor_tensor(rstd[:, tiles], ve[:, tiles], neg_half[:, 0:QT], ALU.pow).then_inc(ln_rstd[k], 1)

            def squares(b):
                tiles = slice(QT * b, QT * (b + 1))
                pool.wait_ge(ln_norm[0], QT * (b + 1))
                g.tensor_tensor(hsq[:, tiles, :], h_tok[:, tiles, :], h_tok[:, tiles, :], ALU.mult) \
                    .then_inc(hsq_done, 1)

            for b in range(NB):
                ln_pow(0, b)
                if b:
                    squares(b - 1)
            squares(NB - 1)
            pool.wait_ge(hsq_summed, 1)
            link(g.tensor_scalar(rn[:, :], rn[:, :], 1e-24, None, ALU.max))
            g.tensor_tensor(rn[:, :], rn[:, :], neg_half[:, 0:XT], ALU.pow).then_inc(rn_done, 1)
            link(g.memset(pair_sel[:, :, :], 0.0))
            for s in range(3):
                view = pair_sel[32 * s:32 * s + 32, :, :].rearrange("p j (c i) -> p j c i", c=2)
                g.affine_select(out=view, in_=view, compare_op=ALU.not_equal, fill=1.0, base=0,
                                pattern=[[-2, PR], [-1, 2], [0, I2]], channel_multiplier=1) \
                    .then_inc(consts_ready, 1)
            pool.wait_ge(consts_ready, 15)
            pool.wait_ge(slots_cleared, 16)
            pool.wait_ge(dest_ready, 2)
            for t in range(XT):
                for k in range(K0):
                    g.indirect_dma_start(
                        out=slots_in[:, :],
                        out_offset=bass.IndirectOffsetOnAxis(ap=dest_in[:, t, k:k + 1], axis=0),
                        in_=h_tok[:, t, :], in_offset=None,
                        bounds_check=NE * CAP - 1, oob_is_err=False).then_inc(scattered, 16)
            for r in range(4):
                pool.wait_ge(y_stored[r], 16 * NE // 4)
            def gather(t):
                for k in range(K0):
                    g.indirect_dma_start(
                        out=yg[:, t, k, :], out_offset=None, in_=slots_out[:, :],
                        in_offset=bass.IndirectOffsetOnAxis(ap=dest_out[:, t, k:k + 1], axis=0),
                        bounds_check=NE * CAP - 1, oob_is_err=False).then_inc(gathered[t], 16)

            for r in range(NB + 2):
                if r < NB:
                    gather(QT * r)
                if 0 <= r - 1 < NB:
                    ln_pow(1, r - 1)
                if r < NB:
                    gather(QT * r + 1)
                if 0 <= r - 2 < NB:
                    ln_pow(2, r - 2)

        @block.tensor
        def _(pe):
            t = nc.tensor

            def emptied(free):
                if free is not None:
                    pe.wait_ge(w_act, free)

            def setup_bank(f):
                if f >= 8:
                    who, n = setup_emptied(f)
                    pe.wait_ge(s0_act if who == "act" else s0_dve, n)
                return f % 8

            pe.wait_ge(consts_ready, 2)
            for f, (kind, _) in enumerate(SETUP):
                k = f - setup_own(kind, 0)
                bank = setup_bank(f)
                if kind == "vec":
                    pe.wait_ge(ld_rows, 16 * n_row_dmas)
                    pe.wait_ge(mask_cast, 1)
                    t.transpose(PS[:, bank, 0:48], vec_rows[:, :], ident[0:48, 0:48])
                    last = t.transpose(PS[:, bank, 64:64 + CT], mask_f[:, :], ident[0:CT, 0:CT])
                elif kind == "ctx_raw":
                    pe.wait_ge(ld_ctx, 32)
                    for i in range(4):
                        last = t.transpose(PS[:, bank, i * P:(i + 1) * P], ctx_tok[:, 4 * k + i, :], ident[:, :])
                elif kind == "cent":
                    pe.wait_ge(cent_ready, 1)
                    last = t.transpose(PS[:, bank, 0:NG + NE], cent[:, :], ident[0:NG + NE, 0:NG + NE])
                elif kind == "lat":
                    pe.wait_ge(norm_x, 4 * k + 4)
                    for i in range(4):
                        last = t.transpose(PS[:, bank, i * P:(i + 1) * P], h_tok[:, 4 * k + i, :], ident[:, :])
                elif kind == "ctx_n":
                    pe.wait_ge(norm_ctx, 4 * k + 4)
                    for i in range(4):
                        last = t.transpose(PS[:, bank, i * P:(i + 1) * P], ctx_n[:, 4 * k + i, :], ident[:, :])
                elif kind == "ff0":
                    pe.wait_ge(ld_ff0, 16)
                    for i in range(CTB):
                        last = t.transpose(PS[:, bank, i * P:(i + 1) * P], ff0[:, k, i * P:(i + 1) * P], ident[:, :])
                last.then_inc(s0_filled, 1)
            pe.wait_ge(s0_act, sum(1 for s in SETUP if s[1] == "act"))
            pe.wait_ge(s0_dve, sum(1 for s in SETUP if s[1] == "dve"))

            def project(m, s, name, info):
                _, bank, free = info
                emptied(free)
                half = int(name[1]) % 2
                if name[0] == "K" and half == 0:
                    pe.wait_ge(cur_done[s % 2], (m - s % 2) * 8 + 16)
                cols = bass.ds(m % HP * P, P)
                for i in range(2 if name == "V1" else 4):
                    tile_i = 4 * half + i
                    a = 1 if name[0] == "V" else 2 if tile_i >= KT else 0
                    if tile_i >= KT:
                        tile_i -= QT
                    last = t.matmul(PS[:, bank, i * P:(i + 1) * P], act_cur[s % 2][:, tile_i * P:(tile_i + 1) * P],
                                    w_qkv[:, a, cols], start=True, stop=True)
                last.then_inc(w_filled, 1)

            def turn(m, name, info):
                _, bank, free = info
                emptied(free)
                j = int(name[1])
                if j < 2:
                    pe.wait_ge(kn_done, 3 * m + 2 + j)
                for i in range(4):
                    last = t.transpose(PS[0:HA, bank, i * P:(i + 1) * P],
                                       kn_aug[:, 4 * (j % 2) + i, j // 2, :], ident[:, :])
                last.then_inc(w_filled, 1)

            def maxima(n, s, i):
                h, qt = i // QT, i % QT
                pe.wait_ge(cast_done, 4 * n + 2 * h + 2)
                if not (s == 0 and i == 0):
                    pe.wait_ge(m_read, 4 * n + i)
                for c in range(2):
                    last = t.matmul(PS[:, M_BANK + c, 0:NKEY // 2], qTb[:, h, qt * P:(qt + 1) * P],
                                    kTb[:, h, c * (NKEY // 2):(c + 1) * (NKEY // 2)], start=True, stop=True)
                last.then_inc(m_filled, 1)

            def shift_rows(n, info):
                _, bank, free = info
                emptied(free)
                pe.wait_ge(m_read, 4 * n + 4)
                for i in range(2 * QT):
                    last = t.matmul(PS[DH:DH + 1, bank, i * P:(i + 1) * P], negm[:, i:i + 1], ident_b[:, :],
                                    start=True, stop=True)
                last.then_inc(w_filled, 1)

            def scores(n, s, c):
                if c == 0:
                    pe.wait_ge(w_act, work_pro("R0")[0] if s == 0 else work(n - 1, s - 1, "R0")[0])
                if not (s == 0 and c < 2):
                    pe.wait_ge(exp_done, 6 * n + c - 1)
                for h in range(2):
                    last = t.matmul(PS[:, E_BANK + c % 2, h * S:(h + 1) * S], kT[s % 2][:, h, c * P:(c + 1) * P],
                                    qT[s % 2][:, h, :], start=True, stop=True)
                last.then_inc(st_done, 1)

            def weigh(n, s, c):
                pe.wait_ge(exp_done, 6 * n + c + 1)
                if c == 0 and s > 0:
                    pe.wait_ge(o_done, n)
                for h in range(2):
                    last = t.matmul(PS[h * DH:(h + 1) * DH, O_BANK, 0:S], v_cur[s % 2][:, c, h, :],
                                    pT[c % 3][:, h, :], start=(c == 0), stop=(c == KT - 1),
                                    skip_group_check=True)
                last.then_inc(pv_done, 1)

            def sums(n, s):
                pe.wait_ge(dve_added, 3 * n + 3)
                for h in range(2):
                    last = t.matmul(PS[h * DH:(h + 1) * DH, O_BANK, S:2 * S], ones_f[:, 0:DH],
                                    p_sum[s % 2][:, h, :], start=True, stop=True, skip_group_check=True)
                last.then_inc(sum_done, 1)

            pe.wait_ge(ld_qkv, 32)
            pe.wait_ge(consts_ready, 12)
            for name in ("K0", "K1", "V0", "V1"):
                project(0, 0, name, work_pro(name))
            for name in ("T0", "T1", "T2", "T3"):
                turn(0, name, work_pro(name))
            for i in range(4):
                maxima(0, 0, i)
            shift_rows(0, work_pro("R0"))
            for name in ("K2", "K3"):
                project(1, 1, name, work_pro(name))

            def pair(n, s):
                def w(name):
                    return work(n, s, name)

                last, kq = s > NP - 2, s < NP - 2

                def turns(*names):
                    if not last:
                        for name in names:
                            turn(n + 1, name, w(name))

                def step(name):
                    if name[0] == "V" and not last:
                        project(n + 1, s + 1, name, w(name))
                    if name[0] == "K" and kq:
                        project(n + 2, s + 2, name, w(name))

                def maxima_next(i):
                    if not last:
                        maxima(n + 1, s + 1, i)

                if s > 0:
                    weigh(n - 1, s - 1, 5)
                scores(n, s, 0)
                if s > 0:
                    sums(n - 1, s - 1)
                turns("T0", "T1")
                step("V0")
                scores(n, s, 1)
                turns("T2", "T3")
                scores(n, s, 2)
                weigh(n, s, 0)
                maxima_next(0)
                step("K0")
                step("K1")
                maxima_next(1)
                step("V1")
                weigh(n, s, 1)
                scores(n, s, 3)
                weigh(n, s, 2)
                maxima_next(2)
                scores(n, s, 4)
                weigh(n, s, 3)
                maxima_next(3)
                scores(n, s, 5)
                weigh(n, s, 4)
                if not last:
                    shift_rows(n + 1, w("R0"))

            pairs(pe, pair)
            weigh(NP - 1, NP - 1, 5)
            sums(NP - 1, NP - 1)

            pe.wait_ge(ld_w0, 64)
            pe.wait_ge(o_done, NP)
            def turn_h(k, b, bank, bank_left):
                pe.wait_ge(ln_norm[k], QT * (b + 1))
                if bank_left > 0:
                    pe.wait_ge(ln_evac[k], bank_left)
                for i in range(QT):
                    last = t.transpose(PS[:, bank, i * P:(i + 1) * P], h_tok[:, QT * b + i, :], ident[:, :])
                last.then_inc(ln_T[k], 1)

            for i in range(XT):
                b, qt = i // QT, i % QT
                for c in range(HP):
                    last = t.matmul(PS[:, i, 0:D], oT[:, b * HP + c, qt * P:(qt + 1) * P], w_out[:, c, :],
                                    start=(c == 0), stop=(c == HP - 1))
                last.then_inc(op_filled, 1)
                if qt == 1 and b:
                    turn_h(0, b - 1, (b - 1) % 2, b - 2)
            turn_h(0, NB - 1, (NB - 1) % 2, NB - 2)

            pe.wait_ge(ln_evac[0], NB)
            for i in range(XT):
                last = t.matmul(PS[:, 6, i * (NG + NE):(i + 1) * (NG + NE)], hT[:, i * P:(i + 1) * P], centT[:, :],
                                start=True, stop=True)
            last.then_inc(scores_ready, 1)

            def shared_up(v):
                j, half = v // 2, v % 2
                if v >= 2:
                    pe.wait_ge(sh_mul, v - 1)
                for a in range(2):
                    last = t.matmul(PS[:, 2 + 2 * a + v % 2, :], w_sh0[:, a, j * P:(j + 1) * P],
                                    hT[:, half * 512:(half + 1) * 512], start=True, stop=True)
                last.then_inc(sh_filled, 1)

            shared_up(0)
            shared_up(1)
            pe.wait_ge(sel_ready, 1)
            for i in range(XT):
                for j in range(i + 1):
                    last = t.matmul(PS[:, 7, i * NE:(i + 1) * NE], earlier[:, :] if j == i else ones_b[:, :],
                                    sel_b[:, j, :], start=(j == 0), stop=(j == i))
            last.then_inc(pos_ready, 1)
            shared_up(2)
            shared_up(3)
            pe.wait_ge(ld_k1, 48)
            pe.wait_ge(ld_bc, 64)
            for f in range(8):
                k, bank = f % 4, f % 2
                if f >= 2:
                    pe.wait_ge(kv1_kept, f - 1)
                if f < 4:
                    last = t.matmul(PS[:, bank, :], w_kqv1[:, 1, :], ctxT[:, 512 * k:512 * (k + 1)],
                                    start=True, stop=True)
                else:
                    for i in range(4):
                        cols = slice(i * P, (i + 1) * P)
                        t.matmul(PS[:, bank, cols], ctxT[:, (4 * k + i) * P:(4 * k + i + 1) * P], w_kqv1[:, 2, :],
                                 start=(i == 0), stop=False, skip_group_check=True)
                        last = t.matmul(PS[:, bank, cols], ones_f[0:1, :], bv_b[0:1, :],
                                        start=False, stop=True, skip_group_check=True)
                last.then_inc(kv1_filled, 1)
            pe.wait_ge(sh_mul, 4)
            pe.wait_ge(kv1_kept, 8)
            for i in range(XT):
                for j in range(HT):
                    last = t.matmul(PS[:, i // 4, (i % 4) * P:(i % 4 + 1) * P], hsT[:, j, i * P:(i + 1) * P],
                                    w_shd0[:, j, :], start=(j == 0), stop=(j == HT - 1))
                if i % 4 == 3:
                    last.then_inc(sh_down, 1)

            pe.wait_ge(sh_added, 2)

            def expert(e, k, up, down, turn_in=True):
                if turn_in:
                    pe.wait_ge(x_slot[k], (e - k) * 2 + 16)
                    if up:
                        if not (isinstance(e, int) and e < 2):
                            pe.wait_ge(xeT_done, e - 1)
                    for c in range(2):
                        last = t.transpose(PS[:, k % 2, c * HCAP:(c + 1) * HCAP], xe[k][:, c, :],
                                           ident[0:HCAP, 0:HCAP])
                    last.then_inc(t_filled, 1)
                if up:
                    r = (k - 1) % RING
                    pe.wait_ge(xeT_done, e)
                    pe.wait_ge(w_slot[r], (e - 1 - r) * 6 + 48)
                    if not (isinstance(e, int) and e < 3):
                        pe.wait_ge(he_done, e - 2)
                    for a, w in enumerate((w_g[r], w_u[r])):
                        for j in range(HT):
                            last = t.matmul(PS[:, 2 + 2 * a + r % 2, j * CAP:(j + 1) * CAP],
                                            w[:, j * P:(j + 1) * P], xeT[r % 2][:, :], start=True, stop=True)
                    last.then_inc(gu_filled, 1)
                if down:
                    r = (k - 2) % RING
                    pe.wait_ge(he_done, e - 1)
                    if not (isinstance(e, int) and e < 4):
                        pe.wait_ge(y_evac, e - 3)
                    for c in range(2):
                        for j in range(HT):
                            last = t.matmul(PS[0:HCAP, 6 + r % 2, c * D:(c + 1) * D],
                                            heT[r % 2][:, j, c * HCAP:(c + 1) * HCAP], w_d[r][:, j, :],
                                            start=(j == 0), stop=(j == HT - 1))
                    last.then_inc(y_filled, 1)

            for e in range(RING):
                expert(e, e, e >= 1, e >= 2)
            with pe.Fori(1, NE // RING) as q:
                e0 = RING * q
                for k in range(RING):
                    expert(e0 + k, k, True, True)
            expert(NE, 0, True, True, turn_in=False)
            expert(NE + 1, 1, False, True, turn_in=False)

            pe.wait_ge(he_done, NE)
            pe.wait_ge(y_evac, NE)

            def queries1(b):
                pe.wait_ge(ln_evac[1], b + 1)
                if b:
                    pe.wait_ge(qp_ready, b)
                t.matmul(PS[:, 2, 0:S], w_kqv1[:, 0, :], hT[:, b * S:(b + 1) * S], start=True, stop=True) \
                    .then_inc(qp_filled, 1)

            def scores1(i):
                b, c = i // 2, i % 2
                pe.wait_ge(qp_ready, b + 1)
                if i >= 2:
                    pe.wait_ge(s2_relu, i - 1)
                for kt in range(2):
                    col = b * SC + (2 * c + kt) * P
                    last = t.matmul(PS[:, 4 + i % 2, kt * S:(kt + 1) * S], kpT[:, col:col + P],
                                    qpT[:, b * S:(b + 1) * S], start=True, stop=True)
                last.then_inc(s2_filled, 1)

            def weigh1(b):
                pe.wait_ge(s2_masked, 2 * b + 2)
                if b >= 2:
                    pe.wait_ge(o2_read, b - 1)
                for qt in range(QT):
                    for kt in range(CTB):
                        last = t.matmul(PS[:, 6 + b % 2, qt * D:(qt + 1) * D], lg[b % 2][:, kt, qt * P:(qt + 1) * P],
                                        vp[:, b * CTB + kt, :], start=(kt == 0), stop=(kt == CTB - 1))
                last.then_inc(o2_filled, 1)

            for r in range(1, NB + 2):
                if r - 1 < NB:
                    turn_h(1, r - 1, 0, r - 1)
                    queries1(r - 1)
                    scores1(2 * (r - 1))
                    scores1(2 * (r - 1) + 1)
                if 0 <= r - 2 < NB:
                    turn_h(2, r - 2, 1, r - 2)
                if r - 1 < NB:
                    weigh1(r - 1)

            pe.wait_ge(ln_evac[2], NB)
            pe.wait_ge(ld_w1, 96)
            for i in range(XT):
                last = t.matmul(PS[:, 6, i * E2:(i + 1) * E2], hT[:, i * P:(i + 1) * P], w_r1[:, :],
                                start=True, stop=True)
            last.then_inc(r1_filled, 1)

            def up1(v, v0, w_gate, w_up, rows, spread=None):
                half = v0 % 2
                if not (isinstance(v, int) and v < 2):
                    pe.wait_ge(f_h, v - 1)
                cols = hT[:, half * 512:(half + 1) * 512]
                t.matmul(PS[0:rows, 0 + half, :], w_gate, cols, start=True, stop=True)
                last = t.matmul(PS[0:rows, 2 + half, :], w_up, cols, start=True, stop=True)
                if spread is not None:
                    last = t.matmul(PS[:, 4 + half, :], spread, splitT[:, half * 512:(half + 1) * 512],
                                    start=True, stop=True)
                last.then_inc(f_filled, 1)

            def down1(v, half, w, rows, first=False):
                pe.wait_ge(f_h, v + 1)
                for q in range(4):
                    last = t.matmul(PS[:, 6 + half, q * D:(q + 1) * D], f_hT[half][0:rows, q * P:(q + 1) * P], w,
                                    start=(first and q == 0), stop=True, skip_group_check=True)
                last.then_inc(f_acc, 1)

            for half in range(2):
                up1(half, half, w_sh1[:, 0, :], w_sh1[:, 1, :], I2)
            pe.wait_ge(w_tok_ready, 1)
            for i in range(XT):
                last = t.transpose(PS[0:E2 + 1, 4 + i // 4, (i % 4) * P:(i % 4 + 1) * P], w_tok[:, i, :], ident[:, :])
                if i % 4 == 3:
                    last.then_inc(wT_filled, 1)
            pe.wait_ge(split_ready, 1)
            split_ps = PS[:, 7, :].bitcast(bf16)
            for i in range(XT):
                last = t.transpose(split_ps[0:96, i * P:(i + 1) * P], split[:, i, :, :].rearrange("p s e -> p (s e)"),
                                   ident_b[:, :])
            last.then_inc(wT_filled, 1)
            pe.wait_ge(wT_ready, 3)
            for half in range(2):
                down1(half, half, w_shd1[:, :], I2, first=True)
            for half in range(2):
                for q in range(4):
                    t.matmul(PS[:, 6 + half, q * D:(q + 1) * D], wT[:, (4 * half + q) * P:(4 * half + q + 1) * P],
                             bd_rows[:, :], start=False, stop=True, skip_group_check=True)

            def unit(j, r, half, down):
                v = 2 * j + 2 + half
                if half == 0:
                    pe.wait_ge(f_slot[r], (j - r) * 12 + 48)
                up1(v, half, f_w[r][:, 0, :, :].rearrange("d e i -> d (e i)"),
                    f_w[r][:, 1, :, :].rearrange("d e i -> d (e i)"), P,
                    spread=pair_sel[:, bass.ds(j, 1), :].rearrange("p a c -> p (a c)"))
                if down:
                    rd = r if half else (r - 1) % 4
                    down1(v - 1, 1 - half, f_wd[rd], P)

            unit(0, 0, 0, False)
            unit(0, 0, 1, True)
            for r in range(1, 4):
                unit(r, r, 0, True)
                unit(r, r, 1, True)
            with pe.Fori(1, PR // 4) as q:
                j0 = 4 * q
                for r in range(4):
                    unit(j0 + r, r, 0, True)
                    unit(j0 + r, r, 1, True)
            down1(2 * PR + 1, 1, f_wd[3], P)

        @block.scalar
        def _(act):
            s_ = nc.scalar
            act.dma_start(x_tok[:, :, :], A["x"].rearrange("b (t p) d -> p (b t) d", p=P)).then_inc(ld_x, 16)
            act.dma_start(mask_u8[:, :], A["mask_BxS2_bf1"].rearrange("b (t p) -> (b t) p", p=P)) \
                .then_inc(ld_mask, 16)
            act.dma_start(cent[0:NG, :], A["L0_ffn_group_centroids"]).then_inc(ld_cent, 16)
            act.dma_start(cent[NG:, :], A["L0_ffn_expert_centroids"]).then_inc(ld_cent, 16)
            act.wait_ge(rows_clear, 1)

            for i, name in enumerate(("L1_xattn_bias_q", "L1_xattn_bias_k")):
                row(act, 4 + i, name, 0, P)
            for i, name in enumerate(("L0_xattn_qn_g", "L0_xattn_kn_g", "L1_ffn_bg_s", "L1_ffn_bu_s")):
                row(act, 6 + i, name, 0, DH)
            act.dma_start(vec_rows[10:10 + PR, :], A["L1_ffn_bg"].rearrange("(j e) i -> j (e i)", e=2)) \
                .then_inc(ld_rows, 16)
            act.dma_start(vec_rows[10 + PR:10 + 2 * PR, :], A["L1_ffn_bu"].rearrange("(j e) i -> j (e i)", e=2)) \
                .then_inc(ld_rows, 16)
            for dst, name, n in ((bias0_b, "L0_ffn_bias", NE), (bv_b, "L1_xattn_bias_v", D),
                                 (bout_b, "L0_xattn_bout", D), (br_b, "L1_ffn_br", E2)):
                act.dma_start(dst[:, :], A[name].partition_broadcast(P)).then_inc(ld_bc, 16)

            for f, (kind, who) in enumerate(SETUP):
                if who != "act":
                    continue
                k = f - setup_own(kind, 0)
                src = PS[:, f % 8, :]
                act.wait_ge(s0_filled, f + 1)
                if kind == "ctx_raw":
                    s_.activation(ctxT[:, 512 * k:512 * (k + 1)], src, ACT.Copy).then_inc(s0_act, 1)
                elif kind == "ff0":
                    s_.activation(ff0T[:, :, k * P:(k + 1) * P], src.rearrange("p (c q) -> p c q", c=CTB), ACT.Copy) \
                        .then_inc(s0_act, 1)

            def keep_v(s, name, info):
                count, bank, _ = info
                act.wait_ge(w_filled, count)
                lo, hi = (0, 4) if name == "V0" else (4, KT)
                s_.activation(v_cur[s % 2][:, lo:hi, :, :],
                              PS[:, bank, 0:(hi - lo) * P].rearrange("p (t h d) -> p t h d", t=hi - lo, h=2),
                              ACT.Copy).then_inc(w_act, 1)

            def keep_kq(m, s, j, info):
                count, bank, _ = info
                act.wait_ge(w_filled, count)
                if j == 0 and s > 0:
                    act.wait_ge(kn_done, 3 * m)
                src = PS[:, bank, :].rearrange("p (t n) -> p t n", t=4)
                s_.activation(kq_sq[:, 4 * j:4 * j + 4, :], src, ACT.Square)
                s_.activation(kq_raw[:, 4 * j:4 * j + 4, :], src, ACT.Copy).then_inc(w_act, 1)

            def keep_turned(s, name, info):
                count, bank, _ = info
                act.wait_ge(w_filled, count)
                h = int(name[1]) // 2
                if int(name[1]) % 2 == 0:
                    s_.activation(kTb[:, h, 0:4 * P], PS[0:HA, bank, :], ACT.Copy).then_inc(cast_done, 1)
                    s_.activation(kT[s % 2][:, h, 0:4 * P], PS[0:HA, bank, :], ACT.Copy).then_inc(w_act, 1)
                else:
                    src_k, src_q = PS[0:HA, bank, 0:2 * P], PS[0:HA, bank, 2 * P:4 * P]
                    s_.activation(kTb[:, h, 4 * P:6 * P], src_k, ACT.Copy)
                    s_.activation(qTb[:, h, :], src_q, ACT.Copy, scale=q_scale[:, 0:1]).then_inc(cast_done, 1)
                    s_.activation(kT[s % 2][:, h, 4 * P:6 * P], src_k, ACT.Copy)
                    s_.activation(qT[s % 2][:, h, :], src_q, ACT.Copy, scale=q_scale[:, 0:1]).then_inc(w_act, 1)

            def keep_rows(s, info):
                count, bank, _ = info
                act.wait_ge(w_filled, count)
                act.wait_ge(w_act, count - 1)
                s_.activation(qT[s % 2][DH:DH + 1, :, :], PS[DH:DH + 1, bank, :].rearrange("p (h q) -> p h q", h=2),
                              ACT.Copy).then_inc(w_act, 1)

            def exps(n, s, c):
                act.wait_ge(st_done, 6 * n + c + 1)
                if not (s == 0 and c < 3):
                    act.wait_ge(pv_done, 6 * n + c - 2)
                    if c < 3:
                        act.wait_ge(dve_added, 3 * n + c - 2)
                    else:
                        act.wait_ge(pool_added, 2 * n + (1, 1, 2)[c - 3])
                s_.activation(pT[c % 3][:, :, :], PS[:, E_BANK + c % 2, :].rearrange("p (h q) -> p h q", h=2),
                              ACT.Exp).then_inc(exp_done, 1)

            for j in range(2):
                keep_kq(0, 0, j, work_pro(f"K{j}"))
            for name in ("V0", "V1"):
                keep_v(0, name, work_pro(name))
            for name in ("T0", "T1", "T2", "T3"):
                keep_turned(0, name, work_pro(name))
            keep_rows(0, work_pro("R0"))
            for j in range(2):
                keep_kq(1, 1, j, work_pro(f"K{2 + j}"))

            def pair(n, s):
                def w(name):
                    return work(n, s, name)

                v, k = s < NP - 1, s < NP - 2
                exps(n, s, 0)
                if v:
                    keep_turned(s + 1, "T0", w("T0"))
                    keep_turned(s + 1, "T1", w("T1"))
                exps(n, s, 1)
                if v:
                    keep_v(s + 1, "V0", w("V0"))
                    keep_turned(s + 1, "T2", w("T2"))
                    keep_turned(s + 1, "T3", w("T3"))
                exps(n, s, 2)
                if k:
                    keep_kq(n + 2, s + 2, 0, w("K0"))
                    keep_kq(n + 2, s + 2, 1, w("K1"))
                if v:
                    keep_v(s + 1, "V1", w("V1"))
                exps(n, s, 3)
                exps(n, s, 4)
                exps(n, s, 5)
                if v:
                    keep_rows(s + 1, w("R0"))

            pairs(act, pair)

            def keep_hT(k, b, bank):
                act.wait_ge(ln_T[k], b + 1)
                s_.activation(hT[:, S * b:S * (b + 1)], PS[:, bank, 0:S], ACT.Copy).then_inc(ln_evac[k], 1)

            for b in range(NB):
                keep_hT(0, b, b % 2)

            def shared_silu(v):
                act.wait_ge(sh_filled, v + 1)
                if v >= 2:
                    act.wait_ge(sh_mul, v - 1)
                s_.activation(sg_t[v % 2][:, :], PS[:, 2 + v % 2, :], ACT.Silu).then_inc(sh_silu, 1)

            shared_silu(0)
            shared_silu(1)
            act.wait_ge(top_ready, 1)
            s_.activation(gate[:, :, :], gate[:, :, :], ACT.Exp).then_inc(gexp_done, 1)
            shared_silu(2)
            shared_silu(3)
            for f in range(8):
                act.wait_ge(kv1_filled, f + 1)
                src = PS[:, f % 2, :]
                if f < 4:
                    s_.activation(kpT[:, 512 * f:512 * (f + 1)], src, ACT.Relu, bias=vec[:, 5:6]).then_inc(kv1_kept, 1)
                else:
                    s_.activation(vp[:, 4 * (f - 4):4 * (f - 3), :], src.rearrange("p (t d) -> p t d", t=4), ACT.Relu) \
                        .then_inc(kv1_kept, 1)

            def expert(e, k, up, turn_in=True):
                if turn_in:
                    act.wait_ge(t_filled, e + 1)
                    if not (isinstance(e, int) and e < 2):
                        act.wait_ge(gu_filled, e - 1)
                    s_.activation(xeT[k % 2][:, :], PS[:, k % 2, 0:CAP], ACT.Copy).then_inc(xeT_done, 1)
                if up:
                    r = (k - 1) % RING
                    act.wait_ge(gu_filled, e)
                    if not (isinstance(e, int) and e < 3):
                        act.wait_ge(he_done, e - 2)
                    s_.activation(sge[r % 2][:, :, :], PS[:, 2 + r % 2, 0:HT * CAP].rearrange("p (j c) -> p j c", j=HT),
                                  ACT.Silu).then_inc(silu_done, 1)

            for e in range(RING):
                expert(e, e, e >= 1)
            with act.Fori(1, NE // RING) as q:
                e0 = RING * q
                for k in range(RING):
                    expert(e0 + k, k, True)
            expert(NE, 0, True, turn_in=False)

            for r in range(1, NB + 2):
                b = r - 1
                if b < NB:
                    keep_hT(1, b, 0)
                    act.wait_ge(qp_filled, b + 1)
                    s_.activation(qpT[:, b * S:(b + 1) * S], PS[:, 2, 0:S], ACT.Relu, bias=vec[:, 4:5]) \
                        .then_inc(qp_ready, 1)
                    for c in range(2):
                        act.wait_ge(s2_filled, 2 * b + c + 1)
                        if b >= 2:
                            act.wait_ge(o2_filled, b - 1)
                        s_.activation(lg[b % 2][:, 2 * c:2 * c + 2, :],
                                      PS[:, 4 + c, :].rearrange("p (k q) -> p k q", k=2),
                                      ACT.Relu, scale=float(D) ** -0.5).then_inc(s2_relu, 1)
                if 0 <= r - 2:
                    keep_hT(2, r - 2, 1)

            act.wait_ge(logits_ready, 1)
            s_.activation(aff2[:, :, :], aff[:, :, :], ACT.Exp, scale=-1.0).then_inc(e1_exp, 1)

            def silu1(v, half, rows, bias):
                act.wait_ge(f_filled, v + 1)
                if not (isinstance(v, int) and v < 2):
                    act.wait_ge(f_h, v - 1)
                act.sem_inc(act_passed, 1)
                s_.activation(f_sg[half][0:rows, :], PS[0:rows, half, :], ACT.Silu, bias=bias).then_inc(f_silu, 1)

            for half in range(2):
                silu1(half, half, I2, vec[0:I2, 8:9])
            for i in range(2):
                act.wait_ge(wT_filled, i + 1)
                s_.activation(wT[:, 512 * i:512 * (i + 1)], PS[0:E2 + 1, 4 + i, :], ACT.Copy).then_inc(wT_ready, 1)
            act.wait_ge(wT_filled, 3)
            s_.activation(splitT[:, :], PS[:, 7, :].bitcast(bf16)[0:96, 0:XT * P], ACT.Copy).then_inc(wT_ready, 1)
            with act.Fori(0, PR) as j:
                for half in range(2):
                    silu1(2 * j + 2 + half, half, P, vec[:, bass.ds(10 + j, 1)])

        @block.vector
        def _(dve):
            v_ = nc.vector
            dve_n = [0]

            def link(ins):
                dve_n[0] += 1
                ins.then_inc(dve_step, 1)
                dve.wait_ge(dve_step, dve_n[0])

            def normalize(dst, src, t):
                return v_.tensor_scalar(dst, src, mv[:, t, 0:1], rstd[:, t:t + 1], ALU.subtract, ALU.mult)

            v_.memset(vec_rows[:, :], 0.0).then_inc(rows_clear, 1)
            link(v_.memset(q_scale[:, :], 1.0))
            dve.wait_ge(ld_x, 16)
            for i in range(XT):
                last = v_.bn_stats(st[:, CT + i, :], x_tok[:, i, :])
            link(last)
            for i in range(XT):
                v_.bn_aggr(mv[:, CT + i, :], st[:, CT + i, :]).then_inc(stats0, 1)
            dve.wait_ge(ld_mask, 16)
            v_.tensor_copy(mask_f[:, :], mask_u8[:, :]).then_inc(mask_cast, 1)
            dve.wait_ge(ld_ctx, 32)
            for i in range(CT):
                last = v_.bn_stats(st[:, i, :], ctx_tok[:, i, :])
            link(last)
            for i in range(CT):
                v_.bn_aggr(mv[:, i, :], st[:, i, :]).then_inc(stats0, 1)
            dve.wait_ge(rstd0, 1)
            for i in range(XT):
                last = normalize(h_tok[:, i, :], x_tok[:, i, :], CT + i)
            link(last)
            for i in range(XT):
                last = v_.bn_stats(st[:, CT + i, :], h_tok[:, i, :])
            link(last)
            for i in range(XT):
                v_.bn_aggr(mv[:, CT + i, :], st[:, CT + i, :]).then_inc(lat_stats, 1)
            dve.wait_ge(rstd0, 2)
            for i in range(CT):
                normalize(ctx_n[:, i, :], ctx_tok[:, i, :], i).then_inc(norm_ctx, 1)
            dve.wait_ge(lat_rstd, 1)
            for i in range(XT):
                normalize(h_tok[:, i, :], h_tok[:, i, :], CT + i).then_inc(norm_x, 1)
            dve.wait_ge(cent_ss, 1)
            v_.tensor_reduce(cent_n[:, :], cent_sq[:, :], AX.X, ALU.add).then_inc(cent_ss, 1)
            for f, (kind, who) in enumerate(SETUP):
                if who != "dve":
                    continue
                k = f - setup_own(kind, 0)
                src = PS[:, f % 8, :]
                dve.wait_ge(s0_filled, f + 1)
                if kind == "vec":
                    v_.tensor_copy(vec[:, :], src[:, 0:48]).then_inc(vec_ready, 1)
                    v_.tensor_scalar(mask_bias[:, :], src[:, 64:64 + CT], -BIG_NEG, BIG_NEG, ALU.mult, ALU.add) \
                        .then_inc(mask_ready, 1)
                    dve.wait_ge(mask_ready, 1)
                    v_.scalar_tensor_tensor(q_scale[0:DH, :], vec[0:DH, 6:7], float(DH) ** -0.5, vec[0:DH, 7:8],
                                            ALU.mult, ALU.mult).then_inc(s0_dve, 1)
                elif kind == "cent":
                    v_.tensor_copy(centT[:, :], src[:, 0:NG + NE]).then_inc(s0_dve, 1)
                elif kind == "lat":
                    v_.tensor_scalar(actT[:, 2 * k:2 * k + 2, SC:NKEY], src.rearrange("p (b s) -> p b s", b=2),
                                     vec[:, 2:3], vec[:, 3:4], ALU.mult, ALU.add).then_inc(s0_dve, 1)
                elif kind == "ctx_n":
                    v_.tensor_scalar(actT[:, k, 0:SC], src, vec[:, 0:1], vec[:, 1:2], ALU.mult, ALU.add) \
                        .then_inc(s0_dve, 1)
            def sum_squares(j, w_act_count):
                dve.wait_ge(w_act, w_act_count)
                v_.tensor_reduce(ss[:, 8 * j:8 * j + 8],
                                 kq_sq[:, 4 * j:4 * j + 4, :].rearrange("p t (h d) -> p (t h) d", h=2), AX.X, ALU.add) \
                    .then_inc(ss_done, 1)

            def row_maxima(n, i):
                dve.wait_ge(m_filled, 4 * n + i + 1)
                v_.tensor_reduce(negm[:, i:i + 1], PS[:, M_BANK:M_BANK + 2, 0:NKEY // 2], AX.XY, ALU.max,
                                 negate=True).then_inc(m_read, 1)

            def divide(n):
                dve.wait_ge(sum_done, n + 1)
                v_.reciprocal(rcT[:, :], PS[:, O_BANK, S:2 * S]).then_inc(rc_done, 1)
                dve.wait_ge(rc_done, n + 1)
                v_.tensor_tensor(oT[:, bass.ds(n, 1), :].rearrange("p a s -> p (a s)"), PS[:, O_BANK, 0:S],
                                 rcT[:, :], ALU.mult).then_inc(o_done, 1)

            def add(n, s, c):
                dve.wait_ge(exp_done, 6 * n + c + 1)
                if c == 3:
                    dve.wait_ge(pool_added, 2 * n + 2)
                else:
                    dve.wait_ge(dve_added, 3 * n + c - 3)
                v_.tensor_tensor(p_sum[s % 2][:, :, :], p_sum[s % 2][:, :, :], pT[c % 3][:, :, :], ALU.add) \
                    .then_inc(dve_added, 1)

            for j in range(2):
                sum_squares(j, work_pro(f"K{j}")[0])
            for i in range(4):
                row_maxima(0, i)
            for j in range(2):
                sum_squares(j, work_pro(f"K{2 + j}")[0])

            def pair(n, s):
                v, k = s < NP - 1, s < NP - 2
                if s > 0:
                    add(n - 1, s - 1, 5)
                    divide(n - 1)
                if v:
                    row_maxima(n + 1, 0)
                    row_maxima(n + 1, 1)
                if k:
                    sum_squares(0, work(n, s, "K0")[0])
                    sum_squares(1, work(n, s, "K1")[0])
                add(n, s, 3)
                if v:
                    row_maxima(n + 1, 2)
                    row_maxima(n + 1, 3)
                add(n, s, 4)

            pairs(dve, pair)
            add(NP - 1, NP - 1, 5)
            divide(NP - 1)

            dve.wait_ge(xb_ready, 1)
            def stats(k, b):
                tiles = range(QT * b, QT * (b + 1))
                for i in tiles:
                    last = v_.bn_stats(st[:, i, :], x_tok[:, i, :])
                link(last)
                for i in tiles:
                    v_.bn_aggr(mv[:, i, :], st[:, i, :]).then_inc(ln_stats[k], 1)

            def layernorm(k, b):
                dve.wait_ge(ln_rstd[k], b + 1)
                for i in range(QT * b, QT * (b + 1)):
                    normalize(h_tok[:, i, :], x_tok[:, i, :], i).then_inc(ln_norm[k], 1)

            for b in range(NB):
                for i in range(QT * b, QT * (b + 1)):
                    dve.wait_ge(op_filled, i + 1)
                    last = v_.tensor_tensor(x_tok[:, i, :], x_tok[:, i, :], PS[:, i, 0:D], ALU.add)
                link(last)
                stats(0, b)
                if b:
                    layernorm(0, b - 1)
            layernorm(0, NB - 1)
            dve.wait_ge(hsq_done, NB)
            v_.tensor_reduce(rn[:, :], hsq[:, :, :], AX.X, ALU.add).then_inc(hsq_summed, 1)
            dve.wait_ge(rn_done, 1)
            dve.wait_ge(scores_ready, 1)
            link(v_.tensor_tensor(score[:, :, :],
                                  PS[:, 6, 0:XT * (NG + NE)].rearrange("p (t g) -> p t g", t=XT),
                                  rn[:, :].unsqueeze(2).broadcast_to([P, XT, NG + NE]), ALU.mult))
            gs = score[:, :, 0:NG]
            other = gs.unsqueeze(2).broadcast_to([P, XT, NG, NG])
            own = gs.unsqueeze(3).broadcast_to([P, XT, NG, NG])
            v_.tensor_tensor(cmp1[:, :, :, :], other, own, ALU.is_gt)
            link(v_.tensor_tensor(cmp2[:, :, :, :], other, own, ALU.is_equal))
            link(v_.tensor_tensor(cmp2[:, :, :, :], cmp2[:, :, :, :],
                                  lower_g[:, :, :].unsqueeze(1).broadcast_to([P, XT, NG, NG]), ALU.mult))
            link(v_.tensor_tensor(cmp1[:, :, :, :], cmp1[:, :, :, :], cmp2[:, :, :, :], ALU.add))
            link(v_.tensor_reduce(gmask[:, :, :], cmp1[:, :, :, :], AX.X, ALU.add))
            link(v_.tensor_scalar(gmask[:, :, :], gmask[:, :, :], float(NG // 2), None, ALU.is_lt))
            v_.tensor_scalar(gneg[:, :, :], gmask[:, :, :], 1e9, -1e9, ALU.mult, ALU.add)
            link(v_.tensor_tensor(masked[:, :, :], score[:, :, NG:], bias0_b[:, :].unsqueeze(1)
                                  .broadcast_to([P, XT, NE]), ALU.add))
            by_group = masked[:, :, :].rearrange("p t (g e) -> p t g e", g=NG)
            link(v_.tensor_tensor(by_group, by_group, gmask[:, :, :].unsqueeze(3)
                                  .broadcast_to([P, XT, NG, EG]), ALU.mult))
            link(v_.tensor_tensor(by_group, by_group, gneg[:, :, :].unsqueeze(3)
                                  .broadcast_to([P, XT, NG, EG]), ALU.add))
            for i in range(XT):
                last = v_.max(top_v[:, i, :], masked[:, i, :])
            link(last)
            for i in range(XT):
                last = v_.max_index(top_i[:, i, :], top_v[:, i, :], masked[:, i, :])
            v_.tensor_tensor(gate[:, :, :], top_v[:, :, 0:K0], top_v[:, :, 0:1].broadcast_to([P, XT, K0]),
                             ALU.subtract).then_inc(top_ready, 1)
            dve.wait_ge(top_ready, 1)
            link(v_.tensor_copy(top_f[:, :, :], top_i[:, :, 0:K0]))
            link(v_.tensor_tensor(oneh[:, :, :, :], iota_e[:, :].unsqueeze(1).unsqueeze(1)
                                  .broadcast_to([P, XT, K0, NE]),
                                  top_f[:, :, :].unsqueeze(3).broadcast_to([P, XT, K0, NE]), ALU.is_equal))
            with nc.allow_low_precision(reason="zeros and ones, exact in bfloat16"):
                v_.tensor_reduce(sel_b[:, :, :], oneh[:, :, :, :].rearrange("p t k e -> p t e k"), AX.X, ALU.add) \
                    .then_inc(sel_ready, 1)
            dve.wait_ge(gexp_done, 1)
            link(v_.tensor_reduce(gsum[:, :], gate[:, :, :], AX.X, ALU.add))
            link(v_.reciprocal(gsum[:, :], gsum[:, :]))
            link(v_.tensor_tensor(gate[:, :, :], gate[:, :, :], gsum[:, :].unsqueeze(2).broadcast_to([P, XT, K0]),
                                  ALU.mult))
            dve.wait_ge(pos_ready, 1)
            link(v_.tensor_tensor(ohp[:, :, :, :], oneh[:, :, :, :],
                                  PS[:, 7, 0:XT * NE].rearrange("p (t e) -> p t e", t=XT).unsqueeze(2)
                                  .broadcast_to([P, XT, K0, NE]), ALU.mult))
            link(v_.tensor_reduce(posk[:, :, :], ohp[:, :, :, :], AX.X, ALU.add))
            v_.tensor_scalar(keep[:, :, :], posk[:, :, :], float(CAP), None, ALU.is_lt)
            link(v_.tensor_scalar(slot_s[:, :, :], posk[:, :, :], float(CAP - 1), None, ALU.min))
            link(v_.scalar_tensor_tensor(slot_f[:, :, :], top_f[:, :, :], float(CAP), slot_s[:, :, :],
                                         ALU.mult, ALU.add))
            v_.tensor_copy(dest_out[:, :, :], slot_f[:, :, :]).then_inc(dest_ready, 1)
            link(v_.scalar_tensor_tensor(posk[:, :, :], keep[:, :, :], -1e6, slot_f[:, :, :], ALU.mult, ALU.add))
            v_.tensor_scalar(dest_in[:, :, :], posk[:, :, :], 1e6, None, ALU.add).then_inc(dest_ready, 1)
            link(v_.tensor_tensor(gate[:, :, :], gate[:, :, :], keep[:, :, :], ALU.mult))
            for v in range(4):
                j, half = v // 2, v % 2
                dve.wait_ge(sh_silu, v + 1)
                v_.tensor_tensor(hsT[:, j, half * 512:(half + 1) * 512], sg_t[v % 2][:, :], PS[:, 4 + v % 2, :],
                                 ALU.mult).then_inc(sh_mul, 1)
            for i in range(2):
                dve.wait_ge(sh_down, i + 1)
                rows = x_tok[:, 4 * i:4 * i + 4, :]
                v_.tensor_tensor(rows, rows, PS[:, i, :].rearrange("p (t d) -> p t d", t=4), ALU.add) \
                    .then_inc(sh_added, 1)

            def expert(e, k, up, down):
                if up:
                    r = (k - 1) % RING
                    dve.wait_ge(silu_done, e)
                    if not (isinstance(e, int) and e < 3):
                        dve.wait_ge(y_filled, e - 2)
                    v_.tensor_tensor(heT[r % 2][:, :, :], sge[r % 2][:, :, :],
                                     PS[:, 4 + r % 2, 0:HT * CAP].rearrange("p (j c) -> p j c", j=HT), ALU.mult) \
                        .then_inc(he_done, 1)
                if down:
                    r = (k - 2) % RING
                    dve.wait_ge(y_filled, e - 1)
                    if not (isinstance(e, int) and e < 6):
                        dve.wait_ge(y_stored[r % 4], (e - 2 - r % 4) * 4)
                    v_.tensor_copy(ye[r % 4][:, :, :], PS[0:HCAP, 6 + r % 2, 0:2 * D]
                                   .rearrange("p (c d) -> p c d", c=2)).then_inc(y_evac, 1)

            for e in range(RING):
                expert(e, e, e >= 1, e >= 2)
            with dve.Fori(1, NE // RING) as q:
                e0 = RING * q
                for k in range(RING):
                    expert(e0 + k, k, True, True)
            expert(NE, 0, True, True)
            expert(NE + 1, 1, False, True)
            dve.wait_ge(sh_added, 2)

            def combine(b):
                for i in range(QT * b, QT * (b + 1)):
                    dve.wait_ge(gathered[i], 16 * K0)
                    for k in range(K0):
                        link(v_.scalar_tensor_tensor(x_tok[:, i, :], yg[:, i, k, :], gate[:, i, k:k + 1],
                                                     x_tok[:, i, :], ALU.mult, ALU.add))

            for r in range(NB + 2):
                if 0 <= r - 1 < NB:
                    layernorm(1, r - 1)
                if 0 <= r - 2:
                    layernorm(2, r - 2)
                if r < NB:
                    combine(r)
                    stats(1, r)
                b = r - 1
                if 0 <= b < NB:
                    for c in range(2):
                        dve.wait_ge(s2_relu, 2 * b + c + 1)
                        scaled = lg[b % 2][:, 2 * c:2 * c + 2, :]
                        v_.tensor_tensor(scaled, scaled, ff0T[:, 2 * c:2 * c + 2, :], ALU.add) \
                            .then_inc(s2_masked, 1)
                    dve.wait_ge(o2_filled, b + 1)
                    rows = x_tok[:, QT * b:QT * (b + 1), :]
                    v_.scalar_tensor_tensor(rows, PS[:, 6 + b % 2, 0:QT * D].rearrange("p (q d) -> p q d", q=QT), 0.0,
                                            rows, ALU.max, ALU.add).then_inc(o2_read, 1)
                    dve.wait_ge(o2_read, b + 1)
                    stats(2, b)

            dve.wait_ge(r1_filled, 1)
            v_.tensor_tensor(aff[:, :, :], PS[:, 6, 0:XT * E2].rearrange("p (t e) -> p t e", t=XT),
                             br_b[:, :].unsqueeze(1).broadcast_to([P, XT, E2]), ALU.add).then_inc(logits_ready, 1)
            dve.wait_ge(e1_exp, 1)
            link(v_.tensor_scalar(aff2[:, :, :], aff2[:, :, :], 1.0, None, ALU.add))
            link(v_.reciprocal(aff[:, :, :], aff2[:, :, :]))
            for i in range(XT):
                last = v_.max(top1[:, i, :], aff[:, i, :])
            link(last)
            link(v_.tensor_reduce(tsum[:, :], top1[:, :, :], AX.X, ALU.add))
            link(v_.tensor_scalar(tsum[:, :], tsum[:, :], 1e-9, None, ALU.add))
            link(v_.reciprocal(tsum[:, :], tsum[:, :]))
            for i in range(XT):
                last = v_.match_replace(aff2[:, i, :], top1[:, i, :], aff[:, i, :], -1.0)
            link(last)
            link(v_.tensor_tensor(aff2[:, :, :], aff2[:, :, :], aff[:, :, :], ALU.not_equal))
            link(v_.tensor_tensor(aff[:, :, :], aff[:, :, :], aff2[:, :, :], ALU.mult))
            v_.tensor_tensor(w_tok[:, :, 0:E2], aff[:, :, :], tsum[:, :].unsqueeze(2).broadcast_to([P, XT, E2]),
                             ALU.mult).then_inc(w_tok_ready, 1)
            dve.wait_ge(w_tok_ready, 1)
            link(v_.tensor_copy(split[:, :, 0, :], w_tok[:, :, 0:E2]))
            link(v_.tensor_tensor(resid[:, :, :], w_tok[:, :, 0:E2], split[:, :, 0, :], ALU.subtract))
            link(v_.tensor_copy(split[:, :, 1, :], resid[:, :, :]))
            link(v_.tensor_tensor(resid[:, :, :], resid[:, :, :], split[:, :, 1, :], ALU.subtract))
            v_.tensor_copy(split[:, :, 2, :], resid[:, :, :]).then_inc(split_ready, 1)

            def gated(v, half, rows, bias, weighted=True):
                dve.wait_ge(f_silu, v + 1)
                if not (isinstance(v, int) and v < 2):
                    dve.wait_ge(f_acc, v - 1)
                dst = f_t[half] if weighted else f_hT[half]
                ins = v_.scalar_tensor_tensor(dst[0:rows, :], PS[0:rows, 2 + half, :], bias, f_sg[half][0:rows, :],
                                              ALU.add, ALU.mult)
                if weighted:
                    ins.then_inc(f_gated, 1)
                    dve.wait_ge(f_gated, v - 1)
                    v_.tensor_tensor(f_hT[half][:, :], f_t[half][:, :], PS[:, 4 + half, :], ALU.mult) \
                        .then_inc(f_h, 1)
                else:
                    ins.then_inc(f_h, 1)

            for half in range(2):
                gated(half, half, I2, vec[0:I2, 9:10], weighted=False)
            with dve.Fori(0, PR) as j:
                for half in range(2):
                    gated(2 * j + 2 + half, half, P, vec[:, bass.ds(10 + PR + j, 1)])
            for i in range(XT):
                dve.wait_ge(f_acc, 2 * PR + 2 if i >= 4 else 2 * PR + 1)
                v_.tensor_tensor(h_tok[:, i, :], x_tok[:, i, :], PS[:, 6 + i // 4, (i % 4) * D:(i % 4 + 1) * D],
                                 ALU.add).then_inc(out_ready, 1)


def kernel(**inputs):
    import numpy as np
    import concourse.bacc as bacc
    from concourse.bass_utils import run_bass_kernel_spmd

    nc = bacc.Bacc("TRN2", target_bir_lowering=False, num_devices=1)
    arrays, aps = {}, {}
    for name, value in inputs.items():
        a = np.ascontiguousarray(value)
        arrays[f"in_{name}"] = a
        aps[name] = nc.dram_tensor(f"in_{name}", a.shape, mybir.dt.from_np(a.dtype), kind="ExternalInput").ap()
    out = nc.dram_tensor("out_x", arrays["in_x"].shape, mybir.dt.float32, kind="ExternalOutput").ap()
    build(nc, aps, out)
    r = run_bass_kernel_spmd(nc, [arrays], core_ids=[0])
    return r.results[0]["out_x"]
```

```python
from contextlib import ExitStack

import concourse.bass as bass
from concourse import mybir


def build(nc, A, out):
    f32, bf16, u8, u32 = mybir.dt.float32, mybir.dt.bfloat16, mybir.dt.uint8, mybir.dt.uint32
    ALU = mybir.AluOpType
    ACT = mybir.ActivationFunctionType
    AX = mybir.AxisListType

    P = 128
    NB, S, D = A["x"].shape
    SC = A["ctx_1024"].shape[1]
    XT = NB * S // P
    CT = NB * SC // P
    CTB = SC // P
    QT = S // P
    KT = CTB + QT
    NKEY = KT * P
    DH = A["L0_xattn_qn_g"].shape[0]
    INNER = A["L0_xattn_Wq"].shape[1]
    HP = INNER // P
    NP = NB * HP
    HA = DH + 2
    NE, _, HID = A["L0_ffn_wg"].shape
    NG = A["L0_ffn_group_centroids"].shape[0]
    EG = NE // NG
    K0 = 4
    CAP = int(NB * S / NE * K0 * 1.25)
    HCAP = CAP // 2
    HT = HID // P
    RING = 16
    XRING = 8
    E2, _, I2 = A["L1_ffn_Wg"].shape
    K1 = 8
    PR = E2 // 2
    NHALF = NB * S // 512
    BIG_NEG = -1.0e30

    ctx = ExitStack()
    with ctx:
        def sb(name, shape, dt=f32):
            return ctx.enter_context(nc.sbuf_tensor(name, shape, dt))

        def sem(name):
            return ctx.enter_context(nc.semaphore(name))

        slots_in = nc.dram_tensor("slots_in", (NE * CAP, D), f32, kind="Internal").ap()
        slots_out = nc.dram_tensor("slots_out", (NE * CAP, D), f32, kind="Internal").ap()

        ident = sb("ident", [P, P])
        ident_b = sb("ident_b", [P, P], bf16)
        earlier = sb("earlier", [P, P], bf16)
        ones_b = sb("ones_b", [P, P], bf16)
        iota_e = sb("iota_e", [P, NE])
        lower_g = sb("lower_g", [P, NG, NG])
        pair_sel = sb("pair_sel", [96, PR, P], bf16)
        neg_half = sb("neg_half", [P, 32])
        zero_row = sb("zero_row", [P, D])

        vec_rows = sb("vec_rows", [48, P])
        vec = sb("vec", [P, 48])
        mask_u8 = sb("mask_u8", [CT, P], u8)
        mask_f = sb("mask_f", [CT, P])
        mask_bias = sb("mask_bias", [P, CT])
        q_scale = sb("q_scale", [HA, 1])
        cent = sb("cent", [NG + NE, D])
        cent_sq = sb("cent_sq", [NG + NE, D])
        cent_n = sb("cent_n", [NG + NE, 1])
        centT = sb("centT", [D, NG + NE])
        bias0_b = sb("bias0_b", [P, NE])
        bv_b = sb("bv_b", [P, D])
        bout_b = sb("bout_b", [P, D])
        br_b = sb("br_b", [P, E2])
        x_tok = sb("x_tok", [P, XT, D])
        ctx_tok = sb("ctx_tok", [P, CT, D])
        ctxT = sb("ctxT", [D, NB * SC])
        actT = sb("actT", [D, NB, NKEY])
        w_qkv = sb("w_qkv", [D, 3, INNER])
        w_out = sb("w_out", [P, HP, D])
        w_kqv1 = sb("w_kqv1", [D, 3, D])
        kpT = sb("kpT", [D, NB * SC])
        vp = sb("vp", [P, CT, D])
        ff0 = sb("ff0", [P, QT, SC])
        ff0T = sb("ff0T", [P, CTB, S])
        w_sh0 = sb("w_sh0", [D, 2, HID])
        w_shd0 = sb("w_shd0", [P, HT, D])
        w_r1 = sb("w_r1", [D, E2])
        w_sh1 = sb("w_sh1", [D, 2, I2])
        w_shd1 = sb("w_shd1", [I2, D])
        bd_rows = sb("bd_rows", [E2 + 1, D])

        st = sb("st", [P, CT + XT, 6])
        mv = sb("mv", [P, CT + XT, 2])
        ve = sb("ve", [P, CT + XT])
        rstd = sb("rstd", [P, CT + XT])
        h_tok = sb("h_tok", [P, XT, D])
        hT = sb("hT", [D, XT * P])

        act_cur = [sb(f"act_cur{p}", [D, NKEY]) for p in range(2)]
        kq_raw = sb("kq_raw", [P, KT + QT, P])
        kq_sq = sb("kq_sq", [P, KT + QT, P])
        ss = sb("ss", [P, 2 * (KT + QT)])
        ssm = sb("ssm", [P, 2 * (KT + QT)])
        rk = sb("rk", [P, 2 * (KT + QT)])
        kn_aug = sb("kn_aug", [P, KT + QT, 2, HA])
        v_cur = [sb(f"v_cur{p}", [P, KT, 2, DH]) for p in range(2)]
        kT = [sb(f"kT{p}", [HA, 2, NKEY]) for p in range(2)]
        qT = [sb(f"qT{p}", [HA, 2, S]) for p in range(2)]
        kTb = sb("kTb", [HA, 2, NKEY], bf16)
        qTb = sb("qTb", [HA, 2, S], bf16)
        negm = sb("negm", [P, 2 * QT], bf16)
        pT = [sb(f"pT{p}", [P, 2, S]) for p in range(3)]
        p_sum = [sb(f"p_sum{p}", [P, 2, S]) for p in range(2)]
        rcT = sb("rcT", [P, S])
        ones_f = sb("ones_f", [P, P])
        oT = sb("oT", [P, NP, S])

        rn = sb("rn", [P, XT])
        hsq = kq_sq
        score = sb("score", [P, XT, NG + NE])
        cmp1, cmp2 = (p_sum[p][:, :, :].rearrange("p h q -> p (h q)").rearrange("p (t g e) -> p t g e", t=XT, g=NG)
                      for p in range(2))
        gmask = sb("gmask", [P, XT, NG])
        gneg = sb("gneg", [P, XT, NG])
        masked = sb("masked", [P, XT, NE])
        top_v = sb("top_v", [P, XT, 8])
        top_i = sb("top_i", [P, XT, 8], u32)
        top_f = sb("top_f", [P, XT, K0])
        gate = sb("gate", [P, XT, K0])
        gsum = sb("gsum", [P, XT])
        oneh = kq_raw[:, :, :].rearrange("p t (k e) -> p t k e", k=K0)
        ohp = kn_aug[:, :, :, :].rearrange("p t h d -> p (t h d)")[:, 0:XT * K0 * NE] \
            .rearrange("p (t k e) -> p t k e", t=XT, k=K0)
        sel_b = sb("sel_b", [P, XT, NE], bf16)
        posk = sb("posk", [P, XT, K0])
        keep = sb("keep", [P, XT, K0])
        slot_f = sb("slot_f", [P, XT, K0])
        slot_s = sb("slot_s", [P, XT, K0])
        dest_in = sb("dest_in", [P, XT, K0], u32)
        dest_out = sb("dest_out", [P, XT, K0], u32)
        sg_t = [ff0[:, p, :] for p in range(2)]
        hsT = ctx_tok[:, :, :].rearrange("p t d -> p (t d)").rearrange("p (j n) -> p j n", j=HT)

        late = oT[:, :, :].rearrange("p n s -> p (n s)")[:, XT * K0 * D:]
        w_g = [sb(f"w_g{r}", [D, HID])[:, :] for r in range(8)] + [late[:, i * HID:(i + 1) * HID] for i in range(8)]
        w_u = ([sb(f"w_u{r}", [D, HID])[:, :] for r in range(8)]
               + [late[:, (8 + i) * HID:(9 + i) * HID] for i in range(8)])
        w_d = ([ctxT[:, r * HT * D:(r + 1) * HT * D] for r in range(8)]
               + [act_cur[p][:, i * HT * D:(i + 1) * HT * D] for p in range(2) for i in range(3)]
               + [pT[2][:, i, :] for i in range(2)])
        w_d = [w.rearrange("p (c d) -> p c d", c=HT) for w in w_d]
        spare1 = actT[:, :, :].rearrange("d b k -> d (b k)")
        spare2 = w_qkv[:, :, :].rearrange("d a n -> d (a n)")
        xe = [spare2[0:HCAP, r * 2 * D:(r + 1) * 2 * D].rearrange("p (c d) -> p c d", c=2) for r in range(XRING)]
        xeT = [spare1[:, p * CAP:(p + 1) * CAP] for p in range(2)]
        sge, heT = ([spare1[:, (2 + 2 * HT * i + HT * p) * CAP:(2 + 2 * HT * i + HT * (p + 1)) * CAP]
                     .rearrange("p (j c) -> p j c", j=HT) for p in range(2)] for i in range(2))
        ye0 = (2 + 4 * HT) * CAP
        ye = [spare1[0:HCAP, ye0 + p * 2 * D:ye0 + (p + 1) * 2 * D].rearrange("p (c d) -> p c d", c=2)
              for p in range(4)]
        yg = oT[:, :, :].rearrange("p n s -> p (n s)")[:, 0:XT * K0 * D] \
            .rearrange("p (t k d) -> p t k d", t=XT, k=K0)

        ctx_n = oT[:, :, :].rearrange("p n s -> p (n s)")[:, 0:CT * D].rearrange("p (t d) -> p t d", t=CT)

        f_w = [w_g[r][:, :].rearrange("d (a e i) -> d a e i", a=2, e=2) for r in range(4)]
        f_wd = [w_u[r][:, 0:D] for r in range(4)]
        w_tok = sb("w_tok", [P, XT, E2 + 1])
        aff, aff2 = (pT[p][:, 0, :].rearrange("p (t e) -> p t e", t=XT) for p in range(2))
        top1 = sb("top1", [P, XT, 8])
        tsum = sb("tsum", [P, XT])
        split = v_cur[0][:, :, :, :].rearrange("p t h d -> p (t h d)").bitcast(bf16)[:, 0:XT * 3 * E2] \
            .rearrange("p (t s e) -> p t s e", t=XT, s=3)
        resid = masked
        wT = kT[0][0:E2 + 1, :, :].rearrange("p h k -> p (h k)")[:, 0:XT * P]
        splitT = v_cur[1][:, :, :, :].rearrange("p t h d -> p (t h d)").bitcast(bf16)[0:96, 0:XT * P]
        lg = [spare1[:, p * CTB * S:(p + 1) * CTB * S].rearrange("p (k q) -> p k q", k=CTB) for p in range(2)]
        qpT = spare1[:, 2 * CTB * S:2 * CTB * S + XT * P]
        f_sg, f_t, f_hT = ([spare2[:, (2 * i + p) * 512:(2 * i + p + 1) * 512] for p in range(2)] for i in range(3))


        PS = ctx.enter_context(nc.psum_tensor("PS", [P, 8, 512], f32))

        ld_x, ld_ctx, ld_rows, ld_mask, ld_cent, ld_qkv, ld_k1, ld_bc, ld_ff0, ld_w0, ld_w1 = (
            sem("ld_" + n) for n in "x ctx rows mask cent qkv k1 bc ff0 w0 w1".split())
        rows_clear = sem("rows_clear")
        consts_ready = sem("consts_ready")
        dve_step, pool_step, act_step = sem("dve_step"), sem("pool_step"), sem("act_step")
        slots_cleared = sem("slots_cleared")
        stats0, rstd0, lat1, lat_stats, lat_rstd, norm_x, norm_ctx = (
            sem(n) for n in "stats0 rstd0 lat1 lat_stats lat_rstd norm_x norm_ctx".split())
        cent_ss, cent_rn, cent_ready = sem("cent_ss"), sem("cent_rn"), sem("cent_ready")
        mask_ready, vec_ready = sem("mask_ready"), sem("vec_ready")
        s0_filled, s0_act, s0_dve = sem("s0_filled"), sem("s0_act"), sem("s0_dve")
        xb_ready, mask_cast, kv1_filled, kv1_kept, op_filled = (
            sem(n) for n in "xb_ready mask_cast kv1_filled kv1_kept op_filled".split())
        nk_step, o2_read, logits_ready, f_gated = (sem(n) for n in "nk_step o2_read logits_ready f_gated".split())
        pool_passed, act_passed = sem("pool_passed"), sem("act_passed")
        n_row_dmas = 12
        cur_done = [sem(f"cur_done{p}") for p in range(2)]
        ss_done, kn_done, cast_done = (sem(n) for n in "ss_done kn_done cast_done".split())
        w_filled, w_act = sem("w_filled"), sem("w_act")
        m_filled, m_read = sem("m_filled"), sem("m_read")
        st_done, exp_done, pv_done, pool_added, dve_added, sum_done, o_done, rc_done = (
            sem(n) for n in "st_done exp_done pv_done pool_added dve_added sum_done o_done rc_done".split())
        ln_stats, ln_rstd, ln_norm, ln_T, ln_evac = (
            [sem(f"{n}{k}") for k in range(3)] for n in "ln_stats ln_rstd ln_norm ln_T ln_evac".split())
        hsq_done, hsq_summed, rn_done, scores_ready, top_ready, gexp_done, sel_ready, pos_ready, dest_ready = (
            sem(n) for n in
            "hsq_done hsq_summed rn_done scores_ready top_ready gexp_done sel_ready pos_ready dest_ready".split())
        sh_filled, sh_silu, sh_mul, sh_down, sh_added = (
            sem(n) for n in "sh_filled sh_silu sh_mul sh_down sh_added".split())
        ahead_filled, ahead_left = sem("ahead_filled"), sem("ahead_left")
        scattered = sem("scattered")
        w_slot = [sem(f"w_slot{r}") for r in range(RING)]
        x_slot = [sem(f"x_slot{r}") for r in range(XRING)]
        t_filled, xeT_done, gu_filled, silu_done, he_done, y_filled, y_evac = (
            sem(n) for n in
            "t_filled xeT_done gu_filled silu_done he_done y_filled y_evac".split())
        y_stored = [sem(f"y_stored{r}") for r in range(4)]
        gathered = [sem(f"gathered{t}") for t in range(XT)]
        qp_filled, qp_ready, s2_filled, s2_relu, s2_masked, o2_filled = (
            sem(n) for n in "qp_filled qp_ready s2_filled s2_relu s2_masked o2_filled".split())
        r1_filled, e1_exp, w_tok_ready, split_ready, wT_filled, wT_ready = (
            sem(n) for n in
            "r1_filled e1_exp w_tok_ready split_ready wT_filled wT_ready".split())
        f_filled, f_silu, f_h, f_acc = sem("f_filled"), sem("f_silu"), sem("f_h"), sem("f_acc")
        f_slot = [sem(f"f_slot{r}") for r in range(4)]
        out_ready, out_stored = sem("out_ready"), sem("out_stored")

        SETUP = ([("ctx_raw", "act")] * 4 + [("vec", "dve")] + [("ctx_n", "act")] * 4
                 + [("lat", "dve")] * 2 + [("ff0", "act")] * 2 + [("cent", "dve")])

        N_EARLY = len(SETUP) - 3
        SETUP_BANK = [f % 8 for f in range(N_EARLY)] + [3, 0, 1]

        def setup_emptied(f):
            before = max(g for g in range(f) if SETUP_BANK[g] == SETUP_BANK[f])
            who = SETUP[before][1]
            return who, sum(1 for s in SETUP[:before + 1] if s[1] == who)

        def setup_own(kind, k):
            return [i for i, s in enumerate(SETUP) if s[0] == kind][k]

        def work_fills(s):
            if s > NP - 2:
                return []
            k = s < NP - 2
            return ["T0", "T1", "V0", "T2", "T3"] + ["K0", "K1"] * k + ["V1", "R0"]

        PRO = ["K0", "K1", "V0", "V1", "T0", "T1", "T2", "T3", "R0"]

        E_BANK, M_BANK, O_BANK = 0, 2, 7
        W_BANK = {name: 4 + k % 3 for k, name in enumerate(work_fills(1))}
        AHEAD_BANK = (O_BANK, W_BANK["R0"])

        def op_bank(i):
            return 2 if i == 6 else i

        def m_bank(s, i):
            return E_BANK if s == 0 and i % 2 else M_BANK

        def until_left(seq, name):
            while seq and W_BANK[seq[-1]] != W_BANK[name]:
                seq = seq[:-1]
            return seq

        def work(n, s, name):
            steady, before = len(work_fills(1)), PRO if s == 0 else work_fills(s - 1)
            k = work_fills(s).index(name)
            at = until_left(before + work_fills(s)[:k], name)
            base = len(PRO) + steady * n
            return base + k + 1, W_BANK[name], base - len(before) + len(at)

        def work_pro(name):
            k = PRO.index(name)
            return k + 1, W_BANK[name], len(until_left(PRO[:k], name)) or None

        def pairs(eng, pair):
            pair(0, 0)
            pair(1, 1)
            with eng.Fori(1, NP // 2 - 1) as q:
                pair(2 * q, 2)
                pair(2 * q + 1, 3)
            pair(NP - 2, NP - 2)
            pair(NP - 1, NP - 1)

        block = ctx.enter_context(nc.Block())

        def row(eng, i, name, lo, n):
            eng.dma_start(vec_rows[i:i + 1, lo:lo + n], A[name].rearrange("(a n) -> a n", a=1)).then_inc(ld_rows, 16)

        @block.sync
        def _(sp):
            sp.dma_start(ctx_tok[:, 0:8, :], A["ctx_1024"].rearrange("b (t p) d -> p (b t) d", p=P)[:, 0:8, :]) \
                .then_inc(ld_ctx, 16)
            sp.dma_start(ctx_tok[:, 8:16, :], A["ctx_1024"].rearrange("b (t p) d -> p (b t) d", p=P)[:, 8:16, :]) \
                .then_inc(ld_ctx, 16)
            sp.wait_ge(rows_clear, 1)
            for i, name in enumerate(("L0_xattn_ln_x_g", "L0_xattn_ln_x_b", "L0_xattn_ln_l_g", "L0_xattn_ln_l_b")):
                row(sp, i, name, 0, P)
            sp.dma_start(w_qkv[:, 0:2, :], A["L0_xattn_Wkv"].rearrange("d (a n) -> d a n", a=2)) \
                .then_inc(ld_qkv, 16)
            sp.dma_start(w_qkv[:, 2, :], A["L0_xattn_Wq"]).then_inc(ld_qkv, 16)
            sp.dma_start(w_kqv1[:, 0, :], A["L1_xattn_kernel_q"][0, 0]).then_inc(ld_k1, 16)
            sp.dma_start(w_kqv1[:, 1, :], A["L1_xattn_kernel_k"][0, 0]).then_inc(ld_k1, 16)
            sp.dma_start(w_kqv1[:, 2, :], A["L1_xattn_kernel_v"][0, 0]).then_inc(ld_k1, 16)
            sp.dma_start(ff0[:, :, :], A["mask_1xSxS2_ff0"][0].rearrange("(t p) k -> p t k", p=P)) \
                .then_inc(ld_ff0, 16)
            sp.dma_start(w_out[:, :, :], A["L0_xattn_Wout"].rearrange("(c p) d -> p c d", p=P)) \
                .then_inc(ld_w0, 16)
            sp.dma_start(w_sh0[:, 0, :], A["L0_ffn_sg"]).then_inc(ld_w0, 16)
            sp.dma_start(w_sh0[:, 1, :], A["L0_ffn_su"]).then_inc(ld_w0, 16)
            sp.dma_start(w_shd0[:, :, :], A["L0_ffn_sd"].rearrange("(c p) d -> p c d", p=P)) \
                .then_inc(ld_w0, 16)
            sp.dma_start(w_r1[:, :], A["L1_ffn_Wr"]).then_inc(ld_w1, 16)
            sp.dma_start(w_sh1[:, 0, :], A["L1_ffn_Wg_s"]).then_inc(ld_w1, 16)
            sp.dma_start(w_sh1[:, 1, :], A["L1_ffn_Wu_s"]).then_inc(ld_w1, 16)
            sp.dma_start(w_shd1[:, :], A["L1_ffn_Wd_s"]).then_inc(ld_w1, 16)
            sp.dma_start(bd_rows[0:E2, :], A["L1_ffn_bd"]).then_inc(ld_w1, 16)
            sp.dma_start(bd_rows[E2:E2 + 1, :], A["L1_ffn_bd_s"].rearrange("(a d) -> a d", a=1)) \
                .then_inc(ld_w1, 16)
            sp.wait_ge(consts_ready, 9)
            sp.dma_start(slots_in.rearrange("(p a) d -> p a d", p=P),
                         zero_row[:, :].unsqueeze(1).broadcast_to([P, NE * CAP // P, D])) \
                .then_inc(slots_cleared, 16)
            def load_weights(e, r):
                sp.dma_start(w_g[r][:, :], A["L0_ffn_wg"][bass.ds(e, 1)].rearrange("a d h -> (a d) h")) \
                    .then_inc(w_slot[r], 16)
                sp.dma_start(w_u[r][:, :], A["L0_ffn_wu"][bass.ds(e, 1)].rearrange("a d h -> (a d) h")) \
                    .then_inc(w_slot[r], 16)

            def load_down(e, r):
                sp.dma_start(w_d[r][:, :, :],
                             A["L0_ffn_wd"][bass.ds(e, 1)].rearrange("a (c p) d -> p (a c) d", p=P)) \
                    .then_inc(w_slot[r], 16)

            def load_slots(e, r):
                sp.dma_start(xe[r][:, :, :],
                             slots_in[bass.ds(e * CAP, CAP), :].rearrange("(c p) d -> p c d", p=HCAP)) \
                    .then_inc(x_slot[r], 16)

            def store_y(e, k):
                sp.wait_ge(y_evac, e + 1)
                sp.dma_start(slots_out[bass.ds(e * CAP, CAP), :].rearrange("(c p) d -> p c d", p=HCAP),
                             ye[k % 4][:, :, :]).then_inc(y_stored[k % 4], 16)

            def copy_cur(m, p):
                sp.dma_start(act_cur[p][:, :], actT[:, bass.ds(m // HP, 1), :].rearrange("d a k -> d (a k)")) \
                    .then_inc(cur_done[p], 16)

            sp.wait_ge(s0_dve, sum(1 for s in SETUP[:N_EARLY] if s[1] == "dve"))
            sp.wait_ge(s0_act, sum(1 for s in SETUP[:N_EARLY] if s[1] == "act"))
            copy_cur(1, 1)
            sp.wait_ge(w_filled, work_pro("V1")[0])
            copy_cur(2, 0)

            def copy_after(n, s):
                sp.wait_ge(w_filled, work(n, s, "V1")[0])
                copy_cur(n + 3, (s + 1) % 2)

            for r in range(8):
                load_weights(r, r)
            copy_after(0, 0)
            copy_after(1, 1)
            with sp.Fori(1, NP // 2 - 2) as q:
                copy_after(2 * q, 2)
                copy_after(2 * q + 1, 3)
            copy_after(NP - 4, NP - 4)
            sp.wait_ge(op_filled, XT)
            for r in range(8, RING):
                load_weights(r, r)
                load_down(r, r)
            sp.wait_ge(kv1_filled, 8)
            for r in range(8):
                load_down(r, r)
            sp.wait_ge(scattered, 16 * XT * K0)
            for r in range(XRING):
                load_slots(r, r)
            with sp.Fori(0, NE // RING - 1) as q:
                e0 = RING * q
                for k in range(RING):
                    sp.wait_ge(y_filled, e0 + k + 1)
                    load_weights(e0 + RING + k, k)
                    load_down(e0 + RING + k, k)
                    load_slots(e0 + XRING + k, k % XRING)
                    store_y(e0 + k, k)
            for e in range(NE - RING, NE - XRING):
                sp.wait_ge(y_filled, e + 1)
                load_slots(e + XRING, e % XRING)
                store_y(e, e)
            for e in range(NE - XRING, NE):
                store_y(e, e)

            def load_pair(j, r):
                dst = f_w[r]
                sp.dma_start(dst[:, 0, :, :], A["L1_ffn_Wg"][bass.ds(2 * j, 2)].rearrange("e d i -> d e i")) \
                    .then_inc(f_slot[r], 16)
                sp.dma_start(dst[:, 1, :, :], A["L1_ffn_Wu"][bass.ds(2 * j, 2)].rearrange("e d i -> d e i")) \
                    .then_inc(f_slot[r], 16)
                sp.dma_start(f_wd[r], A["L1_ffn_Wd"][bass.ds(2 * j, 2)].rearrange("e i d -> (e i) d")) \
                    .then_inc(f_slot[r], 16)

            for r in range(4):
                load_pair(r, r)
            with sp.Fori(0, PR // 4 - 1) as q:
                j0 = 4 * q
                for r in range(4):
                    sp.wait_ge(f_acc, NHALF * (j0 + r + 2))
                    load_pair(j0 + 4 + r, r)
            for t in range(XT):
                sp.wait_ge(out_ready, t + 1)
                sp.dma_start(out.rearrange("b (t p) d -> p (b t) d", p=P)[:, t, :], h_tok[:, t, :]) \
                    .then_inc(out_stored, 16)
            sp.wait_ge(out_stored, 16 * XT)

        @block.gpsimd
        def _(pool):
            g = nc.gpsimd
            pool_n = [0]

            def link(ins):
                pool_n[0] += 1
                ins.then_inc(pool_step, 1)
                pool.wait_ge(pool_step, pool_n[0])

            link(g.memset(ident[:, :], 0.0))
            g.affine_select(out=ident[:, :], in_=ident[:, :], compare_op=ALU.not_equal, fill=1.0, base=0,
                            pattern=[[-1, P]], channel_multiplier=1).then_inc(consts_ready, 1)
            g.memset(neg_half[:, :], -0.5).then_inc(consts_ready, 1)
            pool.wait_ge(consts_ready, 2)
            g.tensor_copy(ident_b[:, :], ident[:, :]).then_inc(consts_ready, 1)
            g.memset(kn_aug[:, :, :, :], 0.0).then_inc(consts_ready, 1)
            link(g.memset(ones_b[:, :], 1.0))
            g.affine_select(out=earlier[:, :], in_=ones_b[:, :], compare_op=ALU.is_gt, fill=0.0, base=0,
                            pattern=[[1, P]], channel_multiplier=-1).then_inc(consts_ready, 1)
            g.iota(iota_e[:, :], pattern=[[1, NE]], base=0, channel_multiplier=0,
                   allow_small_or_imprecise_dtypes=True).then_inc(consts_ready, 1)
            link(g.memset(lower_g[:, :, :], 1.0))
            g.affine_select(out=lower_g[:, :, :], in_=lower_g[:, :, :], compare_op=ALU.is_gt, fill=0.0,
                            base=0, pattern=[[1, NG], [-1, NG]], channel_multiplier=0) \
                .then_inc(consts_ready, 1)
            g.memset(w_tok[:, :, E2:E2 + 1], 1.0).then_inc(consts_ready, 1)
            g.memset(zero_row[:, :], 0.0).then_inc(consts_ready, 1)
            pool.wait_ge(consts_ready, 9)
            g.memset(kn_aug[:, 0:KT, :, DH:DH + 1], 1.0).then_inc(consts_ready, 1)
            g.memset(kn_aug[:, KT:KT + QT, :, DH + 1:DH + 2], 1.0).then_inc(consts_ready, 1)
            g.memset(ones_f[:, :], 1.0).then_inc(consts_ready, 1)
            pool.wait_ge(stats0, XT)
            link(g.tensor_scalar(ve[:, CT:], mv[:, CT:, 1], 1e-5, None, ALU.add))
            g.tensor_tensor(rstd[:, CT:], ve[:, CT:], neg_half[:, 0:XT], ALU.pow).then_inc(rstd0, 1)
            pool.wait_ge(stats0, CT + XT)
            link(g.tensor_scalar(ve[:, 0:CT], mv[:, 0:CT, 1], 1e-5, None, ALU.add))
            g.tensor_tensor(rstd[:, 0:CT], ve[:, 0:CT], neg_half[:, 0:CT], ALU.pow).then_inc(rstd0, 1)
            pool.wait_ge(lat_stats, XT)
            link(g.tensor_scalar(ve[:, CT:], mv[:, CT:, 1], 1e-5, None, ALU.add))
            g.tensor_tensor(rstd[:, CT:], ve[:, CT:], neg_half[:, 0:XT], ALU.pow).then_inc(lat_rstd, 1)
            pool.wait_ge(ld_cent, 32)
            g.tensor_tensor(cent_sq[:, :], cent[:, :], cent[:, :], ALU.mult).then_inc(cent_ss, 1)
            pool.wait_ge(cent_ss, 2)
            link(g.tensor_scalar(cent_n[:, :], cent_n[:, :], 1e-24, None, ALU.max))
            link(g.tensor_tensor(cent_n[:, :], cent_n[:, :], neg_half[0:NG + NE, 0:1], ALU.pow))
            g.tensor_scalar(cent[:, :], cent[:, :], cent_n[:, 0:1], None, ALU.mult).then_inc(cent_ready, 1)
            def stand_alone():
                pool.sem_inc(pool_passed, 1)

            def norm(m, t3_count):
                b = m // HP

                def mean(j):
                    pool.wait_ge(ss_done, 2 * m + j + 1)
                    stand_alone()
                    g.tensor_scalar(ssm[:, 8 * j:8 * j + 8], ss[:, 8 * j:8 * j + 8], 1.0 / DH, 1e-16,
                                    ALU.mult, ALU.max).then_inc(nk_step, 1)

                def root(j):
                    pool.wait_ge(nk_step, 4 * m + 2 * j + 1)
                    g.tensor_tensor(rk[:, 8 * j:8 * j + 8], ssm[:, 8 * j:8 * j + 8], neg_half[:, 0:8], ALU.pow) \
                        .then_inc(nk_step, 1)

                def scale(j, steps):
                    pool.wait_ge(nk_step, 4 * m + steps)
                    g.tensor_tensor(
                        kn_aug[:, 4 * j:4 * j + 4, :, 0:DH],
                        kq_raw[:, 4 * j:4 * j + 4, :].rearrange("p t (h d) -> p t h d", h=2),
                        rk[:, 8 * j:8 * j + 8].rearrange("p (t h) -> p t h", h=2).unsqueeze(3)
                        .broadcast_to([P, 4, 2, DH]), ALU.mult).then_inc(kn_done, 1)

                if t3_count is not None:
                    pool.wait_ge(w_filled, t3_count)
                    stand_alone()
                g.tensor_copy(
                    kn_aug[:, 0:CTB, :, DH + 1:DH + 2].rearrange("p t h a -> p t (h a)"),
                    mask_bias[:, bass.ds(b * CTB, CTB)].unsqueeze(2).broadcast_to([P, CTB, 2])) \
                    .then_inc(kn_done, 1)
                mean(0)
                root(0)
                mean(1)
                scale(0, 2)
                root(1)
                scale(1, 4)

            def add(n, s, c):
                pool.wait_ge(exp_done, 6 * n + c + 1)
                if c == 1:
                    if s > 1:
                        pool.wait_ge(sum_done, n - 1)
                    first = pT[0]
                else:
                    pool.wait_ge(pool_added, 2 * n + c - 1)
                    first = p_sum[s % 2]
                stand_alone()
                g.tensor_tensor(p_sum[s % 2][:, :, :], first[:, :, :], pT[c % 3][:, :, :], ALU.add) \
                    .then_inc(pool_added, 1)

            pool.wait_ge(mask_ready, 1)
            norm(0, None)
            pool.wait_ge(ld_bc, 64)
            g.tensor_tensor(x_tok[:, :, :], x_tok[:, :, :], bout_b[:, :].unsqueeze(1).broadcast_to([P, XT, D]),
                            ALU.add).then_inc(xb_ready, 1)
            norm(1, work_pro("T3")[0])

            def pair(n, s):
                add(n, s, 1)
                add(n, s, 2)
                if s < NP - 2:
                    norm(n + 2, work(n, s, "T3")[0])

            pairs(pool, pair)

            def ln_pow(k, b):
                tiles = slice(QT * b, QT * (b + 1))
                pool.wait_ge(ln_stats[k], QT * (b + 1))
                link(g.tensor_scalar(ve[:, tiles], mv[:, tiles, 1], 1e-5, None, ALU.add))
                g.tensor_tensor(rstd[:, tiles], ve[:, tiles], neg_half[:, 0:QT], ALU.pow).then_inc(ln_rstd[k], 1)

            def squares(b):
                tiles = slice(QT * b, QT * (b + 1))
                pool.wait_ge(ln_norm[0], QT * (b + 1))
                g.tensor_tensor(hsq[:, tiles, :], h_tok[:, tiles, :], h_tok[:, tiles, :], ALU.mult) \
                    .then_inc(hsq_done, 1)

            def roots(b):
                tiles = slice(QT * b, QT * (b + 1))
                pool.wait_ge(hsq_summed, b + 1)
                link(g.tensor_scalar(rn[:, tiles], rn[:, tiles], 1e-24, None, ALU.max))
                g.tensor_tensor(rn[:, tiles], rn[:, tiles], neg_half[:, 0:QT], ALU.pow).then_inc(rn_done, 1)

            for b in range(NB):
                ln_pow(0, b)
                if b:
                    squares(b - 1)
                if b > 1:
                    roots(b - 2)
            squares(NB - 1)
            roots(NB - 2)
            roots(NB - 1)
            link(g.memset(pair_sel[:, :, :], 0.0))
            for s in range(3):
                view = pair_sel[32 * s:32 * s + 32, :, :].rearrange("p j (c i) -> p j c i", c=2)
                g.affine_select(out=view, in_=view, compare_op=ALU.not_equal, fill=1.0, base=0,
                                pattern=[[-2, PR], [-1, 2], [0, I2]], channel_multiplier=1) \
                    .then_inc(consts_ready, 1)
            pool.wait_ge(consts_ready, 15)
            pool.wait_ge(slots_cleared, 16)
            pool.wait_ge(dest_ready, 2)
            for t in range(XT):
                for k in range(K0):
                    g.indirect_dma_start(
                        out=slots_in[:, :],
                        out_offset=bass.IndirectOffsetOnAxis(ap=dest_in[:, t, k:k + 1], axis=0),
                        in_=h_tok[:, t, :], in_offset=None,
                        bounds_check=NE * CAP - 1, oob_is_err=False).then_inc(scattered, 16)
            for r in range(4):
                pool.wait_ge(y_stored[r], 16 * NE // 4)
            def gather(t):
                for k in range(K0):
                    g.indirect_dma_start(
                        out=yg[:, t, k, :], out_offset=None, in_=slots_out[:, :],
                        in_offset=bass.IndirectOffsetOnAxis(ap=dest_out[:, t, k:k + 1], axis=0),
                        bounds_check=NE * CAP - 1, oob_is_err=False).then_inc(gathered[t], 16)

            for r in range(NB + 3):
                if r < NB:
                    gather(QT * r)
                if 0 <= r - 1 < NB:
                    ln_pow(1, r - 1)
                if r >= 3:
                    ln_pow(2, r - 3)
                if r < NB:
                    gather(QT * r + 1)

        @block.tensor
        def _(pe):
            t = nc.tensor

            def emptied(free):
                if free is not None:
                    pe.wait_ge(w_act, free)

            def setup_bank(f):
                if f >= 8:
                    who, n = setup_emptied(f)
                    pe.wait_ge(s0_act if who == "act" else s0_dve, n)
                return SETUP_BANK[f]

            def setup_fill(f, kind):
                k = f - setup_own(kind, 0)
                bank = setup_bank(f)
                if kind == "vec":
                    pe.wait_ge(ld_rows, 16 * n_row_dmas)
                    pe.wait_ge(mask_cast, 1)
                    t.transpose(PS[:, bank, 0:48], vec_rows[:, :], ident[0:48, 0:48])
                    last = t.transpose(PS[:, bank, 64:64 + CT], mask_f[:, :], ident[0:CT, 0:CT])
                elif kind == "ctx_raw":
                    pe.wait_ge(ld_ctx, 32)
                    for i in range(4):
                        last = t.transpose(PS[:, bank, i * P:(i + 1) * P], ctx_tok[:, 4 * k + i, :], ident[:, :])
                elif kind == "cent":
                    pe.wait_ge(cent_ready, 1)
                    last = t.transpose(PS[:, bank, 0:NG + NE], cent[:, :], ident[0:NG + NE, 0:NG + NE])
                elif kind == "lat":
                    pe.wait_ge(norm_x, 4 * k + 4)
                    for i in range(4):
                        last = t.transpose(PS[:, bank, i * P:(i + 1) * P], h_tok[:, 4 * k + i, :], ident[:, :])
                elif kind == "ctx_n":
                    pe.wait_ge(norm_ctx, 4 * k + 4)
                    for i in range(4):
                        last = t.transpose(PS[:, bank, i * P:(i + 1) * P], ctx_n[:, 4 * k + i, :], ident[:, :])
                elif kind == "ff0":
                    pe.wait_ge(ld_ff0, 16)
                    for i in range(CTB):
                        last = t.transpose(PS[:, bank, i * P:(i + 1) * P], ff0[:, k, i * P:(i + 1) * P], ident[:, :])
                last.then_inc(s0_filled, 1)

            pe.wait_ge(consts_ready, 2)
            for f in range(N_EARLY):
                setup_fill(f, SETUP[f][0])

            def project(m, s, name, info, filled=w_filled):
                _, bank, free = info
                emptied(free)
                half = int(name[1]) % 2
                if name[0] == "K" and half == 0 and s > 0:
                    pe.wait_ge(cur_done[s % 2], (m - s % 2) * 8 + (16 if s % 2 else 0))
                cols = bass.ds(m % HP * P, P)
                for i in range(2 if name == "V1" else 4):
                    tile_i = 4 * half + i
                    a = 1 if name[0] == "V" else 2 if tile_i >= KT else 0
                    if tile_i >= KT:
                        tile_i -= QT
                    last = t.matmul(PS[:, bank, i * P:(i + 1) * P], act_cur[s % 2][:, tile_i * P:(tile_i + 1) * P],
                                    w_qkv[:, a, cols], start=True, stop=True)
                last.then_inc(filled, 1)

            def turn(m, name, info):
                _, bank, free = info
                emptied(free)
                j = int(name[1])
                if j < 2:
                    pe.wait_ge(kn_done, 3 * m + 2 + j)
                for i in range(4):
                    last = t.transpose(PS[0:HA, bank, i * P:(i + 1) * P],
                                       kn_aug[:, 4 * (j % 2) + i, j // 2, :], ident[:, :])
                last.then_inc(w_filled, 1)

            def maxima(n, s, i):
                h, qt = i // QT, i % QT
                pe.wait_ge(cast_done, 4 * n + 2 * h + 2)
                if s > 0 or i > 1:
                    pe.wait_ge(m_read, 4 * n + i - (1 if s == 0 else 0))
                for c in range(2):
                    last = t.matmul(PS[:, m_bank(s, i) + c, 0:NKEY // 2], qTb[:, h, qt * P:(qt + 1) * P],
                                    kTb[:, h, c * (NKEY // 2):(c + 1) * (NKEY // 2)], start=True, stop=True)
                last.then_inc(m_filled, 1)

            def shift_rows(n, info):
                _, bank, free = info
                emptied(free)
                pe.wait_ge(m_read, 4 * n + 4)
                for i in range(2 * QT):
                    last = t.matmul(PS[DH:DH + 1, bank, i * P:(i + 1) * P], negm[:, i:i + 1], ident_b[:, :],
                                    start=True, stop=True)
                last.then_inc(w_filled, 1)

            def scores(n, s, c):
                if c == 0:
                    pe.wait_ge(w_act, work_pro("R0")[0] if s == 0 else work(n - 1, s - 1, "R0")[0])
                if not (s == 0 and c < 2):
                    pe.wait_ge(exp_done, 6 * n + c - 1)
                for h in range(2):
                    last = t.matmul(PS[:, E_BANK + c % 2, h * S:(h + 1) * S], kT[s % 2][:, h, c * P:(c + 1) * P],
                                    qT[s % 2][:, h, :], start=True, stop=True)
                last.then_inc(st_done, 1)

            def weigh(n, s, c):
                pe.wait_ge(exp_done, 6 * n + c + 1)
                if c == 0 and s > 0:
                    pe.wait_ge(o_done, n)
                for h in range(2):
                    last = t.matmul(PS[h * DH:(h + 1) * DH, O_BANK, 0:S], v_cur[s % 2][:, c, h, :],
                                    pT[c % 3][:, h, :], start=(c == 0), stop=(c == KT - 1),
                                    skip_group_check=True)
                last.then_inc(pv_done, 1)

            def sums(n, s):
                pe.wait_ge(dve_added, 3 * n + 3)
                for h in range(2):
                    last = t.matmul(PS[h * DH:(h + 1) * DH, O_BANK, S:2 * S], ones_f[:, 0:DH],
                                    p_sum[s % 2][:, h, :], start=True, stop=True, skip_group_check=True)
                last.then_inc(sum_done, 1)

            pe.wait_ge(ld_qkv, 32)
            pe.wait_ge(consts_ready, 12)
            for name in ("K0", "K1", "V0", "V1"):
                if name == "K0":
                    pe.wait_ge(s0_act, sum(1 for s in SETUP[:N_EARLY] if s[1] == "act"))
                    pe.wait_ge(s0_dve, sum(1 for s in SETUP[:setup_own("lat", 0) + 1] if s[1] == "dve"))
                project(0, 0, name, work_pro(name))
            for f in range(N_EARLY, len(SETUP)):
                setup_fill(f, SETUP[f][0])
            pe.wait_ge(s0_dve, sum(1 for s in SETUP if s[1] == "dve"))
            pe.wait_ge(s0_act, sum(1 for s in SETUP if s[1] == "act"))
            pe.wait_ge(w_act, work_pro("V0")[0])
            for j in range(2):
                project(1, 1, f"K{j}", (None, AHEAD_BANK[j], None), ahead_filled)
            for name in ("T0", "T1", "T2", "T3"):
                turn(0, name, work_pro(name))
            for i in range(4):
                maxima(0, 0, i)
            pe.wait_ge(ahead_left, 2)
            shift_rows(0, work_pro("R0"))

            def pair(n, s):
                def w(name):
                    return work(n, s, name)

                last, kq = s > NP - 2, s < NP - 2

                def turns(*names):
                    if not last:
                        for name in names:
                            turn(n + 1, name, w(name))

                def step(name):
                    if name[0] == "V" and not last:
                        project(n + 1, s + 1, name, w(name))
                    if name[0] == "K" and kq:
                        project(n + 2, s + 2, name, w(name))

                def maxima_next(i):
                    if not last:
                        maxima(n + 1, s + 1, i)

                if s > 0:
                    weigh(n - 1, s - 1, 5)
                scores(n, s, 0)
                if s > 0:
                    sums(n - 1, s - 1)
                turns("T0", "T1")
                step("V0")
                scores(n, s, 1)
                turns("T2", "T3")
                scores(n, s, 2)
                weigh(n, s, 0)
                maxima_next(0)
                step("K0")
                step("K1")
                maxima_next(1)
                step("V1")
                scores(n, s, 3)
                weigh(n, s, 1)
                maxima_next(2)
                scores(n, s, 4)
                weigh(n, s, 2)
                maxima_next(3)
                scores(n, s, 5)
                weigh(n, s, 3)
                if not last:
                    shift_rows(n + 1, w("R0"))
                weigh(n, s, 4)

            pairs(pe, pair)
            weigh(NP - 1, NP - 1, 5)
            sums(NP - 1, NP - 1)

            pe.wait_ge(ld_w0, 64)
            def turn_h(k, b, bank, bank_left):
                pe.wait_ge(ln_norm[k], QT * (b + 1))
                if bank_left > 0:
                    pe.wait_ge(ln_evac[k], bank_left)
                for i in range(QT):
                    last = t.transpose(PS[:, bank, i * P:(i + 1) * P], h_tok[:, QT * b + i, :], ident[:, :])
                last.then_inc(ln_T[k], 1)

            def route(b):
                pe.wait_ge(ln_evac[0], b + 1)
                for i in range(QT * b, QT * (b + 1)):
                    last = t.matmul(PS[:, 6, i * (NG + NE):(i + 1) * (NG + NE)], hT[:, i * P:(i + 1) * P],
                                    centT[:, :], start=True, stop=True)
                last.then_inc(scores_ready, 1)

            for i in range(XT):
                b, qt = i // QT, i % QT
                if qt == 0:
                    pe.wait_ge(o_done, HP * (b + 1))
                if op_bank(i) != i:
                    pe.wait_ge(ln_stats[0], QT * (op_bank(i) // QT + 1))
                for c in range(HP):
                    last = t.matmul(PS[:, op_bank(i), 0:D], oT[:, b * HP + c, qt * P:(qt + 1) * P], w_out[:, c, :],
                                    start=(c == 0), stop=(c == HP - 1))
                last.then_inc(op_filled, 1)
                if qt == 0 and b > 2:
                    route(b - 3)
                if qt == 0 and b > 1:
                    turn_h(0, b - 2, b % 2, b - 3)
            route(NB - 3)
            turn_h(0, NB - 2, NB % 2, NB - 3)
            turn_h(0, NB - 1, (NB - 1) % 2, NB - 2)
            route(NB - 2)
            route(NB - 1)


            def shared_up(v):
                j, half = v // 2, v % 2
                if v >= 2:
                    pe.wait_ge(sh_mul, v - 1)
                for a in range(2):
                    last = t.matmul(PS[:, 2 + 2 * a + v % 2, :], w_sh0[:, a, j * P:(j + 1) * P],
                                    hT[:, half * 512:(half + 1) * 512], start=True, stop=True)
                last.then_inc(sh_filled, 1)

            shared_up(0)
            shared_up(1)
            pe.wait_ge(sel_ready, 1)
            for i in range(XT):
                for j in range(i + 1):
                    last = t.matmul(PS[:, 7, i * NE:(i + 1) * NE], earlier[:, :] if j == i else ones_b[:, :],
                                    sel_b[:, j, :], start=(j == 0), stop=(j == i))
            last.then_inc(pos_ready, 1)
            shared_up(2)
            shared_up(3)
            pe.wait_ge(ld_k1, 48)
            pe.wait_ge(ld_bc, 64)
            for f in range(8):
                k, bank = f % 4, f % 2
                if f >= 2:
                    pe.wait_ge(kv1_kept, f - 1)
                if f < 4:
                    last = t.matmul(PS[:, bank, :], w_kqv1[:, 1, :], ctxT[:, 512 * k:512 * (k + 1)],
                                    start=True, stop=True)
                else:
                    for i in range(4):
                        cols = slice(i * P, (i + 1) * P)
                        t.matmul(PS[:, bank, cols], ctxT[:, (4 * k + i) * P:(4 * k + i + 1) * P], w_kqv1[:, 2, :],
                                 start=(i == 0), stop=False, skip_group_check=True)
                        last = t.matmul(PS[:, bank, cols], ones_f[0:1, :], bv_b[0:1, :],
                                        start=False, stop=True, skip_group_check=True)
                last.then_inc(kv1_filled, 1)
            pe.wait_ge(sh_mul, 4)
            pe.wait_ge(kv1_kept, 8)
            for i in range(XT):
                for j in range(HT):
                    last = t.matmul(PS[:, i // 4, (i % 4) * P:(i % 4 + 1) * P], hsT[:, j, i * P:(i + 1) * P],
                                    w_shd0[:, j, :], start=(j == 0), stop=(j == HT - 1))
                if i % 4 == 3:
                    last.then_inc(sh_down, 1)

            pe.wait_ge(sh_added, 2)

            def expert(e, k, up, down, turn_in=True):
                if turn_in:
                    kx = k % XRING
                    pe.wait_ge(x_slot[kx], (e - kx) * 2 + 16)
                    if up:
                        if not (isinstance(e, int) and e < 2):
                            pe.wait_ge(xeT_done, e - 1)
                    for c in range(2):
                        last = t.transpose(PS[:, k % 2, c * HCAP:(c + 1) * HCAP], xe[kx][:, c, :],
                                           ident[0:HCAP, 0:HCAP])
                    last.then_inc(t_filled, 1)
                if up:
                    r = (k - 1) % RING
                    pe.wait_ge(xeT_done, e)
                    pe.wait_ge(w_slot[r], (e - 1 - r) * 3 + 48)
                    if not (isinstance(e, int) and e < 3):
                        pe.wait_ge(he_done, e - 2)
                    for a, w in enumerate((w_g[r], w_u[r])):
                        for j in range(HT):
                            last = t.matmul(PS[:, 2 + 2 * a + r % 2, j * CAP:(j + 1) * CAP],
                                            w[:, j * P:(j + 1) * P], xeT[r % 2][:, :], start=True, stop=True)
                    last.then_inc(gu_filled, 1)
                if down:
                    r = (k - 2) % RING
                    pe.wait_ge(he_done, e - 1)
                    if not (isinstance(e, int) and e < 4):
                        pe.wait_ge(y_evac, e - 3)
                    for c in range(2):
                        for j in range(HT):
                            last = t.matmul(PS[0:HCAP, 6 + r % 2, c * D:(c + 1) * D],
                                            heT[r % 2][:, j, c * HCAP:(c + 1) * HCAP], w_d[r][:, j, :],
                                            start=(j == 0), stop=(j == HT - 1))
                    last.then_inc(y_filled, 1)

            for e in range(RING):
                expert(e, e, e >= 1, e >= 2)
            with pe.Fori(1, NE // RING) as q:
                e0 = RING * q
                for k in range(RING):
                    expert(e0 + k, k, True, True)
            expert(NE, 0, True, True, turn_in=False)
            expert(NE + 1, 1, False, True, turn_in=False)

            pe.wait_ge(he_done, NE)
            pe.wait_ge(y_evac, NE)

            def queries1(b):
                pe.wait_ge(ln_evac[1], b + 1)
                if b:
                    pe.wait_ge(qp_ready, b)
                t.matmul(PS[:, 2, 0:S], w_kqv1[:, 0, :], hT[:, b * S:(b + 1) * S], start=True, stop=True) \
                    .then_inc(qp_filled, 1)

            def scores1(i):
                b, c = i // 2, i % 2
                pe.wait_ge(qp_ready, b + 1)
                if i >= 2:
                    pe.wait_ge(s2_relu, i - 1)
                for kt in range(2):
                    col = b * SC + (2 * c + kt) * P
                    last = t.matmul(PS[:, 4 + i % 2, kt * S:(kt + 1) * S], kpT[:, col:col + P],
                                    qpT[:, b * S:(b + 1) * S], start=True, stop=True)
                last.then_inc(s2_filled, 1)

            def weigh1(b):
                pe.wait_ge(s2_masked, 2 * b + 2)
                if b >= 2:
                    pe.wait_ge(o2_read, b - 1)
                for qt in range(QT):
                    for kt in range(CTB):
                        last = t.matmul(PS[:, 6 + b % 2, qt * D:(qt + 1) * D], lg[b % 2][:, kt, qt * P:(qt + 1) * P],
                                        vp[:, b * CTB + kt, :], start=(kt == 0), stop=(kt == CTB - 1))
                last.then_inc(o2_filled, 1)

            def route1(b):
                pe.wait_ge(ld_w1, 96)
                pe.wait_ge(ln_evac[2], b + 1)
                for i in range(QT * b, QT * (b + 1)):
                    last = t.matmul(PS[:, 3, i * E2:(i + 1) * E2], hT[:, i * P:(i + 1) * P],
                                    w_r1[:, :], start=True, stop=True)
                last.then_inc(r1_filled, 1)

            for r in range(1, NB + 3):
                if r - 1 < NB:
                    turn_h(1, r - 1, 0, r - 1)
                    queries1(r - 1)
                if r == NB + 2:
                    for b in range(NB - 1):
                        route1(b)
                if r >= 3:
                    turn_h(2, r - 3, 1, r - 3)
                if 0 <= r - 2 < NB:
                    weigh1(r - 2)
                if r - 1 < NB:
                    scores1(2 * (r - 1))
                    scores1(2 * (r - 1) + 1)

            route1(NB - 1)


            def up1(v, v0, w_gate, w_up, rows, spread=None):
                half = v0 % 2
                if not (isinstance(v, int) and v < 2):
                    pe.wait_ge(f_h, v - 1)
                cols = hT[:, half * 512:(half + 1) * 512]
                t.matmul(PS[0:rows, 0 + half, :], w_gate, cols, start=True, stop=True)
                if isinstance(v, int) and v == 1:
                    pe.wait_ge(e1_exp, 1)
                last = t.matmul(PS[0:rows, 2 + half, :], w_up, cols, start=True, stop=True)
                if spread is not None:
                    last = t.matmul(PS[:, 4 + half, :], spread, splitT[:, half * 512:(half + 1) * 512],
                                    start=True, stop=True)
                last.then_inc(f_filled, 1)

            def down1(v, half, w, rows, first=False):
                pe.wait_ge(f_h, v + 1)
                for q in range(4):
                    last = t.matmul(PS[:, 6 + half, q * D:(q + 1) * D], f_hT[half][0:rows, q * P:(q + 1) * P], w,
                                    start=(first and q == 0), stop=True, skip_group_check=True)
                last.then_inc(f_acc, 1)

            for half in range(2):
                up1(half, half, w_sh1[:, 0, :], w_sh1[:, 1, :], I2)
            pe.wait_ge(w_tok_ready, 1)
            for i in range(XT):
                last = t.transpose(PS[0:E2 + 1, 4 + i // 4, (i % 4) * P:(i % 4 + 1) * P], w_tok[:, i, :], ident[:, :])
                if i % 4 == 3:
                    last.then_inc(wT_filled, 1)
            pe.wait_ge(split_ready, 1)
            split_ps = PS[:, 7, :].bitcast(bf16)
            for i in range(XT):
                last = t.transpose(split_ps[0:96, i * P:(i + 1) * P], split[:, i, :, :].rearrange("p s e -> p (s e)"),
                                   ident_b[:, :])
            last.then_inc(wT_filled, 1)
            pe.wait_ge(wT_ready, 3)
            for half in range(2):
                down1(half, half, w_shd1[:, :], I2, first=True)
            for half in range(2):
                for q in range(4):
                    t.matmul(PS[:, 6 + half, q * D:(q + 1) * D], wT[:, (4 * half + q) * P:(4 * half + q + 1) * P],
                             bd_rows[:, :], start=False, stop=True, skip_group_check=True)

            def unit(j, r, half, down):
                v = 2 * j + 2 + half
                if half == 0:
                    pe.wait_ge(f_slot[r], (j - r) * 12 + 48)
                up1(v, half, f_w[r][:, 0, :, :].rearrange("d e i -> d (e i)"),
                    f_w[r][:, 1, :, :].rearrange("d e i -> d (e i)"), P,
                    spread=pair_sel[:, bass.ds(j, 1), :].rearrange("p a c -> p (a c)"))
                if down:
                    rd = r if half else (r - 1) % 4
                    down1(v - 1, 1 - half, f_wd[rd], P)

            unit(0, 0, 0, False)
            unit(0, 0, 1, True)
            for r in range(1, 4):
                unit(r, r, 0, True)
                unit(r, r, 1, True)
            with pe.Fori(1, PR // 4) as q:
                j0 = 4 * q
                for r in range(4):
                    unit(j0 + r, r, 0, True)
                    unit(j0 + r, r, 1, True)
            down1(2 * PR + 1, 1, f_wd[3], P)

        @block.scalar
        def _(act):
            s_ = nc.scalar
            act.dma_start(x_tok[:, :, :], A["x"].rearrange("b (t p) d -> p (b t) d", p=P)).then_inc(ld_x, 16)
            act.dma_start(mask_u8[:, :], A["mask_BxS2_bf1"].rearrange("b (t p) -> (b t) p", p=P)) \
                .then_inc(ld_mask, 16)
            act.dma_start(cent[0:NG, :], A["L0_ffn_group_centroids"]).then_inc(ld_cent, 16)
            act.dma_start(cent[NG:, :], A["L0_ffn_expert_centroids"]).then_inc(ld_cent, 16)
            act.wait_ge(rows_clear, 1)

            for i, name in enumerate(("L1_xattn_bias_q", "L1_xattn_bias_k")):
                row(act, 4 + i, name, 0, P)
            for i, name in enumerate(("L0_xattn_qn_g", "L0_xattn_kn_g", "L1_ffn_bg_s", "L1_ffn_bu_s")):
                row(act, 6 + i, name, 0, DH)
            act.dma_start(vec_rows[10:10 + PR, :], A["L1_ffn_bg"].rearrange("(j e) i -> j (e i)", e=2)) \
                .then_inc(ld_rows, 16)
            act.dma_start(vec_rows[10 + PR:10 + 2 * PR, :], A["L1_ffn_bu"].rearrange("(j e) i -> j (e i)", e=2)) \
                .then_inc(ld_rows, 16)
            for dst, name, n in ((bias0_b, "L0_ffn_bias", NE), (bv_b, "L1_xattn_bias_v", D),
                                 (bout_b, "L0_xattn_bout", D), (br_b, "L1_ffn_br", E2)):
                act.dma_start(dst[:, :], A[name].partition_broadcast(P)).then_inc(ld_bc, 16)

            for f in range(N_EARLY):
                kind, who = SETUP[f]
                if who != "act":
                    continue
                k = f - setup_own(kind, 0)
                src = PS[:, SETUP_BANK[f], :]
                act.wait_ge(s0_filled, f + 1)
                if kind == "ctx_raw":
                    s_.activation(ctxT[:, 512 * k:512 * (k + 1)], src, ACT.Copy).then_inc(s0_act, 1)
                elif kind == "ctx_n":
                    act.wait_ge(vec_ready, 1)
                    if k == 0:
                        s_.activation(act_cur[0][:, 0:SC], src, ACT.Identity, bias=vec[:, 1:2], scale=vec[:, 0:1])
                    s_.activation(actT[:, k, 0:SC], src, ACT.Identity, bias=vec[:, 1:2], scale=vec[:, 0:1]) \
                        .then_inc(s0_act, 1)

            def keep_ff0(k):
                f = setup_own("ff0", 0) + k
                act.wait_ge(s0_filled, f + 1)
                s_.activation(ff0T[:, :, k * P:(k + 1) * P],
                              PS[:, SETUP_BANK[f], :].rearrange("p (c q) -> p c q", c=CTB), ACT.Copy) \
                    .then_inc(s0_act, 1)

            def keep_v(s, name, info):
                count, bank, _ = info
                act.wait_ge(w_filled, count)
                lo, hi = (0, 4) if name == "V0" else (4, KT)
                s_.activation(v_cur[s % 2][:, lo:hi, :, :],
                              PS[:, bank, 0:(hi - lo) * P].rearrange("p (t h d) -> p t h d", t=hi - lo, h=2),
                              ACT.Copy).then_inc(w_act, 1)

            def keep_kq(m, s, j, info, filled=w_filled, left=w_act):
                count, bank, _ = info
                act.wait_ge(filled, count)
                if j == 0 and s > 0:
                    act.wait_ge(kn_done, 3 * m)
                src = PS[:, bank, :].rearrange("p (t n) -> p t n", t=4)
                s_.activation(kq_sq[:, 4 * j:4 * j + 4, :], src, ACT.Square)
                s_.activation(kq_raw[:, 4 * j:4 * j + 4, :], src, ACT.Copy).then_inc(left, 1)

            def keep_turned(s, name, info):
                count, bank, _ = info
                act.wait_ge(w_filled, count)
                h = int(name[1]) // 2
                if int(name[1]) % 2 == 0:
                    s_.activation(kTb[:, h, 0:4 * P], PS[0:HA, bank, :], ACT.Copy).then_inc(cast_done, 1)
                    s_.activation(kT[s % 2][:, h, 0:4 * P], PS[0:HA, bank, :], ACT.Copy).then_inc(w_act, 1)
                else:
                    src_k, src_q = PS[0:HA, bank, 0:2 * P], PS[0:HA, bank, 2 * P:4 * P]
                    s_.activation(kTb[:, h, 4 * P:6 * P], src_k, ACT.Copy)
                    s_.activation(qTb[:, h, :], src_q, ACT.Copy, scale=q_scale[:, 0:1]).then_inc(cast_done, 1)
                    s_.activation(kT[s % 2][:, h, 4 * P:6 * P], src_k, ACT.Copy)
                    s_.activation(qT[s % 2][:, h, :], src_q, ACT.Copy, scale=q_scale[:, 0:1]).then_inc(w_act, 1)

            def keep_rows(s, info):
                count, bank, _ = info
                act.wait_ge(w_filled, count)
                act.wait_ge(w_act, count - 1)
                s_.activation(qT[s % 2][DH:DH + 1, :, :], PS[DH:DH + 1, bank, :].rearrange("p (h q) -> p h q", h=2),
                              ACT.Copy).then_inc(w_act, 1)

            def exps(n, s, c):
                act.wait_ge(st_done, 6 * n + c + 1)
                if not (s == 0 and c < 3):
                    act.wait_ge(pv_done, 6 * n + c - 2)
                    if c < 3:
                        act.wait_ge(dve_added, 3 * n + c - 2)
                    else:
                        act.wait_ge(pool_added, 2 * n + (1, 1, 2)[c - 3])
                s_.activation(pT[c % 3][:, :, :], PS[:, E_BANK + c % 2, :].rearrange("p (h q) -> p h q", h=2),
                              ACT.Exp).then_inc(exp_done, 1)

            for j in range(2):
                keep_kq(0, 0, j, work_pro(f"K{j}"))
            for name in ("V0", "V1"):
                keep_v(0, name, work_pro(name))
            for k in range(2):
                keep_ff0(k)
            for name in ("T0", "T1", "T2", "T3"):
                keep_turned(0, name, work_pro(name))
            for j in range(2):
                keep_kq(1, 1, j, (j + 1, AHEAD_BANK[j], None), ahead_filled, ahead_left)
            keep_rows(0, work_pro("R0"))

            def pair(n, s):
                def w(name):
                    return work(n, s, name)

                v, k = s < NP - 1, s < NP - 2
                exps(n, s, 0)
                if v:
                    keep_turned(s + 1, "T0", w("T0"))
                    keep_turned(s + 1, "T1", w("T1"))
                exps(n, s, 1)
                if v:
                    keep_v(s + 1, "V0", w("V0"))
                    keep_turned(s + 1, "T2", w("T2"))
                    keep_turned(s + 1, "T3", w("T3"))
                exps(n, s, 2)
                if k:
                    keep_kq(n + 2, s + 2, 0, w("K0"))
                    keep_kq(n + 2, s + 2, 1, w("K1"))
                if v:
                    keep_v(s + 1, "V1", w("V1"))
                exps(n, s, 3)
                exps(n, s, 4)
                exps(n, s, 5)
                if v:
                    keep_rows(s + 1, w("R0"))

            pairs(act, pair)

            def keep_hT(k, b, bank):
                act.wait_ge(ln_T[k], b + 1)
                s_.activation(hT[:, S * b:S * (b + 1)], PS[:, bank, 0:S], ACT.Copy).then_inc(ln_evac[k], 1)

            for b in range(NB):
                keep_hT(0, b, b % 2)

            def shared_silu(v):
                act.wait_ge(sh_filled, v + 1)
                if v >= 2:
                    act.wait_ge(sh_mul, v - 1)
                s_.activation(sg_t[v % 2][:, :], PS[:, 2 + v % 2, :], ACT.Silu).then_inc(sh_silu, 1)

            shared_silu(0)
            shared_silu(1)
            act.wait_ge(top_ready, 1)
            s_.activation(gate[:, :, :], gate[:, :, :], ACT.Exp).then_inc(gexp_done, 1)
            shared_silu(2)
            shared_silu(3)
            for f in range(8):
                act.wait_ge(kv1_filled, f + 1)
                src = PS[:, f % 2, :]
                if f < 4:
                    s_.activation(kpT[:, 512 * f:512 * (f + 1)], src, ACT.Relu, bias=vec[:, 5:6]).then_inc(kv1_kept, 1)
                else:
                    s_.activation(vp[:, 4 * (f - 4):4 * (f - 3), :], src.rearrange("p (t d) -> p t d", t=4), ACT.Relu) \
                        .then_inc(kv1_kept, 1)

            def expert(e, k, up, turn_in=True):
                if turn_in:
                    act.wait_ge(t_filled, e + 1)
                    if not (isinstance(e, int) and e < 2):
                        act.wait_ge(gu_filled, e - 1)
                    s_.activation(xeT[k % 2][:, :], PS[:, k % 2, 0:CAP], ACT.Copy).then_inc(xeT_done, 1)
                if up:
                    r = (k - 1) % RING
                    act.wait_ge(gu_filled, e)
                    if not (isinstance(e, int) and e < 3):
                        act.wait_ge(he_done, e - 2)
                    s_.activation(sge[r % 2][:, :, :], PS[:, 2 + r % 2, 0:HT * CAP].rearrange("p (j c) -> p j c", j=HT),
                                  ACT.Silu).then_inc(silu_done, 1)

            for e in range(RING):
                expert(e, e, e >= 1)
            with act.Fori(1, NE // RING) as q:
                e0 = RING * q
                for k in range(RING):
                    expert(e0 + k, k, True)
            expert(NE, 0, True, turn_in=False)

            for r in range(1, NB + 3):
                b = r - 1
                if b < NB:
                    keep_hT(1, b, 0)
                    act.wait_ge(qp_filled, b + 1)
                    s_.activation(qpT[:, b * S:(b + 1) * S], PS[:, 2, 0:S], ACT.Relu, bias=vec[:, 4:5]) \
                        .then_inc(qp_ready, 1)
                if r >= 3:
                    keep_hT(2, r - 3, 1)
                if b < NB:
                    for c in range(2):
                        act.wait_ge(s2_filled, 2 * b + c + 1)
                        if b >= 2:
                            act.wait_ge(o2_filled, b - 1)
                        s_.activation(lg[b % 2][:, 2 * c:2 * c + 2, :],
                                      PS[:, 4 + c, :].rearrange("p (k q) -> p k q", k=2),
                                      ACT.Relu, scale=float(D) ** -0.5).then_inc(s2_relu, 1)

            act.wait_ge(logits_ready, 1)
            s_.activation(aff2[:, :, :], aff[:, :, :], ACT.Exp, scale=-1.0).then_inc(e1_exp, 1)

            def silu1(v, half, rows, bias):
                act.wait_ge(f_filled, v + 1)
                if not (isinstance(v, int) and v < 2):
                    act.wait_ge(f_h, v - 1)
                act.sem_inc(act_passed, 1)
                s_.activation(f_sg[half][0:rows, :], PS[0:rows, half, :], ACT.Silu, bias=bias).then_inc(f_silu, 1)

            for half in range(2):
                silu1(half, half, I2, vec[0:I2, 8:9])
            for i in range(2):
                act.wait_ge(wT_filled, i + 1)
                s_.activation(wT[:, 512 * i:512 * (i + 1)], PS[0:E2 + 1, 4 + i, :], ACT.Copy).then_inc(wT_ready, 1)
            act.wait_ge(wT_filled, 3)
            s_.activation(splitT[:, :], PS[:, 7, :].bitcast(bf16)[0:96, 0:XT * P], ACT.Copy).then_inc(wT_ready, 1)
            with act.Fori(0, PR) as j:
                for half in range(2):
                    silu1(2 * j + 2 + half, half, P, vec[:, bass.ds(10 + j, 1)])

        @block.vector
        def _(dve):
            v_ = nc.vector
            dve_n = [0]

            def link(ins):
                dve_n[0] += 1
                ins.then_inc(dve_step, 1)
                dve.wait_ge(dve_step, dve_n[0])

            def normalize(dst, src, t):
                return v_.tensor_scalar(dst, src, mv[:, t, 0:1], rstd[:, t:t + 1], ALU.subtract, ALU.mult)

            v_.memset(vec_rows[:, :], 0.0).then_inc(rows_clear, 1)
            link(v_.memset(q_scale[:, :], 1.0))
            dve.wait_ge(ld_x, 16)
            for i in range(XT):
                last = v_.bn_stats(st[:, CT + i, :], x_tok[:, i, :])
            link(last)
            for i in range(XT):
                v_.bn_aggr(mv[:, CT + i, :], st[:, CT + i, :]).then_inc(stats0, 1)
            dve.wait_ge(ld_mask, 16)
            v_.tensor_copy(mask_f[:, :], mask_u8[:, :]).then_inc(mask_cast, 1)
            dve.wait_ge(ld_ctx, 32)
            for i in range(CT):
                last = v_.bn_stats(st[:, i, :], ctx_tok[:, i, :])
            link(last)
            for i in range(CT):
                v_.bn_aggr(mv[:, i, :], st[:, i, :]).then_inc(stats0, 1)
            dve.wait_ge(rstd0, 1)
            for i in range(XT):
                last = normalize(h_tok[:, i, :], x_tok[:, i, :], CT + i)
            link(last)
            for i in range(XT):
                last = v_.bn_stats(st[:, CT + i, :], h_tok[:, i, :])
            link(last)
            for i in range(XT):
                v_.bn_aggr(mv[:, CT + i, :], st[:, CT + i, :]).then_inc(lat_stats, 1)
            dve.wait_ge(rstd0, 2)
            for i in range(CT):
                normalize(ctx_n[:, i, :], ctx_tok[:, i, :], i).then_inc(norm_ctx, 1)
            vec_fill = setup_own("vec", 0)
            src = PS[:, SETUP_BANK[vec_fill], :]
            dve.wait_ge(s0_filled, vec_fill + 1)
            v_.tensor_copy(vec[:, :], src[:, 0:48]).then_inc(vec_ready, 1)
            v_.tensor_scalar(mask_bias[:, :], src[:, 64:64 + CT], -BIG_NEG, BIG_NEG, ALU.mult, ALU.add) \
                .then_inc(mask_ready, 1)
            dve.wait_ge(vec_ready, 1)
            v_.scalar_tensor_tensor(q_scale[0:DH, :], vec[0:DH, 6:7], float(DH) ** -0.5, vec[0:DH, 7:8],
                                    ALU.mult, ALU.mult).then_inc(s0_dve, 1)
            dve.wait_ge(lat_rstd, 1)
            for i in range(XT):
                normalize(h_tok[:, i, :], h_tok[:, i, :], CT + i).then_inc(norm_x, 1)
                if i == 0:
                    dve.wait_ge(cent_ss, 1)
                    v_.tensor_reduce(cent_n[:, :], cent_sq[:, :], AX.X, ALU.add).then_inc(cent_ss, 1)
            for k in range(2):
                f = setup_own("lat", 0) + k
                src = PS[:, SETUP_BANK[f], :]
                dve.wait_ge(s0_filled, f + 1)
                if k == 0:
                    v_.tensor_scalar(act_cur[0][:, SC:NKEY], src[:, 0:S], vec[:, 2:3], vec[:, 3:4],
                                     ALU.mult, ALU.add)
                v_.tensor_scalar(actT[:, 2 * k:2 * k + 2, SC:NKEY], src.rearrange("p (b s) -> p b s", b=2),
                                 vec[:, 2:3], vec[:, 3:4], ALU.mult, ALU.add).then_inc(s0_dve, 1)

            def sum_squares(j, count, left=w_act):
                dve.wait_ge(left, count)
                v_.tensor_reduce(ss[:, 8 * j:8 * j + 8],
                                 kq_sq[:, 4 * j:4 * j + 4, :].rearrange("p t (h d) -> p (t h) d", h=2), AX.X, ALU.add) \
                    .then_inc(ss_done, 1)

            def row_maxima(n, s, i):
                dve.wait_ge(m_filled, 4 * n + i + 1)
                v_.tensor_reduce(negm[:, i:i + 1], PS[:, m_bank(s, i):m_bank(s, i) + 2, 0:NKEY // 2], AX.XY, ALU.max,
                                 negate=True).then_inc(m_read, 1)

            def divide(n):
                dve.wait_ge(sum_done, n + 1)
                v_.reciprocal(rcT[:, :], PS[:, O_BANK, S:2 * S]).then_inc(rc_done, 1)
                dve.wait_ge(rc_done, n + 1)
                v_.tensor_tensor(oT[:, bass.ds(n, 1), :].rearrange("p a s -> p (a s)"), PS[:, O_BANK, 0:S],
                                 rcT[:, :], ALU.mult).then_inc(o_done, 1)

            def add(n, s, c):
                dve.wait_ge(exp_done, 6 * n + c + 1)
                if c == 3:
                    dve.wait_ge(pool_added, 2 * n + 2)
                else:
                    dve.wait_ge(dve_added, 3 * n + c - 3)
                v_.tensor_tensor(p_sum[s % 2][:, :, :], p_sum[s % 2][:, :, :], pT[c % 3][:, :, :], ALU.add) \
                    .then_inc(dve_added, 1)

            for j in range(2):
                sum_squares(j, work_pro(f"K{j}")[0])
            dve.wait_ge(s0_filled, len(SETUP))
            v_.tensor_copy(centT[:, :], PS[:, SETUP_BANK[-1], 0:NG + NE]).then_inc(s0_dve, 1)
            row_maxima(0, 0, 0)
            row_maxima(0, 0, 1)
            sum_squares(0, 1, ahead_left)
            row_maxima(0, 0, 2)
            row_maxima(0, 0, 3)
            sum_squares(1, 2, ahead_left)

            def pair(n, s):
                v, k = s < NP - 1, s < NP - 2
                if s > 0:
                    add(n - 1, s - 1, 5)
                    divide(n - 1)
                if v:
                    row_maxima(n + 1, s + 1, 0)
                    row_maxima(n + 1, s + 1, 1)
                if k:
                    sum_squares(0, work(n, s, "K0")[0])
                    sum_squares(1, work(n, s, "K1")[0])
                if v:
                    row_maxima(n + 1, s + 1, 2)
                add(n, s, 3)
                if v:
                    row_maxima(n + 1, s + 1, 3)
                add(n, s, 4)

            pairs(dve, pair)
            add(NP - 1, NP - 1, 5)
            divide(NP - 1)

            dve.wait_ge(xb_ready, 1)
            def stats(k, b):
                tiles = range(QT * b, QT * (b + 1))
                for i in tiles:
                    last = v_.bn_stats(st[:, i, :], x_tok[:, i, :])
                link(last)
                for i in tiles:
                    v_.bn_aggr(mv[:, i, :], st[:, i, :]).then_inc(ln_stats[k], 1)

            def layernorm(k, b):
                dve.wait_ge(ln_rstd[k], b + 1)
                for i in range(QT * b, QT * (b + 1)):
                    normalize(h_tok[:, i, :], x_tok[:, i, :], i).then_inc(ln_norm[k], 1)

            def sum_hsq(b):
                tiles = slice(QT * b, QT * (b + 1))
                dve.wait_ge(hsq_done, b + 1)
                v_.tensor_reduce(rn[:, tiles], hsq[:, tiles, :], AX.X, ALU.add).then_inc(hsq_summed, 1)

            for b in range(NB):
                for i in range(QT * b, QT * (b + 1)):
                    dve.wait_ge(op_filled, i + 1)
                    last = v_.tensor_tensor(x_tok[:, i, :], x_tok[:, i, :], PS[:, op_bank(i), 0:D], ALU.add)
                link(last)
                stats(0, b)
                if b:
                    layernorm(0, b - 1)
                if b > 1:
                    sum_hsq(b - 2)
            layernorm(0, NB - 1)
            sum_hsq(NB - 2)
            sum_hsq(NB - 1)
            dve.wait_ge(rn_done, NB)
            dve.wait_ge(scores_ready, NB)
            link(v_.tensor_tensor(score[:, :, :],
                                  PS[:, 6, 0:XT * (NG + NE)].rearrange("p (t g) -> p t g", t=XT),
                                  rn[:, :].unsqueeze(2).broadcast_to([P, XT, NG + NE]), ALU.mult))
            gs = score[:, :, 0:NG]
            other = gs.unsqueeze(2).broadcast_to([P, XT, NG, NG])
            own = gs.unsqueeze(3).broadcast_to([P, XT, NG, NG])
            v_.tensor_tensor(cmp1[:, :, :, :], other, own, ALU.is_gt)
            link(v_.tensor_tensor(cmp2[:, :, :, :], other, own, ALU.is_equal))
            link(v_.tensor_tensor(cmp2[:, :, :, :], cmp2[:, :, :, :],
                                  lower_g[:, :, :].unsqueeze(1).broadcast_to([P, XT, NG, NG]), ALU.mult))
            link(v_.tensor_tensor(cmp1[:, :, :, :], cmp1[:, :, :, :], cmp2[:, :, :, :], ALU.add))
            link(v_.tensor_reduce(gmask[:, :, :], cmp1[:, :, :, :], AX.X, ALU.add))
            link(v_.tensor_scalar(gmask[:, :, :], gmask[:, :, :], float(NG // 2), None, ALU.is_lt))
            v_.tensor_scalar(gneg[:, :, :], gmask[:, :, :], 1e9, -1e9, ALU.mult, ALU.add)
            link(v_.tensor_tensor(masked[:, :, :], score[:, :, NG:], bias0_b[:, :].unsqueeze(1)
                                  .broadcast_to([P, XT, NE]), ALU.add))
            by_group = masked[:, :, :].rearrange("p t (g e) -> p t g e", g=NG)
            link(v_.tensor_tensor(by_group, by_group, gmask[:, :, :].unsqueeze(3)
                                  .broadcast_to([P, XT, NG, EG]), ALU.mult))
            link(v_.tensor_tensor(by_group, by_group, gneg[:, :, :].unsqueeze(3)
                                  .broadcast_to([P, XT, NG, EG]), ALU.add))
            for i in range(XT):
                last = v_.max(top_v[:, i, :], masked[:, i, :])
            link(last)
            for i in range(XT):
                last = v_.max_index(top_i[:, i, :], top_v[:, i, :], masked[:, i, :])
            v_.tensor_tensor(gate[:, :, :], top_v[:, :, 0:K0], top_v[:, :, 0:1].broadcast_to([P, XT, K0]),
                             ALU.subtract).then_inc(top_ready, 1)
            dve.wait_ge(top_ready, 1)
            link(v_.tensor_copy(top_f[:, :, :], top_i[:, :, 0:K0]))
            link(v_.tensor_tensor(oneh[:, :, :, :], iota_e[:, :].unsqueeze(1).unsqueeze(1)
                                  .broadcast_to([P, XT, K0, NE]),
                                  top_f[:, :, :].unsqueeze(3).broadcast_to([P, XT, K0, NE]), ALU.is_equal))
            with nc.allow_low_precision(reason="zeros and ones, exact in bfloat16"):
                v_.tensor_reduce(sel_b[:, :, :], oneh[:, :, :, :].rearrange("p t k e -> p t e k"), AX.X, ALU.add) \
                    .then_inc(sel_ready, 1)
            dve.wait_ge(gexp_done, 1)
            link(v_.tensor_reduce(gsum[:, :], gate[:, :, :], AX.X, ALU.add))
            link(v_.reciprocal(gsum[:, :], gsum[:, :]))
            link(v_.tensor_tensor(gate[:, :, :], gate[:, :, :], gsum[:, :].unsqueeze(2).broadcast_to([P, XT, K0]),
                                  ALU.mult))
            dve.wait_ge(pos_ready, 1)
            link(v_.tensor_tensor(ohp[:, :, :, :], oneh[:, :, :, :],
                                  PS[:, 7, 0:XT * NE].rearrange("p (t e) -> p t e", t=XT).unsqueeze(2)
                                  .broadcast_to([P, XT, K0, NE]), ALU.mult))
            link(v_.tensor_reduce(posk[:, :, :], ohp[:, :, :, :], AX.X, ALU.add))
            v_.tensor_scalar(keep[:, :, :], posk[:, :, :], float(CAP), None, ALU.is_lt)
            link(v_.tensor_scalar(slot_s[:, :, :], posk[:, :, :], float(CAP - 1), None, ALU.min))
            link(v_.scalar_tensor_tensor(slot_f[:, :, :], top_f[:, :, :], float(CAP), slot_s[:, :, :],
                                         ALU.mult, ALU.add))
            v_.tensor_copy(dest_out[:, :, :], slot_f[:, :, :]).then_inc(dest_ready, 1)
            link(v_.scalar_tensor_tensor(posk[:, :, :], keep[:, :, :], -1e6, slot_f[:, :, :], ALU.mult, ALU.add))
            v_.tensor_scalar(dest_in[:, :, :], posk[:, :, :], 1e6, None, ALU.add).then_inc(dest_ready, 1)
            link(v_.tensor_tensor(gate[:, :, :], gate[:, :, :], keep[:, :, :], ALU.mult))
            for v in range(4):
                j, half = v // 2, v % 2
                dve.wait_ge(sh_silu, v + 1)
                v_.tensor_tensor(hsT[:, j, half * 512:(half + 1) * 512], sg_t[v % 2][:, :], PS[:, 4 + v % 2, :],
                                 ALU.mult).then_inc(sh_mul, 1)
            for i in range(2):
                dve.wait_ge(sh_down, i + 1)
                rows = x_tok[:, 4 * i:4 * i + 4, :]
                v_.tensor_tensor(rows, rows, PS[:, i, :].rearrange("p (t d) -> p t d", t=4), ALU.add) \
                    .then_inc(sh_added, 1)

            def expert(e, k, up, down):
                if up:
                    r = (k - 1) % RING
                    dve.wait_ge(silu_done, e)
                    if not (isinstance(e, int) and e < 3):
                        dve.wait_ge(y_filled, e - 2)
                    v_.tensor_tensor(heT[r % 2][:, :, :], sge[r % 2][:, :, :],
                                     PS[:, 4 + r % 2, 0:HT * CAP].rearrange("p (j c) -> p j c", j=HT), ALU.mult) \
                        .then_inc(he_done, 1)
                if down:
                    r = (k - 2) % RING
                    dve.wait_ge(y_filled, e - 1)
                    if not (isinstance(e, int) and e < 6):
                        dve.wait_ge(y_stored[r % 4], (e - 2 - r % 4) * 4)
                    v_.tensor_copy(ye[r % 4][:, :, :], PS[0:HCAP, 6 + r % 2, 0:2 * D]
                                   .rearrange("p (c d) -> p c d", c=2)).then_inc(y_evac, 1)

            for e in range(RING):
                expert(e, e, e >= 1, e >= 2)
            with dve.Fori(1, NE // RING) as q:
                e0 = RING * q
                for k in range(RING):
                    expert(e0 + k, k, True, True)
            expert(NE, 0, True, True)
            expert(NE + 1, 1, False, True)
            dve.wait_ge(sh_added, 2)

            def combine(b):
                for i in range(QT * b, QT * (b + 1)):
                    dve.wait_ge(gathered[i], 16 * K0)
                    for k in range(K0):
                        link(v_.scalar_tensor_tensor(x_tok[:, i, :], yg[:, i, k, :], gate[:, i, k:k + 1],
                                                     x_tok[:, i, :], ALU.mult, ALU.add))

            for r in range(NB + 3):
                if 0 <= r - 1 < NB:
                    layernorm(1, r - 1)
                if r >= 3:
                    layernorm(2, r - 3)
                b = r - 2
                if 0 <= b < NB:
                    for c in range(2):
                        dve.wait_ge(s2_relu, 2 * b + c + 1)
                        scaled = lg[b % 2][:, 2 * c:2 * c + 2, :]
                        v_.tensor_tensor(scaled, scaled, ff0T[:, 2 * c:2 * c + 2, :], ALU.add) \
                            .then_inc(s2_masked, 1)
                if r < NB:
                    combine(r)
                    stats(1, r)
                if 0 <= b < NB:
                    dve.wait_ge(o2_filled, b + 1)
                    rows = x_tok[:, QT * b:QT * (b + 1), :]
                    v_.scalar_tensor_tensor(rows, PS[:, 6 + b % 2, 0:QT * D].rearrange("p (q d) -> p q d", q=QT), 0.0,
                                            rows, ALU.max, ALU.add).then_inc(o2_read, 1)
                    dve.wait_ge(o2_read, b + 1)
                    stats(2, b)

            dve.wait_ge(r1_filled, NB)
            v_.tensor_tensor(aff[:, :, :], PS[:, 3, 0:XT * E2].rearrange("p (t e) -> p t e", t=XT),
                             br_b[:, :].unsqueeze(1).broadcast_to([P, XT, E2]), ALU.add).then_inc(logits_ready, 1)
            dve.wait_ge(e1_exp, 1)
            link(v_.tensor_scalar(aff2[:, :, :], aff2[:, :, :], 1.0, None, ALU.add))
            link(v_.reciprocal(aff[:, :, :], aff2[:, :, :]))
            for i in range(XT):
                last = v_.max(top1[:, i, :], aff[:, i, :])
            link(last)
            link(v_.tensor_reduce(tsum[:, :], top1[:, :, :], AX.X, ALU.add))
            link(v_.tensor_scalar(tsum[:, :], tsum[:, :], 1e-9, None, ALU.add))
            link(v_.reciprocal(tsum[:, :], tsum[:, :]))
            for i in range(XT):
                last = v_.match_replace(aff2[:, i, :], top1[:, i, :], aff[:, i, :], -1.0)
            link(last)
            link(v_.tensor_tensor(aff2[:, :, :], aff2[:, :, :], aff[:, :, :], ALU.not_equal))
            link(v_.tensor_tensor(aff[:, :, :], aff[:, :, :], aff2[:, :, :], ALU.mult))
            v_.tensor_tensor(w_tok[:, :, 0:E2], aff[:, :, :], tsum[:, :].unsqueeze(2).broadcast_to([P, XT, E2]),
                             ALU.mult).then_inc(w_tok_ready, 1)
            dve.wait_ge(w_tok_ready, 1)
            link(v_.tensor_copy(split[:, :, 0, :], w_tok[:, :, 0:E2]))
            link(v_.tensor_tensor(resid[:, :, :], w_tok[:, :, 0:E2], split[:, :, 0, :], ALU.subtract))
            link(v_.tensor_copy(split[:, :, 1, :], resid[:, :, :]))
            link(v_.tensor_tensor(resid[:, :, :], resid[:, :, :], split[:, :, 1, :], ALU.subtract))
            v_.tensor_copy(split[:, :, 2, :], resid[:, :, :]).then_inc(split_ready, 1)

            def gated(v, half, rows, bias, weighted=True):
                dve.wait_ge(f_silu, v + 1)
                if not (isinstance(v, int) and v < 2):
                    dve.wait_ge(f_acc, v - 1)
                dst = f_t[half] if weighted else f_hT[half]
                ins = v_.scalar_tensor_tensor(dst[0:rows, :], PS[0:rows, 2 + half, :], bias, f_sg[half][0:rows, :],
                                              ALU.add, ALU.mult)
                if weighted:
                    ins.then_inc(f_gated, 1)
                    dve.wait_ge(f_gated, v - 1)
                    v_.tensor_tensor(f_hT[half][:, :], f_t[half][:, :], PS[:, 4 + half, :], ALU.mult) \
                        .then_inc(f_h, 1)
                else:
                    ins.then_inc(f_h, 1)

            for half in range(2):
                gated(half, half, I2, vec[0:I2, 9:10], weighted=False)
            with dve.Fori(0, PR) as j:
                for half in range(2):
                    gated(2 * j + 2 + half, half, P, vec[:, bass.ds(10 + PR + j, 1)])
            for i in range(XT):
                dve.wait_ge(f_acc, 2 * PR + 2 if i >= 4 else 2 * PR + 1)
                v_.tensor_tensor(h_tok[:, i, :], x_tok[:, i, :], PS[:, 6 + i // 4, (i % 4) * D:(i % 4 + 1) * D],
                                 ALU.add).then_inc(out_ready, 1)


def kernel(**inputs):
    import numpy as np
    import concourse.bacc as bacc
    from concourse.bass_utils import run_bass_kernel_spmd

    nc = bacc.Bacc("TRN2", target_bir_lowering=False, num_devices=1)
    arrays, aps = {}, {}
    for name, value in inputs.items():
        a = np.ascontiguousarray(value)
        arrays[f"in_{name}"] = a
        aps[name] = nc.dram_tensor(f"in_{name}", a.shape, mybir.dt.from_np(a.dtype), kind="ExternalInput").ap()
    out = nc.dram_tensor("out_x", arrays["in_x"].shape, mybir.dt.float32, kind="ExternalOutput").ap()
    build(nc, aps, out)
    r = run_bass_kernel_spmd(nc, [arrays], core_ids=[0])
    return r.results[0]["out_x"]
```
